# Optimizing a Trainium2 kernel written in Bass

```python
import numpy as np
import jax
import jax.numpy as jnp

def _softmax(x, axis=-1):
    return jax.nn.softmax(x, axis=axis)

def _gelu(x):
    return jax.nn.gelu(x, approximate=True)

def _silu(x):
    return jax.nn.silu(x)

def _sigmoid(x):
    return jax.nn.sigmoid(x)

def _layernorm(x, axis=-1, eps=1e-05):
    m = jnp.mean(x, axis=axis, keepdims=True)
    v = jnp.var(x, axis=axis, keepdims=True)
    return (x - m) / jnp.sqrt(v + eps)

def _scatter_add(tgt, idx, src, axis=0):
    return tgt.at[idx].add(src)

def _segment_sum(src, seg, n):
    return jax.ops.segment_sum(src, seg, n)
kernel_name = 'mk_adaln_d2_jaxref_r8_99975a'

def setup_inputs(seed: int=0):
    np.random.seed(seed)
    _w = jnp.asarray

    def _L0_attn_setup():
        import jax, jax.numpy as jnp
        import numpy as np
        B, T, D_MODEL = (4, 256, 256)
        NUM_HEADS, HEAD_SIZE = (16, 128)
        MODEL_SIZE = 256
        key = jax.random.key(seed)
        ks = jax.random.split(key, 9)
        s = 0.02 / np.sqrt(D_MODEL)
        so = 0.02 / np.sqrt(NUM_HEADS * HEAD_SIZE)
        return {'query': jax.random.normal(ks[0], (B, T, D_MODEL), jnp.float32), 'w_q': jax.random.normal(ks[1], (D_MODEL, NUM_HEADS * HEAD_SIZE), jnp.float32) * s, 'b_q': jnp.zeros((NUM_HEADS * HEAD_SIZE,), jnp.float32), 'w_k': jax.random.normal(ks[2], (D_MODEL, NUM_HEADS * HEAD_SIZE), jnp.float32) * s, 'b_k': jnp.zeros((NUM_HEADS * HEAD_SIZE,), jnp.float32), 'w_v': jax.random.normal(ks[3], (D_MODEL, NUM_HEADS * HEAD_SIZE), jnp.float32) * s, 'b_v': jnp.zeros((NUM_HEADS * HEAD_SIZE,), jnp.float32), 'w_o': jax.random.normal(ks[4], (NUM_HEADS * HEAD_SIZE, MODEL_SIZE), jnp.float32) * so, 'b_o': jnp.zeros((MODEL_SIZE,), jnp.float32)}
    _L0_attn_in = _L0_attn_setup()

    def _L0_ffn_setup():
        import jax, jax.numpy as jnp
        import numpy as np
        TOP_K = 6
        CAP_FACTOR = 2

        def _moe_block(x2d, wg_router, w_gate, w_up, w_down, ws_gate, ws_up, ws_down):
            T, D = x2d.shape
            E = wg_router.shape[0]
            scores = jax.nn.softmax(x2d @ wg_router.T, axis=-1)
            topk_w, topk_idx = jax.lax.top_k(scores, TOP_K)
            topk_w = topk_w / (jnp.sum(topk_w, axis=-1, keepdims=True) + 1e-20)
            flat_idx = topk_idx.reshape(-1)
            oh = jax.nn.one_hot(flat_idx, E, dtype=jnp.int32)
            pos = jnp.cumsum(oh, axis=0) - 1
            pos_in_e = jnp.take_along_axis(pos, flat_idx[:, None], axis=1)[:, 0]
            C = CAP_FACTOR * (T * TOP_K // E)
            valid = pos_in_e < C
            safe_pos = jnp.where(valid, pos_in_e, 0)
            tok_id = jnp.repeat(jnp.arange(T), TOP_K)
            vmask = valid[:, None].astype(x2d.dtype)
            x_rep = x2d[tok_id] * vmask
            xe = jnp.zeros((E, C, D), x2d.dtype).at[flat_idx, safe_pos].add(x_rep)
            g = jnp.einsum('ecd,edf->ecf', xe, w_gate)
            u = jnp.einsum('ecd,edf->ecf', xe, w_up)
            ye = jnp.einsum('ecf,efd->ecd', jax.nn.silu(g) * u, w_down)
            y_tok = ye[flat_idx, safe_pos] * vmask
            y = jnp.sum(y_tok.reshape(T, TOP_K, D) * topk_w[..., None], axis=1)
            sh = jax.nn.silu(x2d @ ws_gate) * (x2d @ ws_up) @ ws_down
            return y + sh
        key = jax.random.key(seed)
        ks = jax.random.split(key, 9)
        B, S, D, F, E = (1, 256, 256, 176, 32)
        FS = F * 2
        s = 0.02
        return {'hidden_states': jax.random.normal(ks[0], (B, S, D), jnp.float32), 'wg_router': jax.random.normal(ks[1], (E, D), jnp.float32) * s, 'w_gate': jax.random.normal(ks[2], (E, D, F), jnp.float32) * s, 'w_up': jax.random.normal(ks[3], (E, D, F), jnp.float32) * s, 'w_down': jax.random.normal(ks[4], (E, F, D), jnp.float32) * s, 'ws_gate': jax.random.normal(ks[5], (D, FS), jnp.float32) * s, 'ws_up': jax.random.normal(ks[6], (D, FS), jnp.float32) * s, 'ws_down': jax.random.normal(ks[7], (FS, D), jnp.float32) * s}
    _L0_ffn_in = _L0_ffn_setup()
    _L0_c = _w((lambda *s: np.random.randn(*s).astype(np.float32) * 0.05)(2, 256))
    _L0_wmod = _w((lambda *s: np.random.randn(*s).astype(np.float32) * 0.05)(256, 6 * 256) * 256 ** (-0.5))

    def _L1_attn_setup():
        import jax, jax.numpy as jnp
        import numpy as np
        H, DK, DV, HID, KSZ, CHUNK = (6, 32, 64, 256, 4, 64)
        EPS = 1e-05

        def _short_conv(x, w):
            C, K = (w.shape[0], w.shape[2])
            y = jax.lax.conv_general_dilated(x.transpose(0, 2, 1), w, window_strides=(1,), padding=[(K - 1, 0)], feature_group_count=C, dimension_numbers=('NCH', 'OIH', 'NCH'))
            return jax.nn.silu(y.transpose(0, 2, 1))

        def _l2norm(x, eps=1e-06):
            return x * jax.lax.rsqrt(jnp.sum(x * x, axis=-1, keepdims=True) + eps)
        key = jax.random.key(seed)
        ks = jax.random.split(key, 16)
        B, T = (2, 256)

        def w(k, shape):
            s = 1.0 / np.sqrt(shape[-1] if len(shape) == 2 else shape[-1] * shape[-2] + 1e-09)
            if len(shape) == 3:
                s = 1.0 / np.sqrt(shape[2])
            return jax.random.uniform(k, shape, jnp.float32, -s, s)
        dt = jnp.exp(jax.random.uniform(ks[7], (H,), jnp.float32) * (np.log(0.1) - np.log(0.001)) + np.log(0.001))
        dt = jnp.clip(dt, 0.0001)
        return {'x': jax.random.normal(ks[0], (B, T, HID), jnp.float32), 'Wq': w(ks[1], (H * DK, HID)), 'Wk': w(ks[2], (H * DK, HID)), 'Wv': w(ks[3], (H * DV, HID)), 'Wa': w(ks[4], (H, HID)), 'Wb': w(ks[5], (H, HID)), 'A_log': jnp.log(jax.random.uniform(ks[6], (H,), jnp.float32, 1.0, 16.0)), 'dt_bias': dt + jnp.log(-jnp.expm1(-dt)), 'conv_q_w': w(ks[8], (H * DK, 1, KSZ)), 'conv_k_w': w(ks[9], (H * DK, 1, KSZ)), 'conv_v_w': w(ks[10], (H * DV, 1, KSZ)), 'Wg': w(ks[11], (H * DV, HID)), 'norm_w': jnp.ones((DV,), jnp.float32), 'Wo': w(ks[12], (HID, H * DV))}
    _L1_attn_in = _L1_attn_setup()

    def _L1_ffn_setup():
        import jax, jax.numpy as jnp
        import numpy as np
        B, S, H = (1, 128, 256)
        I = 176
        E = 32
        K = 6
        G = 8
        TG = 3
        NSH = 2
        SCALE = 16.0
        C = 48

        def _moe_forward(x3, gate_w, w_gate_up, w_down, ws_gate_up, ws_down):
            b, s, h = x3.shape
            x = x3.reshape(-1, h)
            T = x.shape[0]
            logits = x @ gate_w.T
            grouped = logits.reshape(T, G, E // G)
            group_scores = jnp.max(grouped, axis=-1)
            _, group_idx = jax.lax.top_k(group_scores, TG)
            group_keep = jnp.zeros((T, G), bool).at[jnp.arange(T)[:, None], group_idx].set(True)
            masked = jnp.where(group_keep[..., None], grouped, 0.0)
            scores = masked.reshape(T, E)
            probs = jax.nn.softmax(scores.astype(jnp.float32), axis=-1)
            topk_w, topk_idx = jax.lax.top_k(probs, K)
            topk_w = topk_w * SCALE
            flat_e = topk_idx.reshape(-1)
            tok_idx = jnp.repeat(jnp.arange(T), K)
            oh = jax.nn.one_hot(flat_e, E, dtype=jnp.int32)
            pos = jnp.take_along_axis(jnp.cumsum(oh, axis=0) - 1, flat_e[:, None], axis=1)[:, 0]
            valid = pos < C
            slot = jnp.where(valid, flat_e * C + pos, E * C)
            buf = jnp.zeros((E * C + 1, h), x.dtype).at[slot].set(x[tok_idx])
            xb = buf[:E * C].reshape(E, C, h)
            gu = jnp.einsum('ech,ehf->ecf', xb, w_gate_up)
            g, u = jnp.split(gu, 2, axis=-1)
            act = jax.nn.silu(g) * u
            yb = jnp.einsum('eci,eih->ech', act, w_down)
            yflat = jnp.concatenate([yb.reshape(E * C, h), jnp.zeros((1, h), yb.dtype)], axis=0)
            y_pairs = yflat[slot].reshape(T, K, h)
            out = jnp.einsum('tk,tkh->th', topk_w.astype(x.dtype), y_pairs)
            gu_s = x @ ws_gate_up
            gs, us = jnp.split(gu_s, 2, axis=-1)
            out = out + jax.nn.silu(gs) * us @ ws_down
            return out.reshape(b, s, h)
        key = jax.random.key(seed)
        ks = jax.random.split(key, 6)
        s = 0.02
        return {'hidden_states': jax.random.normal(ks[0], (B, S, H), jnp.float32), 'gate_w': jax.random.normal(ks[1], (E, H), jnp.float32) * s, 'w_gate_up': jax.random.normal(ks[2], (E, H, 2 * I), jnp.float32) * s, 'w_down': jax.random.normal(ks[3], (E, I, H), jnp.float32) * s, 'ws_gate_up': jax.random.normal(ks[4], (H, 2 * I * NSH), jnp.float32) * s, 'ws_down': jax.random.normal(ks[5], (I * NSH, H), jnp.float32) * s}
    _L1_ffn_in = _L1_ffn_setup()
    _L1_c = _w((lambda *s: np.random.randn(*s).astype(np.float32) * 0.05)(2, 256))
    _L1_wmod = _w((lambda *s: np.random.randn(*s).astype(np.float32) * 0.05)(256, 6 * 256) * 256 ** (-0.5))
    _d = {'L0_attn_query': _L0_attn_in['query'], 'L0_attn_w_q': _L0_attn_in['w_q'], 'L0_attn_b_q': _L0_attn_in['b_q'], 'L0_attn_w_k': _L0_attn_in['w_k'], 'L0_attn_b_k': _L0_attn_in['b_k'], 'L0_attn_w_v': _L0_attn_in['w_v'], 'L0_attn_b_v': _L0_attn_in['b_v'], 'L0_attn_w_o': _L0_attn_in['w_o'], 'L0_attn_b_o': _L0_attn_in['b_o'], 'L0_ffn_wg_router': _L0_ffn_in['wg_router'], 'L0_ffn_w_gate': _L0_ffn_in['w_gate'], 'L0_ffn_w_up': _L0_ffn_in['w_up'], 'L0_ffn_w_down': _L0_ffn_in['w_down'], 'L0_ffn_ws_gate': _L0_ffn_in['ws_gate'], 'L0_ffn_ws_up': _L0_ffn_in['ws_up'], 'L0_ffn_ws_down': _L0_ffn_in['ws_down'], 'L0_c': _L0_c, 'L0_wmod': _L0_wmod, 'L1_attn_Wq': _L1_attn_in['Wq'], 'L1_attn_Wk': _L1_attn_in['Wk'], 'L1_attn_Wv': _L1_attn_in['Wv'], 'L1_attn_Wa': _L1_attn_in['Wa'], 'L1_attn_Wb': _L1_attn_in['Wb'], 'L1_attn_A_log': _L1_attn_in['A_log'], 'L1_attn_dt_bias': _L1_attn_in['dt_bias'], 'L1_attn_conv_q_w': _L1_attn_in['conv_q_w'], 'L1_attn_conv_k_w': _L1_attn_in['conv_k_w'], 'L1_attn_conv_v_w': _L1_attn_in['conv_v_w'], 'L1_attn_Wg': _L1_attn_in['Wg'], 'L1_attn_norm_w': _L1_attn_in['norm_w'], 'L1_attn_Wo': _L1_attn_in['Wo'], 'L1_ffn_gate_w': _L1_ffn_in['gate_w'], 'L1_ffn_w_gate_up': _L1_ffn_in['w_gate_up'], 'L1_ffn_w_down': _L1_ffn_in['w_down'], 'L1_ffn_ws_gate_up': _L1_ffn_in['ws_gate_up'], 'L1_ffn_ws_down': _L1_ffn_in['ws_down'], 'L1_c': _L1_c, 'L1_wmod': _L1_wmod}
    _x0 = _d['L0_attn_query']
    _d['L0_attn_query'] = jax.random.normal(jax.random.fold_in(jax.random.key(seed), 1), (2, 512, 256), dtype=_x0.dtype)
    del _x0
    return _d

def reference(L0_attn_query, L0_attn_w_q, L0_attn_b_q, L0_attn_w_k, L0_attn_b_k, L0_attn_w_v, L0_attn_b_v, L0_attn_w_o, L0_attn_b_o, L0_ffn_wg_router, L0_ffn_w_gate, L0_ffn_w_up, L0_ffn_w_down, L0_ffn_ws_gate, L0_ffn_ws_up, L0_ffn_ws_down, L0_c, L0_wmod, L1_attn_Wq, L1_attn_Wk, L1_attn_Wv, L1_attn_Wa, L1_attn_Wb, L1_attn_A_log, L1_attn_dt_bias, L1_attn_conv_q_w, L1_attn_conv_k_w, L1_attn_conv_v_w, L1_attn_Wg, L1_attn_norm_w, L1_attn_Wo, L1_ffn_gate_w, L1_ffn_w_gate_up, L1_ffn_w_down, L1_ffn_ws_gate_up, L1_ffn_ws_down, L1_c, L1_wmod):

    def _L0_attn_ref(query, w_q, b_q, w_k, b_k, w_v, b_v, w_o, b_o):
        import jax, jax.numpy as jnp
        import numpy as np
        B, T, D_MODEL = (4, 256, 256)
        NUM_HEADS, HEAD_SIZE = (16, 128)
        MODEL_SIZE = 256
        B_, T_, _ = query.shape
        q = (query @ w_q + b_q).reshape(B_, T_, NUM_HEADS, HEAD_SIZE)
        k = (query @ w_k + b_k).reshape(B_, T_, NUM_HEADS, HEAD_SIZE)
        v = (query @ w_v + b_v).reshape(B_, T_, NUM_HEADS, HEAD_SIZE)
        logits = jnp.einsum('bthd,bThd->bhtT', q, k) * jax.lax.rsqrt(jnp.float32(HEAD_SIZE))
        i = jnp.arange(T_, dtype=jnp.int32)[:, None]
        j = jnp.arange(T_, dtype=jnp.int32)
        mask = (i >= j).astype(logits.dtype)
        logits = logits - 10000000000.0 * (1.0 - mask)
        weights = jax.nn.softmax(logits, axis=-1)
        attn = jnp.einsum('bhtT,bThd->bthd', weights, v).reshape(B_, T_, NUM_HEADS * HEAD_SIZE)
        out = attn @ w_o + b_o
        return out

    def _L0_ffn_ref(hidden_states, wg_router, w_gate, w_up, w_down, ws_gate, ws_up, ws_down):
        import jax, jax.numpy as jnp
        import numpy as np
        TOP_K = 6
        CAP_FACTOR = 2

        def _moe_block(x2d, wg_router, w_gate, w_up, w_down, ws_gate, ws_up, ws_down):
            T, D = x2d.shape
            E = wg_router.shape[0]
            scores = jax.nn.softmax(x2d @ wg_router.T, axis=-1)
            topk_w, topk_idx = jax.lax.top_k(scores, TOP_K)
            topk_w = topk_w / (jnp.sum(topk_w, axis=-1, keepdims=True) + 1e-20)
            flat_idx = topk_idx.reshape(-1)
            oh = jax.nn.one_hot(flat_idx, E, dtype=jnp.int32)
            pos = jnp.cumsum(oh, axis=0) - 1
            pos_in_e = jnp.take_along_axis(pos, flat_idx[:, None], axis=1)[:, 0]
            C = CAP_FACTOR * (T * TOP_K // E)
            valid = pos_in_e < C
            safe_pos = jnp.where(valid, pos_in_e, 0)
            tok_id = jnp.repeat(jnp.arange(T), TOP_K)
            vmask = valid[:, None].astype(x2d.dtype)
            x_rep = x2d[tok_id] * vmask
            xe = jnp.zeros((E, C, D), x2d.dtype).at[flat_idx, safe_pos].add(x_rep)
            g = jnp.einsum('ecd,edf->ecf', xe, w_gate)
            u = jnp.einsum('ecd,edf->ecf', xe, w_up)
            ye = jnp.einsum('ecf,efd->ecd', jax.nn.silu(g) * u, w_down)
            y_tok = ye[flat_idx, safe_pos] * vmask
            y = jnp.sum(y_tok.reshape(T, TOP_K, D) * topk_w[..., None], axis=1)
            sh = jax.nn.silu(x2d @ ws_gate) * (x2d @ ws_up) @ ws_down
            return y + sh
        B, S, D = hidden_states.shape
        x2d = hidden_states.reshape(-1, D)
        out = _moe_block(x2d, wg_router, w_gate, w_up, w_down, ws_gate, ws_up, ws_down)
        return out.reshape(B, S, D)

    def _L1_attn_ref(x, Wq, Wk, Wv, Wa, Wb, A_log, dt_bias, conv_q_w, conv_k_w, conv_v_w, Wg, norm_w, Wo):
        import jax, jax.numpy as jnp
        import numpy as np
        H, DK, DV, HID, KSZ, CHUNK = (6, 32, 64, 256, 4, 64)
        EPS = 1e-05

        def _short_conv(x, w):
            C, K = (w.shape[0], w.shape[2])
            y = jax.lax.conv_general_dilated(x.transpose(0, 2, 1), w, window_strides=(1,), padding=[(K - 1, 0)], feature_group_count=C, dimension_numbers=('NCH', 'OIH', 'NCH'))
            return jax.nn.silu(y.transpose(0, 2, 1))

        def _l2norm(x, eps=1e-06):
            return x * jax.lax.rsqrt(jnp.sum(x * x, axis=-1, keepdims=True) + eps)
        B, T, _ = x.shape
        q = _short_conv(x @ Wq.T, conv_q_w).reshape(B, T, H, DK)
        k = _short_conv(x @ Wk.T, conv_k_w).reshape(B, T, H, DK)
        v = _short_conv(x @ Wv.T, conv_v_w).reshape(B, T, H, DV)
        q = _l2norm(q) * DK ** (-0.5)
        k = _l2norm(k)
        g = -jnp.exp(A_log) * jax.nn.softplus(x @ Wa.T + dt_bias)
        beta = jax.nn.sigmoid(x @ Wb.T)

        def tm(a):
            a = jnp.moveaxis(a, 1, 0)
            return a.reshape((T // CHUNK, CHUNK) + a.shape[1:])
        qc, kc, vc, gc, bc = map(tm, (q, k, v, g, beta))

        def step(S, inp):
            q_t, k_t, v_t, g_t, b_t = inp
            S = S * jnp.exp(g_t)[..., None, None]
            delta = (v_t - jnp.einsum('bhk,bhkv->bhv', k_t, S)) * b_t[..., None]
            S = S + k_t[..., None] * delta[:, :, None, :]
            return (S, jnp.einsum('bhk,bhkv->bhv', q_t, S))

        @jax.checkpoint
        def chunk(S, inp):
            return jax.lax.scan(step, S, inp)
        S0 = jnp.zeros((B, H, DK, DV), x.dtype)
        _, o = jax.lax.scan(chunk, S0, (qc, kc, vc, gc, bc))
        o = jnp.moveaxis(o.reshape(T, B, H, DV), 0, 1)
        gate = (x @ Wg.T).reshape(B, T, H, DV)
        og = o * jax.nn.silu(gate)
        og = og * jax.lax.rsqrt(jnp.mean(og * og, axis=-1, keepdims=True) + EPS) * norm_w
        return og.reshape(B, T, H * DV) @ Wo.T

    def _L1_ffn_ref(hidden_states, gate_w, w_gate_up, w_down, ws_gate_up, ws_down):
        import jax, jax.numpy as jnp
        import numpy as np
        B, S, H = (1, 128, 256)
        I = 176
        E = 32
        K = 6
        G = 8
        TG = 3
        NSH = 2
        SCALE = 16.0
        C = 48

        def _moe_forward(x3, gate_w, w_gate_up, w_down, ws_gate_up, ws_down):
            b, s, h = x3.shape
            x = x3.reshape(-1, h)
            T = x.shape[0]
            logits = x @ gate_w.T
            grouped = logits.reshape(T, G, E // G)
            group_scores = jnp.max(grouped, axis=-1)
            _, group_idx = jax.lax.top_k(group_scores, TG)
            group_keep = jnp.zeros((T, G), bool).at[jnp.arange(T)[:, None], group_idx].set(True)
            masked = jnp.where(group_keep[..., None], grouped, 0.0)
            scores = masked.reshape(T, E)
            probs = jax.nn.softmax(scores.astype(jnp.float32), axis=-1)
            topk_w, topk_idx = jax.lax.top_k(probs, K)
            topk_w = topk_w * SCALE
            flat_e = topk_idx.reshape(-1)
            tok_idx = jnp.repeat(jnp.arange(T), K)
            oh = jax.nn.one_hot(flat_e, E, dtype=jnp.int32)
            pos = jnp.take_along_axis(jnp.cumsum(oh, axis=0) - 1, flat_e[:, None], axis=1)[:, 0]
            valid = pos < C
            slot = jnp.where(valid, flat_e * C + pos, E * C)
            buf = jnp.zeros((E * C + 1, h), x.dtype).at[slot].set(x[tok_idx])
            xb = buf[:E * C].reshape(E, C, h)
            gu = jnp.einsum('ech,ehf->ecf', xb, w_gate_up)
            g, u = jnp.split(gu, 2, axis=-1)
            act = jax.nn.silu(g) * u
            yb = jnp.einsum('eci,eih->ech', act, w_down)
            yflat = jnp.concatenate([yb.reshape(E * C, h), jnp.zeros((1, h), yb.dtype)], axis=0)
            y_pairs = yflat[slot].reshape(T, K, h)
            out = jnp.einsum('tk,tkh->th', topk_w.astype(x.dtype), y_pairs)
            gu_s = x @ ws_gate_up
            gs, us = jnp.split(gu_s, 2, axis=-1)
            out = out + jax.nn.silu(gs) * us @ ws_down
            return out.reshape(b, s, h)
        return _moe_forward(hidden_states, gate_w, w_gate_up, w_down, ws_gate_up, ws_down)
    x = L0_attn_query
    mod = (_silu(L0_c) @ L0_wmod).reshape(L0_c.shape[0], 6, 1, -1)
    sa, ca, ga, sb, cb, gb = (mod[:, 0], mod[:, 1], mod[:, 2], mod[:, 3], mod[:, 4], mod[:, 5])
    ga = (2 * (ga >= 0) - 1) * jnp.maximum(jnp.abs(ga), 0.25)
    gb = (2 * (gb >= 0) - 1) * jnp.maximum(jnp.abs(gb), 0.25)
    h = _layernorm(x, axis=-1) * (1 + ca) + sa
    x = x + ga * _L0_attn_ref(h, L0_attn_w_q, L0_attn_b_q, L0_attn_w_k, L0_attn_b_k, L0_attn_w_v, L0_attn_b_v, L0_attn_w_o, L0_attn_b_o)
    h = _layernorm(x, axis=-1) * (1 + cb) + sb
    x = x + gb * _L0_ffn_ref(h, L0_ffn_wg_router, L0_ffn_w_gate, L0_ffn_w_up, L0_ffn_w_down, L0_ffn_ws_gate, L0_ffn_ws_up, L0_ffn_ws_down)
    mod = (_silu(L1_c) @ L1_wmod).reshape(L1_c.shape[0], 6, 1, -1)
    sa, ca, ga, sb, cb, gb = (mod[:, 0], mod[:, 1], mod[:, 2], mod[:, 3], mod[:, 4], mod[:, 5])
    ga = (2 * (ga >= 0) - 1) * jnp.maximum(jnp.abs(ga), 0.25)
    gb = (2 * (gb >= 0) - 1) * jnp.maximum(jnp.abs(gb), 0.25)
    h = _layernorm(x, axis=-1) * (1 + ca) + sa
    x = x + ga * _L1_attn_ref(h, L1_attn_Wq, L1_attn_Wk, L1_attn_Wv, L1_attn_Wa, L1_attn_Wb, L1_attn_A_log, L1_attn_dt_bias, L1_attn_conv_q_w, L1_attn_conv_k_w, L1_attn_conv_v_w, L1_attn_Wg, L1_attn_norm_w, L1_attn_Wo)
    h = _layernorm(x, axis=-1) * (1 + cb) + sb
    x = x + gb * _L1_ffn_ref(h, L1_ffn_gate_w, L1_ffn_w_gate_up, L1_ffn_w_down, L1_ffn_ws_gate_up, L1_ffn_ws_down)
    return x

_drawn_inputs = setup_inputs


def setup_inputs(seed=0):
    import zlib

    import numpy as np

    out = dict(_drawn_inputs(seed))
    spreads = {'L0_attn_b_q': (0.0, 0.8),
     'L0_attn_b_k': (0.0, 0.8),
     'L0_attn_b_v': (0.0, 0.8),
     'L0_attn_b_o': (0.0, 0.31),
     'L1_attn_norm_w': (1.0, 0.6)}
    factors = {'L0_attn_w_q': 8.0,
     'L0_attn_w_k': 8.0,
     'L0_attn_w_v': 8.0,
     'L0_attn_w_o': 8.0,
     'L0_ffn_wg_router': 8.0,
     'L0_ffn_w_gate': 8.0,
     'L0_ffn_w_up': 8.0,
     'L0_ffn_w_down': 8.0,
     'L0_ffn_ws_gate': 8.0,
     'L0_ffn_ws_up': 8.0,
     'L0_ffn_ws_down': 8.0,
     'L1_attn_Wa': 8.0,
     'L1_attn_A_log': 3.101,
     'L1_ffn_gate_w': 8.0,
     'L1_ffn_w_gate_up': 6.57,
     'L1_ffn_w_down': 6.526,
     'L1_ffn_ws_gate_up': 8.0,
     'L1_ffn_ws_down': 8.0}
    for name, (base, spread) in spreads.items():
        noise = np.random.default_rng([zlib.crc32(name.encode()), seed]).standard_normal(out[name].shape)
        drawn = base * np.exp(spread * noise) if base else spread * noise
        out[name] = jnp.asarray(drawn.astype(out[name].dtype))
    for name, factor in factors.items():
        out[name] = (out[name] * factor).astype(out[name].dtype)
    return out
```

```python
from contextlib import ExitStack, contextmanager

import numpy as np

import concourse.bass as bass
import concourse.mybir as mybir

F32 = mybir.dt.float32
BF16 = mybir.dt.bfloat16
I32 = mybir.dt.int32
ALU = mybir.AluOpType
ACT = mybir.ActivationFunctionType
X = mybir.AxisListType.X

P = 128
B, T, D = 2, 512, 256
TOK = B * T
NT = TOK // P
TB = T // P
KT = D // P
NMOD = 6 * D

HEADS, HD = 16, 128
SCALE = float(HD) ** -0.5

E, TOPK, F = 32, 6, 176
FH = F // 2
FS = 2 * F
FS_CHUNKS = [(0, 128), (128, 128), (256, 96)]
CAP = [2 * (TOK * TOPK // E), 48]
GROUPS, GTOP = 8, 3
ROUTE_SCALE = 16.0
SLOTS = 384
SB = SLOTS // P

DH, DK, DV = 6, 32, 64
QKV = DH * (2 * DK + DV)
CH = 96
NCH = QKV // CH
TAPS = 4
LEVELS = [2, 4, 8, 16, 32, 64]
NEG = -1.0e30

CF = {}
_at = 0
for _n, _w in (("ident", P), ("after", P), ("upto", P), ("ones", DK), ("base0", E), ("base1", E),
               ("row", 1), ("lev", (len(LEVELS) + 1) * P)):
    CF[_n] = (_at, _at + _w)
    _at += _w
CF_W = _at
CB = {}
_at = 0
for _n, _w in (("ident", P), ("future", P), ("past", P), ("before", P), ("ones", P), ("iota", P)):
    CB[_n] = (_at, _at + _w)
    _at += _w
CB_W = _at


def constants():
    i = np.arange(P)
    cf = np.zeros((P, CF_W), np.float32)
    cf[:, slice(*CF["ident"])] = np.eye(P)
    cf[:, slice(*CF["after"])] = i[:, None] > i[None, :]
    cf[:, slice(*CF["upto"])] = i[:, None] <= i[None, :]
    cf[:, slice(*CF["ones"])] = 1.0
    for n in (0, 1):
        cf[:, slice(*CF[f"base{n}"])] = (np.arange(E) * CAP[n] - E * CAP[n])[None, :]
    cf[:, CF["row"][0]] = i
    at = CF["lev"][0]
    for s in [1] + LEVELS:
        j, k = i[:, None], i[None, :]
        cf[:, at:at + P] = (j // (2 * s) == k // (2 * s)) & (j // s % 2 == 0) & (k // s % 2 == 1)
        at += P
    cb = np.zeros((P, CB_W), np.float32)
    cb[:, slice(*CB["ident"])] = np.eye(P)
    cb[:, slice(*CB["future"])] = np.where(i[None, :] > i[:, None], NEG, 0.0)
    cb[:, slice(*CB["past"])] = np.where(i[None, :] < i[:, None], NEG, 0.0)
    cb[:, slice(*CB["before"])] = i[:, None] < i[None, :]
    cb[:, slice(*CB["ones"])] = 1.0
    cb[:, slice(*CB["iota"])] = i[None, :]
    return cf, cb.astype(mybir.dt.np(BF16))


@contextmanager
def stage(nc, *names):
    with ExitStack() as ctx:
        sems = [ctx.enter_context(nc.semaphore(n)) for n in names]
        yield sems
        with nc.Block() as block:
            @block.sync
            def _(sp):
                for s in sems:
                    sp.sem_clear(s)


class Steps:

    def __init__(self, engine, sem, base=0):
        self.engine, self.sem, self.base, self.n = engine, sem, base, 0

    def __call__(self, ins):
        ins.then_inc(self.sem, 1)
        self.n += 1
        self.engine.wait_ge(self.sem, self.base + self.n)


NAMES = {}


def sbuf(nc, name, shape, dt=F32):
    NAMES[name] = NAMES.get(name, -1) + 1
    return nc.sbuf_tensor(f"{name}_{NAMES[name]}" if NAMES[name] else name, shape, dt)


def load_stage(nc, k):
    with stage(nc, "const_in", "c_in", "silu_done", "rep_done", "rows_full", "rows_used", "dve_step") as (
            const_in, c_in, silu_done, rep_done, rows_full, rows_used, dve_step), ExitStack() as ctx:
        ct = ctx.enter_context(sbuf(nc, "ct", [P, 2, KT, B], F32))
        cs = ctx.enter_context(sbuf(nc, "cs", [P, 2, KT, B], F32))
        rep = ctx.enter_context(sbuf(nc, "rep", [P, 2 * KT * B, P], F32))
        wm = ctx.enter_context(sbuf(nc, "wm", [P, 2, KT, NMOD], F32))
        sign = ctx.enter_context(sbuf(nc, "sign", [P, 2, B, D], F32))
        with nc.Block() as block:
            @block.sync
            def _(sp):
                for l in range(2):
                    sp.dma_start(ct[:, l], k.ins[f"c{l}"]).then_inc(c_in, 16)
                sp.dma_start(k.cf[:], k.ins["cf"]).then_inc(const_in, 16)
                sp.dma_start(k.cb[:], k.ins["cb"]).then_inc(const_in, 16)
                sp.dma_start(k.x[:], k.ins["x"]).then_inc(const_in, 16)
                sp.wait_ge(const_in, 48)

            @block.scalar
            def _(act):
                for l in range(2):
                    act.dma_start(wm[:, l], k.ins[f"wmod{l}"]).then_inc(c_in, 16)
                act.wait_ge(c_in, 64)
                nc.scalar.activation(cs[:], ct[:], ACT.Silu).then_inc(silu_done, 1)

            @block.tensor
            def _(pe):
                pe.wait_ge(rep_done, 1)
                pe.wait_ge(c_in, 64)
                n = 0
                for l in range(2):
                    for b in range(B):
                        for c in range(3):
                            if n >= 8:
                                pe.wait_ge(rows_used, n - 7)
                            for kt in range(KT):
                                last = nc.tensor.matmul(k.ps[:, n % 8, :], rep[:, (l * KT + kt) * B + b, :],
                                                        wm[:, l, kt, 512 * c:512 * c + 512],
                                                        start=kt == 0, stop=kt == KT - 1)
                            last.then_inc(rows_full, 1)
                            n += 1

            @block.vector
            def _(dve):
                step = Steps(dve, dve_step)
                dve.wait_ge(silu_done, 1)
                nc.vector.tensor_copy(rep[:], cs[:].rearrange("p l k b -> p (l k b)").unsqueeze(2)
                                      .broadcast_to([P, 2 * KT * B, P])).then_inc(rep_done, 1)
                n = 0
                for l in range(2):
                    for b in range(B):
                        for c in range(3):
                            dve.wait_ge(rows_full, n + 1)
                            nc.vector.tensor_copy(k.mod[:, l, b, 512 * c:512 * c + 512],
                                                  k.ps[:, n % 8, :]).then_inc(rows_used, 1)
                            n += 1
                dve.wait_ge(rows_used, n)
                m = k.mod[:].rearrange("p l b (s d) -> p (l b) s d", d=D)
                for s in (1, 4):
                    step(nc.vector.tensor_scalar_add(m[:, :, s, :], m[:, :, s, :], 1.0))
                sg = sign[:].rearrange("p l b d -> p (l b) d")
                for s in (2, 5):
                    step(nc.vector.tensor_scalar(sg, m[:, :, s, :], 0.0, 2.0, ALU.is_ge, ALU.mult))
                    step(nc.vector.tensor_scalar_add(sg, sg, -1.0))
                    step(nc.vector.tensor_tensor(m[:, :, s, :], m[:, :, s, :], sg, ALU.mult))
                    step(nc.vector.scalar_tensor_tensor(m[:, :, s, :], m[:, :, s, :], 0.25, sg, ALU.max, ALU.mult))


def norm_stage(nc, k, layer, shift, h_dram=None):
    with stage(nc, "moments", "root", "scaled", "hT_full", "hT_used", "dve_step", "h_out") as (
            moments, root, scaled, hT_full, hT_used, dve_step, h_out), ExitStack() as ctx:
        st = ctx.enter_context(sbuf(nc, "st", [P, NT, 6], F32))
        mv = ctx.enter_context(sbuf(nc, "mv", [P, NT, 2], F32))
        rt = ctx.enter_context(sbuf(nc, "rt", [P, NT], F32))
        with nc.Block() as block:
            @block.vector
            def _(dve):
                step = Steps(dve, dve_step)
                for t in range(NT):
                    last = nc.vector.bn_stats(st[:, t], k.x[:, t])
                step(last)
                for t in range(NT):
                    last = nc.vector.bn_aggr(mv[:, t], st[:, t])
                step(last)
                nc.vector.tensor_scalar_add(rt[:], mv[:, :, 1], 1e-5).then_inc(moments, 1)
                dve.wait_ge(root, 1)
                step(nc.vector.reciprocal(rt[:], rt[:]))
                for t in range(NT):
                    b = t // TB
                    step(nc.vector.tensor_scalar(k.h[:, t], k.x[:, t], mv[:, t, 0:1], rt[:, t:t + 1],
                                                 ALU.subtract, ALU.mult))
                    step(nc.vector.tensor_tensor(k.h[:, t], k.h[:, t],
                                                 k.mod[:, layer, b, (shift + 1) * D:(shift + 2) * D], ALU.mult))
                    nc.vector.tensor_tensor(k.h[:, t], k.h[:, t],
                                            k.mod[:, layer, b, shift * D:(shift + 1) * D],
                                            ALU.add).then_inc(scaled, 1)

            @block.scalar
            def _(act):
                act.wait_ge(moments, 1)
                nc.scalar.activation(rt[:], rt[:], ACT.Sqrt).then_inc(root, 1)
                for n in range(2 * KT):
                    kt, half = n % KT, n // KT
                    act.wait_ge(hT_full, n + 1)
                    nc.scalar.copy(k.hT[:, kt, half * T:(half + 1) * T], k.ps[:, n, :]).then_inc(hT_used, 1)

            @block.tensor
            def _(pe):
                for n in range(2 * KT):
                    kt, half = n % KT, n // KT
                    for q in range(TB):
                        t = half * TB + q
                        if kt == 0:
                            pe.wait_ge(scaled, t + 1)
                        last = nc.tensor.transpose(k.ps[:, n, q * P:(q + 1) * P],
                                                   k.h[:, t, kt * P:(kt + 1) * P], k.identf)
                    last.then_inc(hT_full, 1)

            @block.sync
            def _(sp):
                if h_dram is not None:
                    sp.wait_ge(scaled, NT)
                    sp.dma_start(h_dram.rearrange("(t p) d -> p t d", p=P), k.h[:]).then_inc(h_out, 16)
                    sp.wait_ge(h_out, 16)


def attention_stage(nc, k, attn):
    names = ["w0_in", "w1_in", "bias_in", "pj0_full", "pj1_full", "pj0_used", "pj1_used", "s_full", "max_done",
             "p_done", "sums_inv", "p_scaled", "t0_full", "t1_full", "t0_used", "t1_used", "o_full", "o_used"]
    with stage(nc, *names) as sems, ExitStack() as ctx:
        (w0_in, w1_in, bias_in, pj0_full, pj1_full, pj0_used, pj1_used, s_full, max_done, p_done, sums_inv,
         p_scaled, t0_full, t1_full, t0_used, t1_used, o_full, o_used) = sems
        w_in = [w0_in, w1_in]
        pj_full, pj_used = [pj0_full, pj1_full], [pj0_used, pj1_used]

        def sb(name, shape, dt=F32):
            return ctx.enter_context(sbuf(nc, name, shape, dt))

        w = sb("w", [P, 2, 3, KT, HD])
        bias = sb("bias", [P, 3, HEADS])
        qT = sb("qT", [P, 2, TOK])
        kT = sb("kT", [P, 2, TOK])
        v = sb("v", [P, 2, NT, HD])
        at = {3: (0, 512), 2: (512, 896), 0: (896, 1024), 1: (1024, 1280)}
        pr = sb("pr", [P, 2, 1280])
        nmax = sb("nmax", [P, 2, TB])
        sums = sb("sums", [P, 2, TB])
        inv = sb("inv", [P, 2, TB])
        pt = sb("pt", [P, 2, 1280])
        pt_at = [0, 512, 1024, 896]
        PJ, S0, T0, O = 0, 2, 5, 7
        s_banks = [[(3, 0)], [(2, 0), (0, 384)], [(1, 0)]]

        with nc.Block() as block:
            @block.sync
            def _(sp):
                sp.dma_start(bias[:], k.ins["b_qkv"]).then_inc(bias_in, 16)
                for h in range(2):
                    sp.dma_start(w[:, h], k.ins["w_qkv"][h]).then_inc(w_in[h], 16)

                def load(h, slot):
                    sp.wait_ge(pj_full[1], 3 * (h - 1))
                    sp.dma_start(w[:, slot], k.ins["w_qkv"][bass.ds(h, 1)].rearrange("o p a b c -> (o p) a b c")
                                 ).then_inc(w_in[slot], 16)

                with sp.Fori(1, HEADS // 2) as pair:
                    load(2 * pair, 0)
                    load(2 * pair + 1, 1)

            @block.tensor
            def _(pe):
                pe.wait_ge(bias_in, 16)
                fill = [0, 0]

                def project(h, slot, parts):
                    if "q" in parts:
                        pe.wait_ge(w_in[slot], 8 * (h - slot) + 16)
                    for i, what in enumerate("qkv"):
                        if what not in parts:
                            continue
                        for bank in range(2):
                            if not (isinstance(h, int) and h == 0 and i == 0):
                                pe.wait_ge(pj_used[bank], 3 * h + i)
                            if what == "v":
                                for q in range(TB):
                                    t = bank * TB + q
                                    for kt in range(KT):
                                        last = nc.tensor.matmul(k.ps[:, PJ + bank, q * HD:(q + 1) * HD],
                                                                k.hT[:, kt, t * P:(t + 1) * P], w[:, slot, i, kt],
                                                                start=kt == 0, stop=kt == KT - 1)
                            else:
                                for kt in range(KT):
                                    last = nc.tensor.matmul(k.ps[:, PJ + bank, :], w[:, slot, i, kt],
                                                            k.hT[:, kt, bank * T:(bank + 1) * T],
                                                            start=kt == 0, stop=kt == KT - 1)
                            last.then_inc(pj_full[bank], 1)

                def scores(h, slot, b):
                    u = 2 * h + b
                    pe.wait_ge(pj_used[b], 3 * h + 2)
                    for n, tiles in enumerate(s_banks):
                        if not (isinstance(u, int) and u == 0):
                            pe.wait_ge(p_done, 3 * u + n - 2)
                        for q, col in tiles:
                            nk = (q + 1) * P
                            nc.tensor.matmul(k.ps[:, S0 + n, col:col + nk],
                                             qT[:, slot, b * T + q * P:b * T + (q + 1) * P],
                                             kT[:, slot, b * T:b * T + nk], start=True, stop=False)
                            last = nc.tensor.matmul(k.ps[:, S0 + n, col + nk - P:col + nk], k.identb, k.future,
                                                    start=False, stop=True)
                        last.then_inc(s_full, 1)

                def values(h, slot, b):
                    u = 2 * h + b
                    pe.wait_ge(p_scaled, u + 1)
                    for n, js in enumerate(([0], [1, 3], [2])):
                        bank = n % 2
                        if n == 1:
                            pe.wait_ge(t1_used, u + 1)
                        else:
                            pe.wait_ge(t0_used, 2 * u + n // 2 + 1)
                        for j in js:
                            for q in range(j, TB):
                                c = pt_at[j] - pt_at[js[0]] + (q - j) * P
                                last = nc.tensor.transpose(k.ps[:, T0 + bank, c:c + P],
                                                           pr[:, b, at[q][0] + j * P:at[q][0] + (j + 1) * P],
                                                           k.identf)
                        last.then_inc(t1_full if bank else t0_full, 1)
                    pe.wait_ge(pj_used[b], 3 * h + 3)
                    pe.wait_ge(t0_used, 2 * u + 3)
                    pe.wait_ge(t1_used, u + 2)
                    pe.wait_ge(o_used, u + 1)
                    for j in range(TB):
                        nq = (TB - j) * P
                        last = nc.tensor.matmul(k.ps[:, O, j * P:], v[:, slot, b * TB + j],
                                                pt[:, b, pt_at[j]:pt_at[j] + nq], start=j == 0, stop=j == TB - 1)
                    last.then_inc(o_full, 1)

                def head(h, slot, last=False):
                    if not last:
                        project(h + 1, 1 - slot, "q")
                    scores(h, slot, 1)
                    values(h, slot, 0)
                    if not last:
                        project(h + 1, 1 - slot, "kv")
                        scores(h + 1, 1 - slot, 0)
                    values(h, slot, 1)

                project(0, 0, "qkv")
                scores(0, 0, 0)
                with pe.Fori(0, HEADS // 2 - 1) as pair:
                    head(2 * pair, 0)
                    head(2 * pair + 1, 1)
                head(HEADS - 2, 0)
                head(HEADS - 1, 1, last=True)

            @block.vector
            def _(dve):
                def evac_q(h, slot):
                    for b in range(B):
                        dve.wait_ge(pj_full[b], 3 * h + 1)
                        nc.vector.tensor_scalar(qT[:, slot, b * T:(b + 1) * T], k.ps[:, PJ + b, :],
                                                bias[:, 0, bass.ds(h, 1)], SCALE, ALU.add, ALU.mult
                                                ).then_inc(pj_used[b], 1)

                def maxima(h, b):
                    u = 2 * h + b
                    for n, tiles in enumerate(s_banks):
                        dve.wait_ge(s_full, 3 * u + n + 1)
                        for q, col in tiles:
                            last = nc.vector.tensor_reduce(nmax[:, b, q:q + 1], k.ps[:, S0 + n, col:col + (q + 1) * P],
                                                           axis=X, op=ALU.max, negate=True)
                        last.then_inc(max_done, 1)

                def invert(h, b):
                    dve.wait_ge(p_done, 3 * (2 * h + b) + 3)
                    nc.vector.reciprocal(inv[:, b], sums[:, b]).then_inc(sums_inv, 1)

                def evac_t(h, b):
                    u = 2 * h + b
                    dve.wait_ge(t0_full, 2 * u + 1)
                    nc.vector.tensor_copy(pt[:, b, 0:512], k.ps[:, T0, :]).then_inc(t0_used, 1)
                    dve.wait_ge(t0_full, 2 * u + 2)
                    nc.vector.tensor_copy(pt[:, b, 1024:1280], k.ps[:, T0, 0:256]).then_inc(t0_used, 1)

                def head(h, slot, last=False):
                    if not last:
                        evac_q(h + 1, 1 - slot)
                    maxima(h, 1)
                    invert(h, 1)
                    evac_t(h, 0)
                    if not last:
                        maxima(h + 1, 0)
                        invert(h + 1, 0)
                    evac_t(h, 1)

                dve.wait_ge(bias_in, 16)
                dve.sem_inc(t0_used, 1)
                evac_q(0, 0)
                maxima(0, 0)
                invert(0, 0)
                with dve.Fori(0, HEADS // 2 - 1) as pair:
                    head(2 * pair, 0)
                    head(2 * pair + 1, 1)
                head(HEADS - 2, 0)
                head(HEADS - 1, 1, last=True)

            @block.gpsimd
            def _(pool):
                def scale(h, b):
                    pool.wait_ge(sums_inv, 2 * h + b + 1)
                    for q in range(TB):
                        s = pr[:, b, at[q][0]:at[q][1]]
                        last = nc.gpsimd.tensor_tensor(s, s, inv[:, b, q:q + 1].broadcast_to([P, (q + 1) * P]), ALU.mult)
                    last.then_inc(p_scaled, 1)

                with pool.Fori(0, HEADS) as h:
                    scale(h, 0)
                    scale(h, 1)

            @block.scalar
            def _(act):
                def evac_kv(h, slot):
                    for b in range(B):
                        act.wait_ge(pj_full[b], 3 * h + 2)
                    for b in range(B):
                        nc.scalar.activation(kT[:, slot, b * T:(b + 1) * T], k.ps[:, PJ + b, :], ACT.Identity,
                                             bias=bias[:, 1, bass.ds(h, 1)]).then_inc(pj_used[b], 1)
                    for b in range(B):
                        act.wait_ge(pj_full[b], 3 * h + 3)
                        nc.scalar.copy(v[:, slot, b * TB:(b + 1) * TB].rearrange("p t d -> p (t d)"),
                                       k.ps[:, PJ + b, :]).then_inc(pj_used[b], 1)

                def exponentials(h, b):
                    u = 2 * h + b
                    if not (isinstance(u, int) and u < 2):
                        act.wait_ge(t0_full, 2 * u - 2)
                    for n, tiles in enumerate(s_banks):
                        act.wait_ge(max_done, 3 * u + n + 1)
                        for q, col in tiles:
                            last = nc.scalar.activation(pr[:, b, at[q][0]:at[q][1]],
                                                        k.ps[:, S0 + n, col:col + (q + 1) * P], ACT.Exp,
                                                        bias=nmax[:, b, q:q + 1], accum_out=sums[:, b, q:q + 1])
                        last.then_inc(p_done, 1)

                def evac_t1(h, b):
                    act.wait_ge(t1_full, 2 * h + b + 1)
                    nc.scalar.copy(pt[:, b, 512:1024], k.ps[:, T0 + 1, :]).then_inc(t1_used, 1)

                def evac_o(h, b):
                    act.wait_ge(o_full, 2 * h + b + 1)
                    nc.scalar.activation(attn[:, bass.ds(2 * h + b, 1)].rearrange("p o t -> p (o t)"), k.ps[:, O, :],
                                         ACT.Identity, bias=bias[:, 2, bass.ds(h, 1)]).then_inc(o_used, 1)

                def head(h, slot, last=False):
                    exponentials(h, 1)
                    evac_t1(h, 0)
                    evac_o(h, 0)
                    if not last:
                        evac_kv(h + 1, 1 - slot)
                        exponentials(h + 1, 0)
                    evac_t1(h, 1)
                    evac_o(h, 1)

                act.wait_ge(bias_in, 16)
                act.sem_inc(t1_used, 1)
                act.sem_inc(o_used, 1)
                evac_kv(0, 0)
                exponentials(0, 0)
                head(0, 0)
                with act.Fori(0, HEADS // 2 - 1) as pair:
                    head(2 * pair + 1, 1)
                    head(2 * pair + 2, 0)
                head(HEADS - 1, 1, last=True)


def attn_out_stage(nc, k, attn, wo):
    with stage(nc, "b_in", "y_full", "y_used", "dve_step") as (b_in, y_full, y_used, dve_step), ExitStack() as ctx:
        bo = ctx.enter_context(sbuf(nc, "bo", [P, D], F32))
        y = ctx.enter_context(sbuf(nc, "y", [P, 2, D], F32))
        with nc.Block() as block:
            @block.sync
            def _(sp):
                sp.dma_start(bo[:], k.ins["b_o"].partition_broadcast(P)).then_inc(b_in, 16)

            @block.tensor
            def _(pe):
                pe.wait_ge(k.wo_in, 16)
                for t in range(NT):
                    b, q = divmod(t, TB)
                    for h in range(HEADS):
                        last = nc.tensor.matmul(k.ps[:, t, 0:D], attn[:, 2 * h + b, q * P:(q + 1) * P], wo[:, h],
                                                start=h == 0, stop=h == HEADS - 1)
                    last.then_inc(y_full, 1)

            @block.vector
            def _(dve):
                step = Steps(dve, dve_step)
                dve.wait_ge(b_in, 16)
                for t in range(NT):
                    dve.wait_ge(y_full, t + 1)
                    step(nc.vector.tensor_tensor(y[:, t % 2], k.ps[:, t, 0:D], bo[:], ALU.add))
                    step(nc.vector.tensor_tensor(y[:, t % 2], y[:, t % 2], k.mod[:, 0, t // TB, 2 * D:3 * D], ALU.mult))
                    nc.vector.tensor_tensor(k.x[:, t], k.x[:, t], y[:, t % 2], ALU.add).then_inc(y_used, 1)


def route_stage(nc, k, n):
    cap, trash, na = CAP[n], E * CAP[n], E * CAP[n] // P
    HIT, OUT = 10.0, -1.0e4
    TAKEN, NONE = 3.0e38, -3.0e38
    names = ["w_in", "logits_full", "key_done", "exp_done", "sel_done", "place_full", "hot_done", "hot_used",
             "rhs_done", "table_full", "dve_step"]
    with stage(nc, *names) as sems, ExitStack() as ctx:
        (w_in, logits_full, key_done, exp_done, sel_done, place_full, hot_done, hot_used, rhs_done, table_full,
         dve_step) = sems

        def sb(name, shape, dt=F32):
            return ctx.enter_context(sbuf(nc, name, shape, dt))

        wr = sb("wr", [P, KT, E])
        lg = sb("lg", [P, NT, E])
        gx = sb("gx", [P, NT, GROUPS + 8 - GTOP])
        gm = sb("gm", [P, NT, 8])
        mx = sb("mx", [P, NT])
        key = sb("key", [P, NT, E + 2])
        rep = sb("rep", [P, NT, E + 2])
        m8 = sb("m8", [P, NT, 8])
        ex = sb("ex", [P, NT, E])
        z = sb("z", [P, NT])
        sel = sb("sel", [P, NT, E])
        selb = sb("selb", [P, NT, E], BF16)
        valid = sb("valid", [P, NT, E])
        sv = sb("sv", [P, NT, E])
        s8 = sb("s8", [P, NT, 8])
        eq = sb("eq", [P, NT, TOPK, E])
        ai = sb("ai", [P, NT, TOPK], I32)
        af = sb("af", [P, NT, TOPK])
        bf = sb("bf", [P, NT, TOPK])
        hot_b = sb("hot_b", [P, 2, TOPK, P], BF16)
        hot_a = sb("hot_a", [P, 2, TOPK, na], BF16)
        rhs = sb("rhs", [P, 2, 2, TOPK, na], BF16)
        iota = k.cb[:, slice(*CB["iota"])]
        before, ones = k.cb[:, slice(*CB["before"])], k.cb[:, slice(*CB["ones"])]
        LOGITS, PLACE, TABLE = 0, 1, 2

        with nc.Block() as block:
            @block.sync
            def _(sp):
                sp.dma_start(wr[:], k.ins[f"router{n}"]).then_inc(w_in, 16)

            @block.tensor
            def _(pe):
                pe.wait_ge(w_in, 16)
                for t in range(NT):
                    for kt in range(KT):
                        last = nc.tensor.matmul(k.ps[:, LOGITS, t * E:(t + 1) * E], k.hT[:, kt, t * P:(t + 1) * P],
                                                wr[:, kt], start=kt == 0, stop=kt == KT - 1)
                last.then_inc(logits_full, 1)
                pe.wait_ge(sel_done, 1)
                for t in range(NT):
                    last = nc.tensor.matmul(k.ps[:, PLACE, t * E:(t + 1) * E], before, selb[:, t],
                                            start=True, stop=t == 0)
                    for u in range(t):
                        last = nc.tensor.matmul(k.ps[:, PLACE, t * E:(t + 1) * E], ones, selb[:, u],
                                                start=False, stop=u == t - 1)
                last.then_inc(place_full, 1)
                for t in range(NT):
                    pe.wait_ge(hot_done, t + 1)
                    for c in range(TOPK):
                        for part in range(2):
                            last = nc.tensor.matmul(k.ps[:, TABLE, 0:na], hot_b[:, t % 2, c], rhs[:, t % 2, part, c],
                                                    start=t + c + part == 0,
                                                    stop=t == NT - 1 and c == TOPK - 1 and part == 1)
                    last.then_inc(hot_used, 1)

            @block.scalar
            def _(act):
                act.wait_ge(key_done, 1)
                nc.scalar.activation(ex[:], key[:, :, 0:E], ACT.Exp).then_inc(exp_done, 1)

            @block.vector
            def _(dve):
                step = Steps(dve, dve_step)
                v = nc.vector
                step(v.memset(gx[:], NONE))
                step(v.memset(key[:], OUT))
                dve.wait_ge(logits_full, 1)
                step(v.tensor_copy(lg[:], k.ps[:, LOGITS, 0:NT * E].rearrange("p (t e) -> p t e", e=E)))
                if n == 1:
                    step(v.tensor_reduce(gx[:, :, 0:GROUPS], lg[:].rearrange("p t (g e) -> p t g e", g=GROUPS),
                                         axis=X, op=ALU.max))
                    for t in range(NT):
                        last = v.max(gm[:, t], gx[:, t, 0:GROUPS])
                    step(last)
                    step(v.memset(gm[:, :, GTOP:8], NONE))
                    for t in range(NT):
                        last = v.match_replace(gx[:, t], gm[:, t], gx[:, t], TAKEN)
                    step(last)
                    step(v.tensor_scalar(gx[:], gx[:], 1.0e38, None, ALU.is_ge))
                    step(v.tensor_tensor(lg[:].rearrange("p t (g e) -> p t g e", g=GROUPS),
                                         lg[:].rearrange("p t (g e) -> p t g e", g=GROUPS),
                                         gx[:, :, 0:GROUPS].unsqueeze(3).broadcast_to([P, NT, GROUPS, E // GROUPS]),
                                         ALU.mult))
                step(v.tensor_reduce(mx[:], lg[:], axis=X, op=ALU.max))
                step(v.tensor_tensor(lg[:], lg[:], mx[:].unsqueeze(2).broadcast_to([P, NT, E]), ALU.subtract))
                v.tensor_scalar_max(key[:, :, 0:E], lg[:], -88.0).then_inc(key_done, 1)
                dve.wait_ge(key_done, 1)
                for t in range(NT):
                    last = v.max(m8[:, t], key[:, t, 0:E])
                step(last)
                step(v.memset(m8[:, :, TOPK:8], OUT))
                for t in range(NT):
                    last = v.match_replace(rep[:, t], m8[:, t], key[:, t], HIT)
                step(last)
                step(v.tensor_scalar(sel[:], rep[:, :, 0:E], HIT / 2, None, ALU.is_ge))
                v.tensor_copy(selb[:], sel[:]).then_inc(sel_done, 1)
                dve.wait_ge(exp_done, 1)
                step(v.tensor_reduce(z[:], ex[:], axis=X, op=ALU.add))
                step(v.reciprocal(z[:], z[:]))
                step(v.tensor_tensor(ex[:], ex[:], z[:].unsqueeze(2).broadcast_to([P, NT, E]), ALU.mult))
                step(v.tensor_tensor(ex[:], ex[:], sel[:], ALU.mult))
                if n == 0:
                    step(v.tensor_reduce(z[:], ex[:], axis=X, op=ALU.add))
                    step(v.tensor_scalar_add(z[:], z[:], 1e-20))
                    step(v.reciprocal(z[:], z[:]))
                    step(v.tensor_tensor(ex[:], ex[:], z[:].unsqueeze(2).broadcast_to([P, NT, E]), ALU.mult))
                else:
                    step(v.tensor_scalar(ex[:], ex[:], ROUTE_SCALE, None, ALU.mult))
                dve.wait_ge(place_full, 1)
                place = k.ps[:, PLACE, 0:NT * E].rearrange("p (t e) -> p t e", e=E)
                base = k.cf[:, slice(*CF[f"base{n}"])].unsqueeze(1).broadcast_to([P, NT, E])
                step(v.tensor_scalar(valid[:], place, float(cap), None, ALU.is_lt))
                step(v.tensor_tensor(ex[:], ex[:], valid[:], ALU.mult))
                step(v.tensor_tensor(sv[:], place, base, ALU.add))
                step(v.tensor_tensor(sv[:], sv[:], valid[:], ALU.mult))
                step(v.scalar_tensor_tensor(sv[:], sv[:], float(trash + 1), sel[:], ALU.add, ALU.mult))
                step(v.tensor_scalar_add(sv[:], sv[:], -1.0))
                for t in range(NT):
                    last = v.max(s8[:, t], sv[:, t])
                step(last)
                top = s8[:, :, 0:TOPK]
                step(v.tensor_copy(k.slot[:], top))
                step(v.tensor_tensor(eq[:], sv[:].unsqueeze(2).broadcast_to([P, NT, TOPK, E]),
                                     top.unsqueeze(3).broadcast_to([P, NT, TOPK, E]), ALU.is_equal))
                step(v.tensor_tensor(eq[:], eq[:], ex[:].unsqueeze(2).broadcast_to([P, NT, TOPK, E]), ALU.mult))
                step(v.tensor_reduce(k.wk[:], eq[:], axis=X, op=ALU.add))
                step(v.tensor_scalar(ai[:], top, -63.5, 1.0 / P, ALU.add, ALU.mult))
                step(v.tensor_copy(af[:], ai[:]))
                step(v.scalar_tensor_tensor(bf[:], af[:], -float(P), top, ALU.mult, ALU.add))
                for t in range(NT):
                    if t >= 2:
                        dve.wait_ge(hot_used, t - 1)
                    s = t % 2
                    v.tensor_tensor(hot_b[:, s], iota.unsqueeze(1).broadcast_to([P, TOPK, P]),
                                    bf[:, t].unsqueeze(2).broadcast_to([P, TOPK, P]), ALU.is_equal)
                    step(v.tensor_tensor(hot_a[:, s], iota[:, 0:na].unsqueeze(1).broadcast_to([P, TOPK, na]),
                                         af[:, t].unsqueeze(2).broadcast_to([P, TOPK, na]), ALU.is_equal))
                    v.tensor_scalar(rhs[:, s, 0], hot_a[:, s], k.cf[:, CF["row"][0]:CF["row"][0] + 1], None, ALU.mult)
                    v.tensor_scalar(rhs[:, s, 1], hot_a[:, s], float(t * P), None, ALU.mult).then_inc(hot_done, 1)
                dve.wait_ge(hot_used, NT)
                step(v.tensor_copy(k.table[:, 0:na], k.ps[:, TABLE, 0:na]))


def expert_stage(nc, k, n, h_dram, y_dram):
    cap = CAP[n]
    per = SLOTS // cap
    U = max(4, per)
    GU = U // per
    XS = min(2, GU)
    WS = 4
    nb = -(-cap // P)
    rows = min(cap, P)
    turns = E // U
    names = ["w0_in", "w1_in", "w2_in", "w3_in", "ids_done", "x0_in", "x1_in", "xT0_full", "xT1_full", "xT0_used",
             "xT1_used", "gu_full", "gate_done", "act_done", "y_full", "y_done", "y0_out", "y1_out", "zero_done", "zero_out",
             "ids_seen"]
    with stage(nc, *names) as sems, ExitStack() as ctx:
        (w0_in, w1_in, w2_in, w3_in, ids_done, x0_in, x1_in, xT0_full, xT1_full, xT0_used, xT1_used, gu_full,
         gate_done, act_done, y_full, y_done, y0_out, y1_out, zero_done, zero_out, ids_seen) = sems
        w_in, x_in, y_out = [w0_in, w1_in, w2_in, w3_in], [x0_in, x1_in], [y0_out, y1_out]
        xT_full, xT_used = [xT0_full, xT1_full], [xT0_used, xT1_used]

        def sb(name, shape, dt=F32):
            return ctx.enter_context(sbuf(nc, name, shape, dt))

        wgu = sb("wgu", [P, WS, KT, 2, F])
        wd = sb("wd", [FH, WS, 2, D])
        ids = sb("ids", [P, XS, SB], I32)
        xe = sb("xe", [P, XS, SB, D])
        xT = sb("xT", [P, XS, KT, SLOTS])
        gate = sb("gate", [FH, 2, cap])
        ac = sb("ac", [FH, 2, 2, cap])
        ye = sb("ye", [P, 2, nb, D])
        zero = sb("zero", [1, D])
        XT, GUB, YB = 0, 2, 6

        with nc.Block() as block:
            @block.sync
            def _(sp):
                def load(e, slot):
                    sp.dma_start(wgu[:, slot], k.ins[f"w_gu{n}"][bass.ds(e, 1)]
                                 .rearrange("o p a b c -> (o p) a b c")).then_inc(w_in[slot], 16)
                    sp.dma_start(wd[:, slot], k.ins[f"w_down{n}"][bass.ds(e, 1)]
                                 .rearrange("o p a b -> (o p) a b")).then_inc(w_in[slot], 16)

                for e in range(WS):
                    load(e, e)
                with sp.Fori(1, E // WS) as turn:
                    for s in range(WS):
                        sp.wait_ge(y_full, WS * turn + (s - WS + 1))
                        load(WS * turn + s, s)

            @block.gpsimd
            def _(pool):
                nc.gpsimd.memset(zero[:], 0.0).then_inc(zero_done, 1)
                def gather(g, slot):
                    nc.gpsimd.tensor_copy(ids[:, slot], k.table[:, bass.ds(g * SB, SB)]).then_inc(ids_done, 1)
                    pool.wait_ge(ids_done, g + 1)
                    pool.sem_inc(ids_seen, 1)
                    for s in range(SB):
                        nc.gpsimd.indirect_dma_start(
                            out=xe[:, slot, s], out_offset=None, in_=h_dram,
                            in_offset=bass.IndirectOffsetOnAxis(ap=ids[:, slot, s:s + 1], axis=0),
                        ).then_inc(x_in[slot], 16)

                for g in range(XS):
                    gather(g, g)
                with pool.Fori(1, E // per // XS) as turn:
                    for s in range(XS):
                        pool.wait_ge(xT_full[1], XS * turn + (s - XS + 1))
                        gather(XS * turn + s, s)

            @block.tensor
            def _(pe):
                def transpose(turn, j):
                    g, slot = turn * GU + j, j % XS
                    pe.wait_ge(x_in[slot], turn * (16 * SB * GU // XS) + 16 * SB * (j // XS + 1))
                    for kt in range(KT):
                        pe.wait_ge(xT_used[kt], g + 1)
                        for s in range(SB):
                            last = nc.tensor.transpose(k.ps[:, XT + kt, s * P:(s + 1) * P],
                                                       xe[:, slot, s, kt * P:(kt + 1) * P], k.identf)
                        last.then_inc(xT_full[kt], 1)

                def gate_up(turn, i):
                    g, slot, col = turn * GU + i // per, (i // per) % XS, (i % per) * cap
                    pe.wait_ge(w_in[i % WS], turn * (32 * U // WS) + 32 * (i // WS + 1))
                    for kt in range(KT):
                        pe.wait_ge(xT_used[kt], g + 2)
                    pe.wait_ge(act_done, turn * U + i + 1)
                    for gu in range(2):
                        for f in range(2):
                            for kt in range(KT):
                                last = nc.tensor.matmul(k.ps[0:FH, GUB + 2 * gu + f, 0:cap],
                                                        wgu[:, i % WS, kt, gu, f * FH:(f + 1) * FH],
                                                        xT[:, slot, kt, col:col + cap],
                                                        start=kt == 0, stop=kt == KT - 1)
                    last.then_inc(gu_full, 1)

                def down(turn, i):
                    pe.wait_ge(act_done, turn * U + i + 2)
                    pe.wait_ge(y_done, turn * U + i + 1)
                    for s in range(nb):
                        for f in range(2):
                            last = nc.tensor.matmul(k.ps[0:rows, YB + s // 2, (s % 2) * D:(s % 2 + 1) * D],
                                                    ac[:, i % 2, f, s * P:s * P + rows], wd[:, i % WS, f],
                                                    start=f == 0, stop=f == 1)
                    last.then_inc(y_full, 1)

                with pe.Fori(0, turns) as turn:
                    transpose(turn, 0)
                    for i in range(U):
                        gate_up(turn, i)
                        if (i + 1) % per == 0 and i + 1 < U:
                            transpose(turn, (i + 1) // per)
                        if i:
                            down(turn, i - 1)
                    down(turn, U - 1)

            @block.scalar
            def _(act):
                def output(turn, i):
                    e, slot = turn * U + i, i % 2
                    act.wait_ge(y_out[slot], turn * (8 * U) + 16 * (i // 2 + 1))
                    act.wait_ge(y_full, e + 1)
                    yf = ye[0:rows, slot].rearrange("p b d -> p (b d)")
                    pf = k.ps[0:rows, YB:YB + 2, :].rearrange("p b d -> p (b d)")
                    nc.scalar.copy(yf, pf[:, 0:nb * D]).then_inc(y_done, 1)
                    act.wait_ge(y_done, e + 2)
                    act.dma_start(y_dram[bass.ds(e * cap, cap), :].rearrange("(s p) d -> p s d", p=rows),
                                  ye[0:rows, slot]).then_inc(y_out[slot], 16)

                act.wait_ge(zero_done, 1)
                act.dma_start(y_dram[E * cap:E * cap + 1, :], zero[:]).then_inc(zero_out, 16)
                act.sem_inc(xT_used[1], 1)
                act.sem_inc(y_done, 1)
                for s in y_out:
                    act.sem_inc(s, 16)
                with act.Fori(0, turns) as turn:
                    for i in range(U):
                        if i % per == 0:
                            act.wait_ge(xT_full[1], turn * GU + i // per + 1)
                            nc.scalar.copy(xT[:, (i // per) % XS, 1], k.ps[:, XT + 1, 0:SLOTS]).then_inc(xT_used[1], 1)
                        act.wait_ge(gu_full, turn * U + i + 1)
                        nc.scalar.activation(gate[:], k.ps[0:FH, GUB:GUB + 2, 0:cap], ACT.Silu).then_inc(gate_done, 1)
                        if i:
                            output(turn, i - 1)
                    output(turn, U - 1)
                for s in y_out:
                    act.wait_ge(s, 16 + 16 * E // 2)
                act.wait_ge(zero_out, 16)

            @block.vector
            def _(dve):
                dve.sem_inc(xT_used[0], 1)
                dve.sem_inc(act_done, 1)
                with dve.Fori(0, turns) as turn:
                    for i in range(U):
                        if i % per == 0:
                            dve.wait_ge(xT_full[0], turn * GU + i // per + 1)
                            nc.vector.tensor_copy(xT[:, (i // per) % XS, 0], k.ps[:, XT, 0:SLOTS]).then_inc(xT_used[0], 1)
                        dve.wait_ge(gate_done, turn * U + i + 1)
                        nc.vector.tensor_tensor(ac[:, i % 2], gate[:], k.ps[0:FH, GUB + 2:GUB + 4, 0:cap],
                                                ALU.mult).then_inc(act_done, 1)


def shared_stage(nc, k, n):
    with stage(nc, "w_in", "gu_full", "gate_done", "act_done", "y_full", "y_done") as (
            w_in, gu_full, gate_done, act_done, y_full, y_done), ExitStack() as ctx:
        wgu = ctx.enter_context(sbuf(nc, "wsgu", [P, KT, 2, FS], F32))
        wd = ctx.enter_context(sbuf(nc, "wsd", [P, 3, D], F32))
        gate = ctx.enter_context(sbuf(nc, "sgate", [P, 2, T], F32))
        ac = ctx.enter_context(sbuf(nc, "sact", [P, 3, TOK], F32))
        with nc.Block() as block:
            @block.sync
            def _(sp):
                sp.dma_start(wgu[:], k.ins[f"ws_gu{n}"]).then_inc(w_in, 16)
                for c, (at, w) in enumerate(FS_CHUNKS):
                    sp.dma_start(wd[0:w, c], k.ins[f"ws_down{n}"][at:at + w, :]).then_inc(w_in, 16)

            @block.tensor
            def _(pe):
                pe.wait_ge(w_in, 64)
                m = 0
                for half in range(2):
                    for at, w in FS_CHUNKS:
                        if m >= 2:
                            pe.wait_ge(act_done, m - 1)
                        for gu in range(2):
                            for kt in range(KT):
                                last = nc.tensor.matmul(k.ps[0:w, 2 * (m % 2) + gu, :], wgu[:, kt, gu, at:at + w],
                                                        k.hT[:, kt, half * T:(half + 1) * T],
                                                        start=kt == 0, stop=kt == KT - 1)
                        last.then_inc(gu_full, 1)
                        m += 1
                for t in range(NT):
                    pe.wait_ge(act_done, 3 * (t // TB + 1))
                    if t >= 4:
                        pe.wait_ge(y_done, t - 3)
                    for c, (at, w) in enumerate(FS_CHUNKS):
                        last = nc.tensor.matmul(k.ps[:, 4 + t % 4, 0:D], ac[0:w, c, t * P:(t + 1) * P], wd[0:w, c],
                                                start=c == 0, stop=c == 2)
                    last.then_inc(y_full, 1)

            @block.scalar
            def _(act):
                m = 0
                for half in range(2):
                    for at, w in FS_CHUNKS:
                        act.wait_ge(gu_full, m + 1)
                        if m >= 2:
                            act.wait_ge(act_done, m - 1)
                        nc.scalar.activation(gate[0:w, m % 2], k.ps[0:w, 2 * (m % 2), :], ACT.Silu).then_inc(gate_done, 1)
                        m += 1
                for t in range(NT):
                    act.wait_ge(y_full, t + 1)
                    nc.scalar.copy(k.sh[:, t], k.ps[:, 4 + t % 4, 0:D]).then_inc(y_done, 1)

            @block.vector
            def _(dve):
                m = 0
                for half in range(2):
                    for c, (at, w) in enumerate(FS_CHUNKS):
                        dve.wait_ge(gate_done, m + 1)
                        nc.vector.tensor_tensor(ac[0:w, c, half * T:(half + 1) * T], gate[0:w, m % 2],
                                                k.ps[0:w, 2 * (m % 2) + 1, :], ALU.mult).then_inc(act_done, 1)
                        m += 1


def combine_stage(nc, k, n, y_dram, out=None):
    with stage(nc, "ids_done", "ids_seen", "g0_in", "g1_in", "tile_done", "dve_step", "out_done") as (
            ids_done, ids_seen, g0_in, g1_in, tile_done, dve_step, out_done), ExitStack() as ctx:
        g_in = [g0_in, g1_in]
        ids = ctx.enter_context(sbuf(nc, "cids", [P, 2, TOPK], I32))
        rows = ctx.enter_context(sbuf(nc, "rows", [P, 2, TOPK, D], F32))
        acc = ctx.enter_context(sbuf(nc, "acc", [P, 2, D], F32))
        STEPS = TOPK + 1
        with nc.Block() as block:
            @block.gpsimd
            def _(pool):
                def gather(t, slot):
                    nc.gpsimd.tensor_copy(ids[:, slot], k.slot[:, bass.ds(t, 1)].rearrange("p o c -> p (o c)")
                                          ).then_inc(ids_done, 1)
                    pool.wait_ge(ids_done, t + 1)
                    pool.sem_inc(ids_seen, 1)
                    for c in range(TOPK):
                        nc.gpsimd.indirect_dma_start(
                            out=rows[:, slot, c], out_offset=None, in_=y_dram,
                            in_offset=bass.IndirectOffsetOnAxis(ap=ids[:, slot, c:c + 1], axis=0),
                        ).then_inc(g_in[slot], 16)

                for t in range(2):
                    gather(t, t)
                with pool.Fori(1, NT // 2) as turn:
                    for s in range(2):
                        pool.wait_ge(tile_done, 2 * turn + s - 1)
                        gather(2 * turn + s, s)

            @block.vector
            def _(dve):
                v = nc.vector
                for b in range(B):
                    with dve.Fori(0, TB // 2) as turn:
                        for s in range(2):
                            t = turn * 2 + (b * TB + s)
                            dve.wait_ge(g_in[s], turn * (16 * TOPK) + 16 * TOPK * (b * TB // 2 + 1))
                            step = Steps(dve, dve_step, t * STEPS)
                            x = k.x[:, bass.ds(t, 1)].rearrange("p o d -> p (o d)")
                            sh = k.sh[:, bass.ds(t, 1)].rearrange("p o d -> p (o d)")
                            for c in range(TOPK):
                                step(v.scalar_tensor_tensor(
                                    acc[:, s], rows[:, s, c], k.wk[:, bass.ds(t, 1), c].rearrange("p o -> p o"),
                                    sh if c == 0 else acc[:, s], ALU.mult, ALU.add))
                            step(v.tensor_tensor(acc[:, s], acc[:, s], k.mod[:, n, b, 5 * D:6 * D], ALU.mult))
                            v.tensor_tensor(x, x, acc[:, s], ALU.add).then_inc(tile_done, 1)

            @block.sync
            def _(sp):
                if out is not None:
                    sp.wait_ge(tile_done, NT)
                    sp.dma_start(out, k.x[:]).then_inc(out_done, 16)
                    sp.wait_ge(out_done, 16)


SK, SKB, SQ, SQG, SKBG, SKE, SVB = range(7)


def delta_project_stage(nc, k, qkv, gate, g, scl, tot):
    names = ["w_in", "v_in", "ab_full", "x0_full", "x1_full", "x0_used", "x1_used", "conv_done", "t_full", "t_used",
             "gate_full", "gate_used", "abs_done", "exp_done", "sig_done", "sq_done", "root_done", "g_done",
             "cum_full", "cum_done", "dve_step"]
    with stage(nc, *names) as sems, ExitStack() as ctx:
        (w_in, v_in, ab_full, x0_full, x1_full, x0_used, x1_used, conv_done, t_full, t_used, gate_full, gate_used,
         abs_done, exp_done, sig_done, sq_done, root_done, g_done, cum_full, cum_done, dve_step) = sems
        x_full, x_used = [x0_full, x1_full], [x0_used, x1_used]

        def sb(name, shape, dt=F32):
            return ctx.enter_context(sbuf(nc, name, shape, dt))

        NGAB = DH * DV + 2 * DH
        wq = sb("wq", [P, KT, QKV])
        wg = sb("wg", [P, KT, NGAB])
        cw = sb("cw", [CH, NCH, TAPS])
        al = sb("al", [P, 2, DH])
        cv = sb("cv", [CH, 2, T])
        ab = sb("ab", [P, NT, 2 * DH])
        xa = sb("xa", [P, NT, DH])
        u = sb("u", [P, NT, DH])
        s = sb("s", [P, NT, DH])
        s2 = sb("s2", [P, NT, DH])
        pl = sb("pl", [P, NT, DH])
        sq = sb("sq", [P, NT, 2 * DH * DK])
        ss = sb("ss", [P, NT, 2 * DH])
        cum = sb("cum", [P, 2, NT, DH])
        XB, TBK, GB, AB, CUM = 0, 2, 4, 6, 7

        with nc.Block() as block:
            @block.sync
            def _(sp):
                sp.dma_start(wg[:], k.ins["w_gab"]).then_inc(w_in, 16)
                sp.dma_start(wq[:], k.ins["w_qkv1"]).then_inc(w_in, 16)
                sp.dma_start(cw[:], k.ins["conv"]).then_inc(v_in, 16)
                sp.dma_start(al[:, 0], k.ins["A_log"].partition_broadcast(P)).then_inc(v_in, 16)
                sp.dma_start(al[:, 1], k.ins["dt_bias"].partition_broadcast(P)).then_inc(v_in, 16)

            @block.tensor
            def _(pe):
                pe.wait_ge(w_in, 32)
                for t in range(NT):
                    for kt in range(KT):
                        last = nc.tensor.matmul(k.ps[:, AB, t * 2 * DH:(t + 1) * 2 * DH], k.hT[:, kt, t * P:(t + 1) * P],
                                                wg[:, kt, DH * DV:], start=kt == 0, stop=kt == KT - 1)
                last.then_inc(ab_full, 1)

                def project(m):
                    c, b = divmod(m, B)
                    if m >= 2:
                        pe.wait_ge(x_used[m % 2], m // 2)
                    for kt in range(KT):
                        last = nc.tensor.matmul(k.ps[0:CH, XB + m % 2, :], wq[:, kt, c * CH:(c + 1) * CH],
                                                k.hT[:, kt, b * T:(b + 1) * T], start=kt == 0, stop=kt == KT - 1)
                    last.then_inc(x_full[m % 2], 1)

                def transpose(m):
                    pe.wait_ge(conv_done, m + 1)
                    if m >= 2:
                        pe.wait_ge(t_used, m - 1)
                    for q in range(TB):
                        last = nc.tensor.transpose(k.ps[:, TBK + m % 2, q * CH:(q + 1) * CH], cv[:, m % 2, q * P:(q + 1) * P],
                                                   k.identf[0:CH, 0:CH])
                    last.then_inc(t_full, 1)

                project(0)
                for m in range(1, B * NCH):
                    project(m)
                    if m % 2:
                        t = m // 2
                        if t >= 2:
                            pe.wait_ge(gate_used, t - 1)
                        for kt in range(KT):
                            last = nc.tensor.matmul(k.ps[:, GB + t % 2, 0:DH * DV], k.hT[:, kt, t * P:(t + 1) * P],
                                                    wg[:, kt, 0:DH * DV], start=kt == 0, stop=kt == KT - 1)
                        last.then_inc(gate_full, 1)
                    transpose(m - 1)
                transpose(B * NCH - 1)
                pe.wait_ge(g_done, 1)
                gf = g[:].rearrange("p t h -> p (t h)")
                n = NT * DH
                nc.tensor.matmul(k.ps[:, CUM, 0:n], k.cf[:, slice(*CF["upto"])], gf, start=True, stop=True)
                nc.tensor.matmul(k.ps[:, CUM, n:2 * n], k.cf[:, slice(*CF["after"])], gf, start=True, stop=True)
                nc.tensor.matmul(k.ps[0:DK, CUM, 2 * n:3 * n], k.cf[:, slice(*CF["ones"])], gf,
                                 start=True, stop=True).then_inc(cum_full, 1)

            @block.scalar
            def _(act):
                for m in range(B * NCH):
                    c, b = divmod(m, B)
                    act.wait_ge(t_full, m + 1)
                    nc.scalar.activation(qkv[:, b * TB:(b + 1) * TB, c * CH:(c + 1) * CH],
                                         k.ps[:, TBK + m % 2, 0:TB * CH].rearrange("p (t c) -> p t c", c=CH),
                                         ACT.Silu).then_inc(t_used, 1)
                    if m % 2:
                        t = m // 2
                        act.wait_ge(gate_full, t + 1)
                        nc.scalar.activation(gate[:, t], k.ps[:, GB + t % 2, 0:DH * DV], ACT.Silu).then_inc(gate_used, 1)
                act.wait_ge(abs_done, 1)
                act.wait_ge(v_in, 48)
                nc.scalar.activation(al[:, 0], al[:, 0], ACT.Exp)
                nc.scalar.activation(u[:], u[:], ACT.Exp).then_inc(exp_done, 1)
                nc.scalar.activation(scl[:, :, SVB], ab[:, :, DH:2 * DH], ACT.Sigmoid).then_inc(sig_done, 1)
                act.wait_ge(sq_done, 1)
                nc.scalar.activation(ss[:], ss[:], ACT.Sqrt).then_inc(root_done, 1)
                act.wait_ge(cum_full, 1)
                n = NT * DH
                nc.scalar.activation(cum[:].rearrange("p a t h -> p (a t h)"), k.ps[:, CUM, 0:2 * n], ACT.Exp)
                nc.scalar.activation(tot[:].rearrange("p t h -> p (t h)"), k.ps[0:DK, CUM, 2 * n:3 * n],
                                     ACT.Exp).then_inc(cum_done, 1)

            @block.vector
            def _(dve):
                step = Steps(dve, dve_step)
                v = nc.vector
                dve.wait_ge(v_in, 48)
                dve.wait_ge(ab_full, 1)
                step(v.tensor_copy(ab[:], k.ps[:, AB, 0:NT * 2 * DH].rearrange("p (t c) -> p t c", c=2 * DH)))
                step(v.tensor_tensor(xa[:], ab[:, :, 0:DH], al[:, 1].unsqueeze(1).broadcast_to([P, NT, DH]), ALU.add))
                v.scalar_tensor_tensor(u[:], xa[:], -1.0, xa[:], ALU.mult, ALU.min).then_inc(abs_done, 1)
                for m in range(B * NCH):
                    c, b = divmod(m, B)
                    dve.wait_ge(x_full[m % 2], m // 2 + 1)
                    if m >= 2:
                        dve.wait_ge(t_full, m - 1)
                    y, x = cv[:, m % 2], k.ps[0:CH, XB + m % 2, :]
                    step(v.tensor_scalar(y, x, cw[:, c, TAPS - 1:TAPS], None, ALU.mult))
                    for back in range(1, TAPS):
                        ins = v.scalar_tensor_tensor(y[:, back:], x[:, 0:T - back], cw[:, c, TAPS - 1 - back:TAPS - back],
                                                     y[:, back:], ALU.mult, ALU.add)
                        if back < TAPS - 1:
                            step(ins)
                    ins.then_inc(conv_done, 1)
                    dve.wait_ge(conv_done, m + 1)
                    dve.sem_inc(x_used[m % 2], 1)
                dve.wait_ge(exp_done, 1)
                step(v.tensor_scalar_add(s[:], u[:], 2.0))
                step(v.reciprocal(s[:], s[:]))
                step(v.tensor_tensor(s[:], s[:], u[:], ALU.mult))
                step(v.tensor_tensor(s2[:], s[:], s[:], ALU.mult))
                step(v.tensor_scalar(pl[:], s2[:], 1.0 / 17, None, ALU.mult))
                for d in (15, 13, 11, 9, 7, 5, 3):
                    step(v.scalar_tensor_tensor(pl[:], pl[:], 1.0 / d, s2[:], ALU.add, ALU.mult))
                step(v.scalar_tensor_tensor(pl[:], pl[:], 1.0, s[:], ALU.add, ALU.mult))
                step(v.tensor_scalar(xa[:], xa[:], 0.0, None, ALU.max))
                step(v.scalar_tensor_tensor(xa[:], pl[:], 2.0, xa[:], ALU.mult, ALU.add))
                v.scalar_tensor_tensor(g[:], xa[:], -1.0, al[:, 0].unsqueeze(1).broadcast_to([P, NT, DH]),
                                       ALU.mult, ALU.mult).then_inc(g_done, 1)
                dve.wait_ge(t_used, B * NCH)
                qk = qkv[:, :, 0:2 * DH * DK]
                step(v.tensor_tensor(sq[:], qk, qk, ALU.mult))
                step(v.tensor_reduce(ss[:], sq[:].rearrange("p t (h d) -> p t h d", d=DK), axis=X, op=ALU.add))
                v.tensor_scalar_add(ss[:], ss[:], 1e-6).then_inc(sq_done, 1)
                dve.wait_ge(root_done, 1)
                step(v.reciprocal(ss[:], ss[:]))
                dve.wait_ge(sig_done, 1)
                dve.wait_ge(cum_done, 1)
                rq, rk, beta = ss[:, :, 0:DH], ss[:, :, DH:2 * DH], scl[:, :, SVB]
                step(v.tensor_copy(scl[:, :, SK], rk))
                step(v.tensor_tensor(scl[:, :, SKB], rk, beta, ALU.mult))
                step(v.tensor_scalar(scl[:, :, SQ], rq, float(DK) ** -0.5, None, ALU.mult))
                step(v.tensor_tensor(scl[:, :, SQG], scl[:, :, SQ], cum[:, 0], ALU.mult))
                step(v.tensor_tensor(scl[:, :, SKBG], scl[:, :, SKB], cum[:, 0], ALU.mult))
                step(v.tensor_tensor(scl[:, :, SKE], rk, cum[:, 1], ALU.mult))


def delta_stage(nc, k, qkv, g, scl, tot, o_all):
    HP = DH * P
    HB = HP // 2
    NL = len(LEVELS)
    L_KT, L_QT, L_D, L_KQ, L_P, L_W1T, L_O, NLF = 0, 1, 2, 3, 4, 4 + 2 * NL, 5 + 2 * NL, 6 + 2 * NL
    R_KBT, R_QGT, R_KK, R_X0, R_XP, R_W1, R_DELTA, R_S, NRF = 0, 1, 2, 3, 4, 3 + NL, 4 + NL, 5 + NL, 6 + NL
    names = []
    for b in range(B):
        names += [f"l{b}_full", f"l{b}_used", f"r{b}_full", f"r{b}_used", f"prep{b}_done", f"decay{b}_done",
                  f"y{b}_done", f"lev{b}_done", f"pool{b}_step", f"s{b}_step", f"state{b}_zero"]
    with stage(nc, *names) as sems, ExitStack() as ctx:
        per = len(names) // B
        (l_full, l_used, r_full, r_used, prep_done, decay_done, y_done, lev_done, pool_step, s_step, s_zero) = (
            [sems[b * per + i] for b in range(B)] for i in range(per))

        def sb(name, shape, dt=F32):
            return [ctx.enter_context(sbuf(nc, f"{name}{b}", shape, dt)) for b in range(B)]

        mats = sb("mats", [P, 4, DH, DK])
        ke = sb("ke", [P, DH, DK])
        wr = sb("wr", [P, DH, DV + DK])
        matT = sb("matT", [DK, 4, 2, HB])
        ex = sb("ex", [P, 2, HB])
        spare = [[buf[:].rearrange("p t d -> p (t d)")[:, i * HP:(i + 1) * HP].rearrange("p (a n) -> p a n", a=2)
                  for i in range(2)] for buf in (k.h, k.sh)]
        at, mt = [spare[b][0] for b in range(B)], [spare[b][1] for b in range(B)]
        RING = 2
        lev = sb("lev", [P, RING, 2, HB])
        xx = sb("xx", [P, 2, HB])
        yy = sb("yy", [P, 2, HB])
        pp = sb("pp", [P, 2, HB])
        gs = [x[:].rearrange("p a (h j) -> p (a h) j", j=P) for x in pp]
        w1 = sb("w1", [P, 2, DH // 2, DV + DK])
        w1t = sb("w1t", [DK, 2, HB])
        de = sb("de", [P, DH, DV])
        state = sb("state", [DK, DH, DV])
        base = CF["lev"][0]

        def bank(b, side):
            return 4 * b + 2 * side

        def pair(b, side, p=P, w=HB):
            return k.ps[0:p, bank(b, side):bank(b, side) + 2, 0:w]

        def at_head(b, side, h, p=P, w=P):
            c = (h % 3) * w
            return k.ps[0:p, bank(b, side) + h // 3, c:c + w]

        def head(t, h, w=P):
            return t[:, h // 3, (h % 3) * w:(h % 3 + 1) * w]

        with nc.Block() as block:
            @block.gpsimd
            def _(pool):
                g_ = nc.gpsimd
                for b in range(B):
                    g_.memset(state[b][:], 0.0).then_inc(s_zero[b], 1)

                def prepare(c, b):
                    t = c + b * TB
                    pool.wait_ge(r_used[b], c * NRF + 1)

                    def scaled(out, at_, width, m):
                        src = qkv[:, bass.ds(t, 1), at_:at_ + DH * width].rearrange("p o (h d) -> p (o h) d", d=width)
                        sc = scl[:, bass.ds(t, 1), m].rearrange("p o h -> p (o h)").unsqueeze(2)
                        return g_.tensor_tensor(out, src, sc.broadcast_to([P, DH, width]), ALU.mult)

                    q_at, k_at, v_at = 0, DH * DK, 2 * DH * DK
                    scaled(mats[b][:, 0], k_at, DK, SK)
                    scaled(mats[b][:, 1], k_at, DK, SKB)
                    scaled(mats[b][:, 2], q_at, DK, SQ)
                    scaled(mats[b][:, 3], q_at, DK, SQG)
                    scaled(ke[b][:], k_at, DK, SKE)
                    scaled(wr[b][:, :, 0:DV], v_at, DV, SVB)
                    scaled(wr[b][:, :, DV:], k_at, DK, SKBG).then_inc(prep_done[b], 1)

                def mask(i):
                    return k.cf[:, base + i * P:base + (i + 1) * P].unsqueeze(1).broadcast_to([P, DH, P])

                def heads_of(t):
                    return t.rearrange("p a (h i) -> p (a h) i", i=P)

                def first(c, b):
                    y = heads_of(yy[b][:])
                    pool.wait_ge(r_used[b], c * NRF + R_KK + 2)
                    g_.tensor_tensor(y, heads_of(at[b]), mask(0), ALU.mult).then_inc(pool_step[b], 1)
                    pool.wait_ge(pool_step[b], c + 1)
                    g_.tensor_tensor(y, k.identf.unsqueeze(1).broadcast_to([P, DH, P]), y,
                                     ALU.subtract).then_inc(y_done[b], 1)

                def level(c, b, i):
                    if i >= RING:
                        pool.wait_ge(l_full[b], c * NLF + (L_P + 2 * (i - RING) + 1))
                    g_.tensor_tensor(heads_of(lev[b][:, i % RING]), heads_of(at[b]), mask(i + 1),
                                     ALU.mult).then_inc(lev_done[b], 1)

                with pool.Fori(0, TB) as c:
                    for b in range(B):
                        prepare(c, b)
                    for b in range(B):
                        first(c, b)
                    for i in range(NL):
                        for b in range(B):
                            level(c, b, i)

            @block.tensor
            def _(pe):
                def left_free(c, b, i):
                    pe.wait_ge(l_used[b], c * NLF + i + 1)

                def left_there(c, b, i):
                    pe.wait_ge(l_used[b], c * NLF + i + 2)

                def right_free(c, b, i):
                    pe.wait_ge(r_used[b], c * NRF + i + 1)

                def right_there(c, b, i):
                    pe.wait_ge(r_used[b], c * NRF + i + 2)

                def transposes(c, b, side, m, i):
                    (right_free if side else left_free)(c, b, i)
                    for h in range(DH):
                        last = nc.tensor.transpose(at_head(b, side, h, DK), mats[b][:, m, h], k.identf)
                    last.then_inc((r_full if side else l_full)[b], 1)

                for b in range(B):
                    pe.wait_ge(s_zero[b], 1)
                with pe.Fori(0, TB) as c:
                    for b in range(B):
                        pe.wait_ge(prep_done[b], c + 1)
                        transposes(c, b, 0, 0, L_KT)
                        transposes(c, b, 1, 1, R_KBT)
                        transposes(c, b, 0, 2, L_QT)
                        transposes(c, b, 1, 3, R_QGT)
                    for b in range(B):
                        pe.wait_ge(decay_done[b], c + 1)
                        left_free(c, b, L_D)
                        for h in range(DH):
                            nc.tensor.matmul(at_head(b, 0, h), gs[b][:, h], k.cf[:, slice(*CF["upto"])],
                                             start=True, stop=False)
                            last = nc.tensor.matmul(at_head(b, 0, h), k.identb, k.cb[:, slice(*CB["past"])],
                                                    start=False, stop=True)
                        last.then_inc(l_full[b], 1)
                    for b in range(B):
                        right_free(c, b, R_KK)
                        left_there(c, b, L_KT)
                        for h in range(DH):
                            last = nc.tensor.matmul(at_head(b, 1, h), head(matT[b][:, 0], h), head(matT[b][:, 1], h),
                                                    start=True, stop=True)
                        last.then_inc(r_full[b], 1)
                    for b in range(B):
                        left_free(c, b, L_KQ)
                        for h in range(DH):
                            last = nc.tensor.matmul(at_head(b, 0, h), head(matT[b][:, 0], h), head(matT[b][:, 2], h),
                                                    start=True, stop=True)
                        last.then_inc(l_full[b], 1)
                    for b in range(B):
                        right_free(c, b, R_X0)
                        pe.wait_ge(y_done[b], c + 1)
                        for h in range(DH):
                            last = nc.tensor.transpose(at_head(b, 1, h), head(yy[b], h), k.identf)
                        last.then_inc(r_full[b], 1)
                    for i in range(NL):
                        for b in range(B):
                            left_free(c, b, L_P + 2 * i)
                            pe.wait_ge(lev_done[b], c * NL + i + 1)
                            right_there(c, b, R_X0 + i)
                            for h in range(DH):
                                last = nc.tensor.matmul(at_head(b, 0, h), head(lev[b][:, i % RING], h), head(xx[b], h),
                                                        start=True, stop=True)
                            last.then_inc(l_full[b], 1)
                        for b in range(B):
                            left_there(c, b, L_P + 2 * i)
                            if i < NL - 1:
                                right_free(c, b, R_XP + i)
                                for h in range(DH):
                                    last = nc.tensor.matmul(at_head(b, 1, h), head(yy[b], h), head(pp[b], h),
                                                            start=True, stop=True)
                                last.then_inc(r_full[b], 1)
                            for h in range(DH):
                                last = nc.tensor.matmul(at_head(b, 0, h), head(pp[b], h), head(yy[b], h),
                                                        start=True, stop=True)
                            last.then_inc(l_full[b], 1)
                    for b in range(B):
                        left_there(c, b, L_P + 2 * NL - 1)
                        right_free(c, b, R_W1)
                        for h in range(DH):
                            last = nc.tensor.matmul(at_head(b, 1, h, P, DV + DK), head(yy[b], h), wr[b][:, h],
                                                    start=True, stop=True)
                        last.then_inc(r_full[b], 1)
                        for h in range(DH):
                            last = nc.tensor.matmul(at_head(b, 0, h, DK), wr[b][:, h, DV:], head(yy[b], h),
                                                    start=True, stop=True)
                        last.then_inc(l_full[b], 1)
                    for b in range(B):
                        left_there(c, b, L_W1T)
                        right_free(c, b, R_DELTA)
                        for h in range(DH):
                            last = nc.tensor.matmul(k.ps[:, bank(b, 1), h * DV:(h + 1) * DV], head(w1t[b], h),
                                                    state[b][:, h], start=True, stop=True)
                        last.then_inc(r_full[b], 1)
                    for b in range(B):
                        right_there(c, b, R_DELTA)
                        left_free(c, b, L_O)
                        for h in range(DH):
                            o = k.ps[:, bank(b, 0), h * DV:(h + 1) * DV]
                            nc.tensor.matmul(o, head(matT[b][:, 3], h), state[b][:, h], start=True, stop=False)
                            last = nc.tensor.matmul(o, head(mt[b], h), de[b][:, h], start=False, stop=True)
                        last.then_inc(l_full[b], 1)
                        for h in range(DH):
                            last = nc.tensor.matmul(k.ps[0:DK, bank(b, 1), h * DV:(h + 1) * DV], ke[b][:, h],
                                                    de[b][:, h], start=True, stop=True)
                        last.then_inc(r_full[b], 1)

            @block.scalar
            def _(act):
                def left(c, b, i, out, src, func=ACT.Copy):
                    act.wait_ge(l_full[b], c * NLF + i + 1)
                    nc.scalar.activation(out, src, func).then_inc(l_used[b], 1)

                def right(c, b, i, out, src):
                    act.wait_ge(r_full[b], c * NRF + i + 1)
                    nc.scalar.activation(out, src, ACT.Copy).then_inc(r_used[b], 1)

                for b in range(B):
                    act.sem_inc(l_used[b], 1)
                    act.sem_inc(r_used[b], 1)
                with act.Fori(0, TB) as c:
                    for b in range(B):
                        left(c, b, L_KT, matT[b][:, 0], pair(b, 0, DK))
                        right(c, b, R_KBT, matT[b][:, 1], pair(b, 1, DK))
                        left(c, b, L_QT, matT[b][:, 2], pair(b, 0, DK))
                        right(c, b, R_QGT, matT[b][:, 3], pair(b, 1, DK))
                    for b in range(B):
                        left(c, b, L_D, ex[b][:], pair(b, 0), ACT.Exp)
                    for b in range(B):
                        right(c, b, R_X0, xx[b][:], pair(b, 1))
                    for i in range(NL):
                        for b in range(B):
                            left(c, b, L_P + 2 * i, pp[b][:], pair(b, 0))
                    for b in range(B):
                        right(c, b, R_W1, w1[b][:].rearrange("p a h d -> p a (h d)"), pair(b, 1, P, 3 * (DV + DK)))
                        left(c, b, L_W1T, w1t[b][:], pair(b, 0, DK))
                    for b in range(B):
                        left(c, b, L_O, o_all[:, bass.ds(c + b * TB, 1)].rearrange("p o n -> p (o n)"),
                             k.ps[:, bank(b, 0), 0:DH * DV])

            @block.vector
            def _(dve):
                v = nc.vector
                with dve.Fori(0, TB) as c:
                    for b in range(B):
                        dve.wait_ge(l_used[b], c * NLF + 1)
                        gt = g[:, bass.ds(c + b * TB, 1)].rearrange("p o h -> p (o h)").unsqueeze(2)
                        v.tensor_tensor(gs[b], k.cf[:, slice(*CF["after"])].unsqueeze(1).broadcast_to([P, DH, P]),
                                        gt.broadcast_to([P, DH, P]), ALU.mult).then_inc(decay_done[b], 1)
                    for b in range(B):
                        dve.wait_ge(r_full[b], c * NRF + R_KK + 1)
                        dve.wait_ge(l_used[b], c * NLF + L_D + 2)
                        v.tensor_tensor(at[b], pair(b, 1), ex[b][:], ALU.mult).then_inc(r_used[b], 1)
                    for b in range(B):
                        dve.wait_ge(l_full[b], c * NLF + L_KQ + 1)
                        v.tensor_tensor(mt[b], pair(b, 0), ex[b][:], ALU.mult).then_inc(l_used[b], 1)
                    for i in range(NL):
                        for b in range(B):
                            if i < NL - 1:
                                dve.wait_ge(r_full[b], c * NRF + R_XP + i + 1)
                                v.tensor_tensor(xx[b][:], xx[b][:], pair(b, 1), ALU.subtract).then_inc(r_used[b], 1)
                            dve.wait_ge(l_full[b], c * NLF + L_P + 2 * i + 2)
                            v.tensor_tensor(yy[b][:], yy[b][:], pair(b, 0), ALU.subtract).then_inc(l_used[b], 1)
                    for b in range(B):
                        dve.wait_ge(r_full[b], c * NRF + R_DELTA + 1)
                        v.tensor_tensor(de[b][:].rearrange("p (a h) d -> p a h d", a=2), w1[b][:, :, :, 0:DV],
                                        k.ps[:, bank(b, 1), 0:DH * DV].rearrange("p (a h d) -> p a h d", a=2, d=DV),
                                        ALU.subtract).then_inc(r_used[b], 1)
                    for b in range(B):
                        dve.wait_ge(r_full[b], c * NRF + R_S + 1)
                        tt = tot[:, bass.ds(c + b * TB, 1)].rearrange("p o h -> p (o h)").unsqueeze(2)
                        v.tensor_tensor(state[b][:], state[b][:], tt.broadcast_to([DK, DH, DV]),
                                        ALU.mult).then_inc(s_step[b], 1)
                        dve.wait_ge(s_step[b], c + 1)
                        v.tensor_tensor(state[b][:], state[b][:],
                                        k.ps[0:DK, bank(b, 1), 0:DH * DV].rearrange("p (h d) -> p h d", d=DV),
                                        ALU.add).then_inc(r_used[b], 1)


def delta_out_stage(nc, k, gate, o_all):
    NJ = DH * DV // P
    with stage(nc, "w_in", "n_in", "sum_done", "root_done", "og_done", "t_full", "t_used", "y_full", "dve_step") as (
            w_in, n_in, sum_done, root_done, og_done, t_full, t_used, y_full, dve_step), ExitStack() as ctx:
        wo = ctx.enter_context(sbuf(nc, "wo1", [P, NJ, D], F32))
        nw = ctx.enter_context(sbuf(nc, "nw", [P, DV], F32))
        sq = ctx.enter_context(sbuf(nc, "osq", [P, NT, DH * DV], F32))
        ms = ctx.enter_context(sbuf(nc, "ms", [P, NT, DH], F32))
        ogT = ctx.enter_context(sbuf(nc, "ogT", [P, 2, NJ, P], F32))
        y = ctx.enter_context(sbuf(nc, "y1", [P, 2, D], F32))
        with nc.Block() as block:
            @block.sync
            def _(sp):
                sp.dma_start(wo[:], k.ins["w_o1"]).then_inc(w_in, 16)
                sp.dma_start(nw[:], k.ins["norm_w"].partition_broadcast(P)).then_inc(n_in, 16)

            @block.scalar
            def _(act):
                act.wait_ge(sum_done, 1)
                nc.scalar.activation(ms[:], ms[:], ACT.Sqrt).then_inc(root_done, 1)
                for t in range(NT):
                    act.wait_ge(t_full, t + 1)
                    if t >= 2:
                        act.wait_ge(y_full, t - 1)
                    nc.scalar.copy(ogT[:, t % 2].rearrange("p j t -> p (j t)"), k.ps[:, t % 2, 0:NJ * P]).then_inc(t_used, 1)

            OG, STEPS = 5 + NT, 2

            @block.tensor
            def _(pe):
                pe.wait_ge(w_in, 16)

                def transpose(t):
                    pe.wait_ge(og_done, t + 1)
                    if t >= 2:
                        pe.wait_ge(t_used, t - 1)
                    for j in range(NJ):
                        last = nc.tensor.transpose(k.ps[:, t % 2, j * P:(j + 1) * P], o_all[:, t, j * P:(j + 1) * P], k.identf)
                    last.then_inc(t_full, 1)

                def project(t):
                    pe.wait_ge(t_used, t + 1)
                    if t >= 4:
                        pe.wait_ge(dve_step, OG + STEPS * (t - 3))
                    for j in range(NJ):
                        last = nc.tensor.matmul(k.ps[:, 4 + t % 4, 0:D], ogT[:, t % 2, j], wo[:, j],
                                                start=j == 0, stop=j == NJ - 1)
                    last.then_inc(y_full, 1)

                transpose(0)
                for t in range(NT):
                    if t + 1 < NT:
                        transpose(t + 1)
                    project(t)

            @block.vector
            def _(dve):
                v = nc.vector
                step = Steps(dve, dve_step)
                step(v.tensor_tensor(o_all[:], o_all[:], gate[:], ALU.mult))
                step(v.tensor_tensor(sq[:], o_all[:], o_all[:], ALU.mult))
                step(v.tensor_reduce(ms[:], sq[:].rearrange("p t (h d) -> p t h d", d=DV), axis=X, op=ALU.add))
                v.tensor_scalar(ms[:], ms[:], 1.0 / DV, 1e-5, ALU.mult, ALU.add).then_inc(sum_done, 1)
                dve.wait_ge(root_done, 1)
                step(v.reciprocal(ms[:], ms[:]))
                dve.wait_ge(n_in, 16)
                hd = "p (h d) -> p h d"
                for t in range(NT):
                    o = o_all[:, t].rearrange(hd, d=DV)
                    step(v.tensor_tensor(o, o, ms[:, t].unsqueeze(2).broadcast_to([P, DH, DV]), ALU.mult))
                    v.tensor_tensor(o, o, nw[:].unsqueeze(1).broadcast_to([P, DH, DV]), ALU.mult).then_inc(og_done, 1)
                step(v.memset(y[:], 0.0))
                for t in range(NT):
                    dve.wait_ge(y_full, t + 1)
                    step(v.tensor_tensor(y[:, t % 2], k.ps[:, 4 + t % 4, 0:D], k.mod[:, 1, t // TB, 2 * D:3 * D], ALU.mult))
                    step(v.tensor_tensor(k.x[:, t], k.x[:, t], y[:, t % 2], ALU.add))


class Kernel:
    pass


def build(nc, ins, out):
    NAMES.clear()
    k = Kernel()
    k.ins = ins
    ctx = ExitStack()
    with ctx:
        def sb(name, shape, dt=F32):
            return ctx.enter_context(sbuf(nc, name, shape, dt))

        k.ps = ctx.enter_context(nc.psum_tensor("ps", [P, 8, 512], F32))
        k.x = sb("x", [P, NT, D])
        k.h = sb("h", [P, NT, D])
        k.hT = sb("hT", [P, KT, TOK])
        k.mod = sb("mod", [P, 2, B, NMOD])
        k.cf = sb("cf", [P, CF_W])
        k.cb = sb("cb", [P, CB_W], BF16)
        k.identf = k.cf[:, slice(*CF["ident"])]
        k.identb = k.cb[:, slice(*CB["ident"])]
        k.future = k.cb[:, slice(*CB["future"])]
        k.sh = sb("sh", [P, NT, D])
        k.slot = sb("slot", [P, NT, TOPK], I32)
        k.wk = sb("wk", [P, NT, TOPK])
        k.table = sb("table", [P, E * CAP[0] // P], I32)
        h_dram = nc.dram_tensor("h_rows", [TOK, D], F32).ap()
        y_dram = [nc.dram_tensor(f"y_rows{n}", [E * CAP[n] + 1, D], F32).ap() for n in (0, 1)]
        k.wo_in = ctx.enter_context(nc.semaphore("wo_in"))

        load_stage(nc, k)
        norm_stage(nc, k, 0, 0)
        with ExitStack() as scope:
            attn = scope.enter_context(sbuf(nc, "attn", [P, HEADS * B, T], F32))
            wo = scope.enter_context(sbuf(nc, "wo", [P, HEADS, D], F32))
            with nc.Block() as block:
                @block.sync
                def _(sp):
                    sp.dma_start(wo[:], ins["w_o"]).then_inc(k.wo_in, 16)
            attention_stage(nc, k, attn)
            attn_out_stage(nc, k, attn, wo)
        norm_stage(nc, k, 0, 3, h_dram)
        route_stage(nc, k, 0)
        shared_stage(nc, k, 0)
        expert_stage(nc, k, 0, h_dram, y_dram[0])
        combine_stage(nc, k, 0, y_dram[0])
        norm_stage(nc, k, 1, 0)
        with ExitStack() as scope:
            def buf(name, shape):
                return scope.enter_context(sbuf(nc, name, shape))

            gate = buf("gate_act", [P, NT, DH * DV])
            g = buf("g", [P, NT, DH])
            tot = buf("tot", [DK, NT, DH])
            o_all = buf("o_all", [P, NT, DH * DV])
            scl = buf("scl", [P, NT, 7, DH])
            with sbuf(nc, "qkv", [P, NT, QKV]) as qkv:
                delta_project_stage(nc, k, qkv, gate, g, scl, tot)
                delta_stage(nc, k, qkv, g, scl, tot, o_all)
            delta_out_stage(nc, k, gate, o_all)
        norm_stage(nc, k, 1, 3, h_dram)
        route_stage(nc, k, 1)
        shared_stage(nc, k, 1)
        expert_stage(nc, k, 1, h_dram, y_dram[1])
        combine_stage(nc, k, 1, y_dram[1], out)
        return k


def layouts(a):
    g = {name: np.asarray(v) for name, v in a.items()}

    def rows(m, p=P):
        return np.ascontiguousarray(m.reshape(m.shape[0] // p, p, *m.shape[1:]).swapaxes(0, 1))

    o = {}
    o["cf"], o["cb"] = constants()
    o["x"] = rows(g["L0_attn_query"].reshape(TOK, D))
    for n in (0, 1):
        o[f"c{n}"] = rows(g[f"L{n}_c"].T)
        o[f"wmod{n}"] = rows(g[f"L{n}_wmod"])
    qkv = np.stack([g[f"L0_attn_w_{c}"].reshape(KT, P, HEADS, HD) for c in "qkv"])
    o["w_qkv"] = np.ascontiguousarray(qkv.transpose(3, 2, 0, 1, 4))
    o["b_qkv"] = np.ascontiguousarray(np.stack([g[f"L0_attn_b_{c}"].reshape(HEADS, HD) for c in "qkv"]).transpose(2, 0, 1))
    o["w_o"] = rows(g["L0_attn_w_o"])
    o["b_o"] = g["L0_attn_b_o"]
    o["router0"] = rows(g["L0_ffn_wg_router"].T)
    o["router1"] = rows(g["L1_ffn_gate_w"].T)
    gu0 = np.stack([g["L0_ffn_w_gate"], g["L0_ffn_w_up"]], 2)
    gu1 = g["L1_ffn_w_gate_up"].reshape(E, D, 2, F)
    for n, gu in ((0, gu0), (1, gu1)):
        o[f"w_gu{n}"] = np.ascontiguousarray(gu.reshape(E, KT, P, 2, F).transpose(0, 2, 1, 3, 4))
        wd = g[f"L{n}_ffn_w_down"]
        o[f"w_down{n}"] = np.ascontiguousarray(wd.reshape(E, 2, FH, D).transpose(0, 2, 1, 3))
        o[f"ws_down{n}"] = g[f"L{n}_ffn_ws_down"]
    o["ws_gu0"] = rows(np.stack([g["L0_ffn_ws_gate"], g["L0_ffn_ws_up"]], 1))
    o["ws_gu1"] = rows(g["L1_ffn_ws_gate_up"].reshape(D, 2, FS))
    o["w_qkv1"] = rows(np.concatenate([g["L1_attn_Wq"], g["L1_attn_Wk"], g["L1_attn_Wv"]]).T)
    o["w_gab"] = rows(np.concatenate([g["L1_attn_Wg"], g["L1_attn_Wa"], g["L1_attn_Wb"]]).T)
    conv = np.concatenate([g["L1_attn_conv_q_w"], g["L1_attn_conv_k_w"], g["L1_attn_conv_v_w"]])[:, 0]
    o["conv"] = rows(conv, CH)
    o["A_log"], o["dt_bias"], o["norm_w"] = g["L1_attn_A_log"], g["L1_attn_dt_bias"], g["L1_attn_norm_w"]
    o["w_o1"] = rows(g["L1_attn_Wo"].T)
    return {n: np.ascontiguousarray(v) for n, v in o.items()}


def kernel(**inputs):
    import concourse.bacc as bacc
    from concourse.bass_utils import run_bass_kernel_spmd

    nc = bacc.Bacc("TRN2", target_bir_lowering=False, num_devices=1)
    arrays = {f"in_{n}": v for n, v in layouts(inputs).items()}
    ins = {n[3:]: nc.dram_tensor(n, v.shape, mybir.dt.from_np(v.dtype), kind="ExternalInput").ap()
           for n, v in arrays.items()}
    out = nc.dram_tensor("out", [P, NT, D], F32, kind="ExternalOutput").ap()
    build(nc, ins, out)
    r = run_bass_kernel_spmd(nc, [arrays], core_ids=[0])
    y = r.results[0]["out"]
    return np.ascontiguousarray(y.swapaxes(0, 1)).reshape(B, T, D)
```

```python
from contextlib import ExitStack, contextmanager

import numpy as np

import concourse.bass as bass
import concourse.mybir as mybir

F32 = mybir.dt.float32
BF16 = mybir.dt.bfloat16
F16 = mybir.dt.float16
I32 = mybir.dt.int32
ALU = mybir.AluOpType
ACT = mybir.ActivationFunctionType
X = mybir.AxisListType.X

P = 128
B, T, D = 2, 512, 256
TOK = B * T
NT = TOK // P
TB = T // P
KT = D // P
NMOD = 6 * D

HEADS, HD = 16, 128
SCALE = float(HD) ** -0.5

E, TOPK, F = 32, 6, 176
FH = F // 2
FS = 2 * F
HOTS = 4
EARLY = 3
FS_CHUNKS = [(0, 128), (128, 128), (256, 96)]
CAP = [2 * (TOK * TOPK // E), 48]
GROUPS, GTOP = 8, 3
ROUTE_SCALE = 16.0
SLOTS = 384
SB = SLOTS // P

DH, DK, DV = 6, 32, 64
QKV = DH * (2 * DK + DV)
CH = 96
NCH = QKV // CH
TAPS = 4
LEVELS = [2, 4, 8, 16, 32, 64]
NEG = -1.0e30

CF = {}
_at = 0
for _n, _w in (("ident", P), ("after", P), ("upto", P), ("ones", DK), ("base0", E), ("base1", E),
               ("token", NT), ("lev", (len(LEVELS) + 1) * P)):
    CF[_n] = (_at, _at + _w)
    _at += _w
CF_W = _at
CB = {}
_at = 0
for _n, _w in (("ident", P), ("future", P), ("past", P), ("before", P), ("ones", P), ("iota", P)):
    CB[_n] = (_at, _at + _w)
    _at += _w
CB_W = _at


def constants():
    i = np.arange(P)
    cf = np.zeros((P, CF_W), np.float32)
    cf[:, slice(*CF["ident"])] = np.eye(P)
    cf[:, slice(*CF["after"])] = i[:, None] > i[None, :]
    cf[:, slice(*CF["upto"])] = i[:, None] <= i[None, :]
    cf[:, slice(*CF["ones"])] = 1.0
    for n in (0, 1):
        cf[:, slice(*CF[f"base{n}"])] = (np.arange(E) * CAP[n] - E * CAP[n])[None, :]
    cf[:, slice(*CF["token"])] = i[:, None] + P * np.arange(NT)[None, :]
    at = CF["lev"][0]
    for s in [1] + LEVELS:
        j, k = i[:, None], i[None, :]
        cf[:, at:at + P] = (j // (2 * s) == k // (2 * s)) & (j // s % 2 == 0) & (k // s % 2 == 1)
        at += P
    cb = np.zeros((P, CB_W), np.float32)
    cb[:, slice(*CB["ident"])] = np.eye(P)
    cb[:, slice(*CB["future"])] = np.where(i[None, :] > i[:, None], NEG, 0.0)
    cb[:, slice(*CB["past"])] = np.where(i[None, :] < i[:, None], NEG, 0.0)
    cb[:, slice(*CB["before"])] = i[:, None] < i[None, :]
    cb[:, slice(*CB["ones"])] = 1.0
    cb[:, slice(*CB["iota"])] = i[None, :]
    return cf, cb.astype(mybir.dt.np(BF16))


SEMS = []


@contextmanager
def stage(nc, *names, gathers=0):
    NAMES["stage"] = NAMES.get("stage", 0) + 1
    guards = [nc.semaphore(f"{n}_s{NAMES['stage']}") for n in names]
    sems = [g.__enter__() for g in guards]
    SEMS.append((gathers, guards, sems))
    yield sems


def renew(nc):
    with nc.Block() as block:
        @block.sync
        def _(sp):
            for n, _, sems in SEMS:
                for s in sems[n:]:
                    sp.sem_clear(s)
    for n, guards, _ in reversed(SEMS):
        for g in reversed(guards[n:]):
            g.__exit__(None, None, None)
    SEMS.clear()


class Steps:

    def __init__(self, engine, sem, base=0):
        self.engine, self.sem, self.base, self.n = engine, sem, base, 0

    def __call__(self, ins):
        ins.then_inc(self.sem, 1)
        self.n += 1
        self.engine.wait_ge(self.sem, self.base + self.n)


NAMES = {}


def sbuf(nc, name, shape, dt=F32):
    NAMES[name] = NAMES.get(name, -1) + 1
    return nc.sbuf_tensor(f"{name}_{NAMES[name]}" if NAMES[name] else name, shape, dt)


class Modulation:
    NAMES = ["c_in", "silu_done", "rep_done", "rows_full", "rows_used"]
    FILLS = [(b, c) for b in range(B) for c in range(NMOD // 512)]

    def __init__(self, nc, k, ctx, sems, layer):
        self.nc, self.k, self.layer = nc, k, layer
        self.c_in, self.silu_done, self.rep_done, self.rows_full, self.rows_used = sems
        self.ct = ctx.enter_context(sbuf(nc, "ct", [P, KT, B], F32))
        self.rep = ctx.enter_context(sbuf(nc, "rep", [P, KT * B, P], F32))
        self.wm = ctx.enter_context(sbuf(nc, "wm", [P, KT, NMOD], F32))
        self.sign = ctx.enter_context(sbuf(nc, "sign", [P, B, 2, D], F32))

    def scalar_loads(self, act):
        act.dma_start(self.ct[:], self.k.ins[f"c{self.layer}"]).then_inc(self.c_in, 16)
        act.dma_start(self.wm[:], self.k.ins[f"wmod{self.layer}"]).then_inc(self.c_in, 16)

    def scalar_silu(self, act):
        act.wait_ge(self.c_in, 32)
        self.nc.scalar.activation(self.ct[:], self.ct[:], ACT.Silu).then_inc(self.silu_done, 1)

    def vector_repeat(self, dve):
        dve.wait_ge(self.silu_done, 1)
        self.nc.vector.tensor_copy(self.rep[:], self.ct[:].rearrange("p k b -> p (k b)").unsqueeze(2)
                                   .broadcast_to([P, KT * B, P])).then_inc(self.rep_done, 1)

    def tensor_rows(self, pe):
        pe.wait_ge(self.c_in, 32)
        pe.wait_ge(self.rep_done, 1)
        for n, (b, c) in enumerate(self.FILLS):
            for kt in range(KT):
                last = self.nc.tensor.matmul(self.k.ps[:, n, :], self.rep[:, kt * B + b, :],
                                             self.wm[:, kt, 512 * c:512 * c + 512], start=kt == 0, stop=kt == KT - 1)
            last.then_inc(self.rows_full, 1)

    def scalar_rows(self, act):
        for n, (b, c) in enumerate(self.FILLS):
            act.wait_ge(self.rows_full, n + 1)
            self.nc.scalar.copy(self.k.mod[:, self.layer, b, 512 * c:512 * c + 512],
                                self.k.ps[:, n, :]).then_inc(self.rows_used, 1)

    def vector_scales(self, dve, step):
        dve.wait_ge(self.rows_used, len(self.FILLS))
        m = self.k.mod[:, self.layer].rearrange("p b (s d) -> p b s d", d=D)[:, :, 1:5:3]
        step(self.nc.vector.tensor_scalar_add(m, m, 1.0))

    def vector_gates(self, step):
        v, sg = self.nc.vector, self.sign[:]
        m = self.k.mod[:, self.layer].rearrange("p b (s d) -> p b s d", d=D)[:, :, 2:6:3]
        step(v.tensor_scalar(sg, m, 0.0, 2.0, ALU.is_ge, ALU.mult))
        step(v.tensor_scalar_add(sg, sg, -1.0))
        step(v.tensor_tensor(m, m, sg, ALU.mult))
        step(v.scalar_tensor_tensor(m, m, 0.25, sg, ALU.max, ALU.mult))


class Norm:
    NAMES = ["moments", "root", "shaped", "scaled", "hT_full", "hT_used"]

    def __init__(self, nc, k, ctx, sems, layer, shift, banks):
        self.nc, self.k, self.layer, self.shift, self.banks = nc, k, layer, shift, banks
        self.moments, self.root, self.shaped, self.scaled, self.hT_full, self.hT_used = sems
        self.st = ctx.enter_context(sbuf(nc, "st", [P, NT, 6], F32))
        self.mv = ctx.enter_context(sbuf(nc, "mv", [P, NT, 2], F32))
        self.rt = ctx.enter_context(sbuf(nc, "rt", [P, NT], F32))

    def vector_moments(self, step, half):
        v, tiles = self.nc.vector, range(half * TB, (half + 1) * TB)
        for t in tiles:
            last = v.bn_stats(self.st[:, t], self.k.x[:, t])
        step(last)
        for t in tiles:
            last = v.bn_aggr(self.mv[:, t], self.st[:, t])
        step(last)
        s = slice(half * TB, (half + 1) * TB)
        v.tensor_scalar_add(self.rt[:, s], self.mv[:, s, 1], 1e-5).then_inc(self.moments, 1)

    def scalar_root(self, act, half):
        s = slice(half * TB, (half + 1) * TB)
        act.wait_ge(self.moments, half + 1)
        self.nc.scalar.activation(self.rt[:, s], self.rt[:, s], ACT.Sqrt).then_inc(self.root, 1)

    def vector_scale(self, dve, step, half):
        v, k = self.nc.vector, self.k
        s = slice(half * TB, (half + 1) * TB)
        dve.wait_ge(self.root, half + 1)
        step(v.reciprocal(self.rt[:, s], self.rt[:, s]))
        tiles = range(half * TB, (half + 1) * TB)
        for t in tiles:
            last = v.tensor_scalar(k.h[:, t], k.x[:, t], self.mv[:, t, 0:1], self.rt[:, t:t + 1],
                                   ALU.subtract, ALU.mult)
            if t % 2:
                step(last)
                for u in (t - 1, t):
                    v.tensor_tensor(k.h[:, u], k.h[:, u], k.mod[:, self.layer, half, (self.shift + 1) * D:
                                                                (self.shift + 2) * D], ALU.mult).then_inc(self.shaped, 1)

    def gpsimd_shift(self, pool, half):
        k = self.k
        for t in range(half * TB, (half + 1) * TB):
            pool.wait_ge(self.shaped, t + 1)
            self.nc.gpsimd.tensor_tensor(k.h[:, t], k.h[:, t], k.mod[:, self.layer, half, self.shift * D:
                                                                     (self.shift + 1) * D], ALU.add
                                         ).then_inc(self.scaled, 1)

    def tensor_transpose(self, pe, half):
        if half:
            pe.wait_ge(self.hT_used, KT)
        for kt in range(KT):
            for q in range(TB):
                t = half * TB + q
                if kt == 0:
                    pe.wait_ge(self.scaled, t + 1)
                last = self.nc.tensor.transpose(self.k.ps[:, self.banks[kt], q * P:(q + 1) * P],
                                                self.k.h[:, t, kt * P:(kt + 1) * P], self.k.identf)
            last.then_inc(self.hT_full, 1)

    def scalar_evacuate(self, act, half):
        for kt in range(KT):
            act.wait_ge(self.hT_full, half * KT + kt + 1)
            self.nc.scalar.copy(self.k.hT[:, kt, half * T:(half + 1) * T],
                                self.k.ps[:, self.banks[kt], :]).then_inc(self.hT_used, 1)


def first_stage(nc, k):
    with stage(nc, "x_in", "const_in", "dve_step") as (x_in, const_in, dve_step), \
            stage(nc, *Modulation.NAMES) as mod_sems, stage(nc, *Norm.NAMES) as norm_sems, ExitStack() as ctx:
        mod = Modulation(nc, k, ctx, mod_sems, 0)
        norm = Norm(nc, k, ctx, norm_sems, 0, 0, (6, 7))
        with nc.Block() as block:
            @block.sync
            def _(sp):
                sp.dma_start(k.x[:], k.ins["x"]).then_inc(x_in, 16)
                sp.dma_start(k.cf[:], k.ins["cf"]).then_inc(const_in, 16)
                sp.dma_start(k.cb[:], k.ins["cb"]).then_inc(const_in, 16)

            @block.scalar
            def _(act):
                mod.scalar_loads(act)
                mod.scalar_silu(act)
                for half in range(2):
                    norm.scalar_root(act, half)
                mod.scalar_rows(act)
                for half in range(2):
                    norm.scalar_evacuate(act, half)

            @block.tensor
            def _(pe):
                mod.tensor_rows(pe)
                pe.wait_ge(const_in, 32)
                for half in range(2):
                    norm.tensor_transpose(pe, half)

            @block.vector
            def _(dve):
                step = Steps(dve, dve_step)
                dve.wait_ge(x_in, 16)
                norm.vector_moments(step, 0)
                mod.vector_repeat(dve)
                norm.vector_moments(step, 1)
                mod.vector_scales(dve, step)
                for half in range(2):
                    norm.vector_scale(dve, step, half)
                mod.vector_gates(step)

            @block.gpsimd
            def _(pool):
                for half in range(2):
                    norm.gpsimd_shift(pool, half)


def attention_stage(nc, k, attn):
    names = ["w0_in", "w1_in", "bias_in", "pj0_full", "pj1_full", "pj0_used", "pj1_used", "s_full", "max_done",
             "p_done", "sums_inv", "p_scaled", "t0_full", "t1_full", "t0_used", "t1_used", "o_full", "o_used"]
    with stage(nc, *names) as sems, ExitStack() as ctx:
        (w0_in, w1_in, bias_in, pj0_full, pj1_full, pj0_used, pj1_used, s_full, max_done, p_done, sums_inv,
         p_scaled, t0_full, t1_full, t0_used, t1_used, o_full, o_used) = sems
        w_in = [w0_in, w1_in]
        pj_full, pj_used = [pj0_full, pj1_full], [pj0_used, pj1_used]

        def sb(name, shape, dt=F32):
            return ctx.enter_context(sbuf(nc, name, shape, dt))

        w = sb("w", [P, 2, 3, KT, HD])
        bias = sb("bias", [P, 3, HEADS])
        qT = sb("qT", [P, 2, TOK])
        kT = sb("kT", [P, 2, TOK])
        v = sb("v", [P, 2, NT, HD])
        at = {3: (0, 512), 2: (512, 896), 0: (896, 1024), 1: (1024, 1280)}
        pr = sb("pr", [P, 2, 1280])
        nmax = sb("nmax", [P, 2, TB])
        sums = sb("sums", [P, 2, TB])
        inv = sb("inv", [P, 2, TB])
        pt = sb("pt", [P, 2, 1280])
        pt_at = [0, 512, 1024, 896]
        PJ, S0, T0, O = 0, 2, 5, 7
        s_banks = [[(3, 0)], [(2, 0), (0, 384)], [(1, 0)]]

        with nc.Block() as block:
            @block.sync
            def _(sp):
                sp.dma_start(bias[:], k.ins["b_qkv"]).then_inc(bias_in, 16)
                for h in range(2):
                    sp.dma_start(w[:, h], k.ins["w_qkv"][h]).then_inc(w_in[h], 16)

                def load(h, slot):
                    sp.wait_ge(pj_full[1], 3 * (h - 1))
                    sp.dma_start(w[:, slot], k.ins["w_qkv"][bass.ds(h, 1)].rearrange("o p a b c -> (o p) a b c")
                                 ).then_inc(w_in[slot], 16)

                with sp.Fori(1, HEADS // 2) as pair:
                    load(2 * pair, 0)
                    load(2 * pair + 1, 1)

            @block.tensor
            def _(pe):
                pe.wait_ge(bias_in, 16)
                fill = [0, 0]

                def project(h, slot, parts, banks=(0, 1)):
                    if "q" in parts:
                        pe.wait_ge(w_in[slot], 8 * (h - slot) + 16)
                    for i, what in enumerate("qkv"):
                        if what not in parts:
                            continue
                        for bank in banks:
                            if not (isinstance(h, int) and h == 0 and i == 0):
                                pe.wait_ge(pj_used[bank], 3 * h + i)
                            if what == "v":
                                for q in range(TB):
                                    t = bank * TB + q
                                    for kt in range(KT):
                                        last = nc.tensor.matmul(k.ps[:, PJ + bank, q * HD:(q + 1) * HD],
                                                                k.hT[:, kt, t * P:(t + 1) * P], w[:, slot, i, kt],
                                                                start=kt == 0, stop=kt == KT - 1)
                            else:
                                for kt in range(KT):
                                    last = nc.tensor.matmul(k.ps[:, PJ + bank, :], w[:, slot, i, kt],
                                                            k.hT[:, kt, bank * T:(bank + 1) * T],
                                                            start=kt == 0, stop=kt == KT - 1)
                            last.then_inc(pj_full[bank], 1)

                def scores(h, slot, b):
                    u = 2 * h + b
                    pe.wait_ge(pj_used[b], 3 * h + 2)
                    for n, tiles in enumerate(s_banks):
                        if not (isinstance(u, int) and u == 0):
                            pe.wait_ge(p_done, 3 * u + n - 2)
                        for q, col in tiles:
                            nk = (q + 1) * P
                            nc.tensor.matmul(k.ps[:, S0 + n, col:col + nk],
                                             qT[:, slot, b * T + q * P:b * T + (q + 1) * P],
                                             kT[:, slot, b * T:b * T + nk], start=True, stop=False)
                            last = nc.tensor.matmul(k.ps[:, S0 + n, col + nk - P:col + nk], k.identb, k.future,
                                                    start=False, stop=True)
                        last.then_inc(s_full, 1)

                def weights(h, slot, b, ns):
                    u = 2 * h + b
                    for n in ns:
                        js, bank = ([0], [1, 3], [2])[n], n % 2
                        if n == 0:
                            pe.wait_ge(p_scaled, u + 1)
                        if n == 1:
                            pe.wait_ge(t1_used, u + 1)
                        else:
                            pe.wait_ge(t0_used, 2 * u + n // 2 + 1)
                        for j in js:
                            for q in range(j, TB):
                                c = pt_at[j] - pt_at[js[0]] + (q - j) * P
                                last = nc.tensor.transpose(k.ps[:, T0 + bank, c:c + P],
                                                           pr[:, b, at[q][0] + j * P:at[q][0] + (j + 1) * P],
                                                           k.identf)
                        last.then_inc(t1_full if bank else t0_full, 1)

                def values(h, slot, b):
                    u = 2 * h + b
                    pe.wait_ge(pj_used[b], 3 * h + 3)
                    pe.wait_ge(t0_used, 2 * u + 3)
                    pe.wait_ge(t1_used, u + 2)
                    pe.wait_ge(o_used, u + 1)
                    for j in range(TB):
                        nq = (TB - j) * P
                        last = nc.tensor.matmul(k.ps[:, O, j * P:], v[:, slot, b * TB + j],
                                                pt[:, b, pt_at[j]:pt_at[j] + nq], start=j == 0, stop=j == TB - 1)
                    last.then_inc(o_full, 1)

                def head(h, slot, last=False):
                    nxt = not last
                    if nxt:
                        project(h + 1, 1 - slot, "q", (0, 1))
                    scores(h, slot, 1)
                    weights(h, slot, 0, (0, 1))
                    if nxt:
                        project(h + 1, 1 - slot, "k", (0,))
                    weights(h, slot, 0, (2,))
                    if nxt:
                        project(h + 1, 1 - slot, "k", (1,))
                    values(h, slot, 0)
                    if nxt:
                        project(h + 1, 1 - slot, "v", (0,))
                        scores(h + 1, 1 - slot, 0)
                    weights(h, slot, 1, (0, 1))
                    if nxt:
                        project(h + 1, 1 - slot, "v", (1,))
                    weights(h, slot, 1, (2,))
                    values(h, slot, 1)

                project(0, 0, "qkv")
                scores(0, 0, 0)
                with pe.Fori(0, HEADS // 2 - 1) as pair:
                    head(2 * pair, 0)
                    head(2 * pair + 1, 1)
                head(HEADS - 2, 0)
                head(HEADS - 1, 1, last=True)

            @block.vector
            def _(dve):
                def evac_q(h, slot):
                    for b in range(B):
                        dve.wait_ge(pj_full[b], 3 * h + 1)
                        nc.vector.tensor_scalar(qT[:, slot, b * T:(b + 1) * T], k.ps[:, PJ + b, :],
                                                bias[:, 0, bass.ds(h, 1)], SCALE, ALU.add, ALU.mult
                                                ).then_inc(pj_used[b], 1)

                def maxima(h, b):
                    u = 2 * h + b
                    for n, tiles in enumerate(s_banks):
                        dve.wait_ge(s_full, 3 * u + n + 1)
                        for q, col in tiles:
                            last = nc.vector.tensor_reduce(nmax[:, b, q:q + 1], k.ps[:, S0 + n, col:col + (q + 1) * P],
                                                           axis=X, op=ALU.max, negate=True)
                        last.then_inc(max_done, 1)

                def invert(h, b):
                    dve.wait_ge(p_done, 3 * (2 * h + b) + 3)
                    nc.vector.reciprocal(inv[:, b], sums[:, b]).then_inc(sums_inv, 1)

                def evac_t(h, b):
                    u = 2 * h + b
                    dve.wait_ge(t0_full, 2 * u + 1)
                    nc.vector.tensor_copy(pt[:, b, 0:512], k.ps[:, T0, :]).then_inc(t0_used, 1)
                    dve.wait_ge(t0_full, 2 * u + 2)
                    nc.vector.tensor_copy(pt[:, b, 1024:1280], k.ps[:, T0, 0:256]).then_inc(t0_used, 1)

                def head(h, slot, last=False):
                    if not last:
                        evac_q(h + 1, 1 - slot)
                    maxima(h, 1)
                    invert(h, 1)
                    evac_t(h, 0)
                    if not last:
                        maxima(h + 1, 0)
                        invert(h + 1, 0)
                    evac_t(h, 1)

                dve.wait_ge(bias_in, 16)
                dve.sem_inc(t0_used, 1)
                evac_q(0, 0)
                maxima(0, 0)
                invert(0, 0)
                with dve.Fori(0, HEADS // 2 - 1) as pair:
                    head(2 * pair, 0)
                    head(2 * pair + 1, 1)
                head(HEADS - 2, 0)
                head(HEADS - 1, 1, last=True)

            @block.gpsimd
            def _(pool):
                def scale(h, b):
                    pool.wait_ge(sums_inv, 2 * h + b + 1)
                    for q in range(TB):
                        s = pr[:, b, at[q][0]:at[q][1]]
                        last = nc.gpsimd.tensor_tensor(s, s, inv[:, b, q:q + 1].broadcast_to([P, (q + 1) * P]), ALU.mult)
                    last.then_inc(p_scaled, 1)

                with pool.Fori(0, HEADS) as h:
                    scale(h, 0)
                    scale(h, 1)

            @block.scalar
            def _(act):
                def evac_k(h, slot):
                    for b in range(B):
                        act.wait_ge(pj_full[b], 3 * h + 2)
                    for b in range(B):
                        nc.scalar.activation(kT[:, slot, b * T:(b + 1) * T], k.ps[:, PJ + b, :], ACT.Identity,
                                             bias=bias[:, 1, bass.ds(h, 1)]).then_inc(pj_used[b], 1)

                def evac_v(h, slot, b):
                    act.wait_ge(pj_full[b], 3 * h + 3)
                    nc.scalar.copy(v[:, slot, b * TB:(b + 1) * TB].rearrange("p t d -> p (t d)"),
                                   k.ps[:, PJ + b, :]).then_inc(pj_used[b], 1)

                def exponentials(h, b):
                    u = 2 * h + b
                    if not (isinstance(u, int) and u < 2):
                        act.wait_ge(t0_full, 2 * u - 2)
                    for n, tiles in enumerate(s_banks):
                        act.wait_ge(max_done, 3 * u + n + 1)
                        for q, col in tiles:
                            last = nc.scalar.activation(pr[:, b, at[q][0]:at[q][1]],
                                                        k.ps[:, S0 + n, col:col + (q + 1) * P], ACT.Exp,
                                                        bias=nmax[:, b, q:q + 1], accum_out=sums[:, b, q:q + 1])
                        last.then_inc(p_done, 1)

                def evac_t1(h, b):
                    act.wait_ge(t1_full, 2 * h + b + 1)
                    nc.scalar.copy(pt[:, b, 512:1024], k.ps[:, T0 + 1, :]).then_inc(t1_used, 1)

                def evac_o(h, b):
                    act.wait_ge(o_full, 2 * h + b + 1)
                    nc.scalar.activation(attn[:, bass.ds(2 * h + b, 1)].rearrange("p o t -> p (o t)"), k.ps[:, O, :],
                                         ACT.Identity, bias=bias[:, 2, bass.ds(h, 1)]).then_inc(o_used, 1)

                def head(h, slot, last=False):
                    exponentials(h, 1)
                    evac_t1(h, 0)
                    if not last:
                        evac_k(h + 1, 1 - slot)
                    evac_o(h, 0)
                    if not last:
                        evac_v(h + 1, 1 - slot, 0)
                        exponentials(h + 1, 0)
                    evac_t1(h, 1)
                    if not last:
                        evac_v(h + 1, 1 - slot, 1)
                    evac_o(h, 1)

                act.wait_ge(bias_in, 16)
                act.sem_inc(t1_used, 1)
                act.sem_inc(o_used, 1)
                evac_k(0, 0)
                for b in range(B):
                    evac_v(0, 0, b)
                exponentials(0, 0)
                head(0, 0)
                with act.Fori(0, HEADS // 2 - 1) as pair:
                    head(2 * pair + 1, 1)
                    head(2 * pair + 2, 0)
                head(HEADS - 1, 1, last=True)


class AttentionOut:
    NAMES = ["b_in", "y_full", "y_used"]

    def __init__(self, nc, k, ctx, sems, attn, wo):
        self.nc, self.k, self.attn, self.wo = nc, k, attn, wo
        self.b_in, self.y_full, self.y_used = sems
        self.bo = ctx.enter_context(sbuf(nc, "bo", [P, D], F32))
        self.y = ctx.enter_context(sbuf(nc, "y", [P, 2, D], F32))

    def sync_loads(self, sp):
        sp.dma_start(self.bo[:], self.k.ins["b_o"].partition_broadcast(P)).then_inc(self.b_in, 16)

    def tensor_tile(self, pe, t, bank):
        b, q = divmod(t, TB)
        if t == 0:
            pe.wait_ge(self.k.wo_in, 16)
        if t >= 2:
            pe.wait_ge(self.y_used, t - 1)
        for h in range(HEADS):
            last = self.nc.tensor.matmul(self.k.ps[:, bank, 0:D], self.attn[:, 2 * h + b, q * P:(q + 1) * P],
                                         self.wo[:, h], start=h == 0, stop=h == HEADS - 1)
        last.then_inc(self.y_full, 1)

    def vector_tile(self, dve, step, t, bank):
        v, k, y = self.nc.vector, self.k, self.y[:, t % 2]
        if t == 0:
            dve.wait_ge(self.b_in, 16)
        dve.wait_ge(self.y_full, t + 1)
        step(v.tensor_tensor(y, k.ps[:, bank, 0:D], self.bo[:], ALU.add))
        dve.sem_inc(self.y_used, 1)
        step(v.tensor_tensor(y, y, k.mod[:, 0, t // TB, 2 * D:3 * D], ALU.mult))
        step(v.tensor_tensor(k.x[:, t], k.x[:, t], y, ALU.add))

    def vector_before(self, dve, step, half):
        pass

    def gpsimd_before(self, pool):
        pass

    def scalar_before(self, act, half):
        pass

    def scalar_tile(self, act, t):
        pass


class DeltaOut:
    NAMES = ["w_in", "n_in", "sq_done", "sum_done", "root_done", "w_done", "og_done", "t_full", "t_used", "y_full",
             "y_used"]
    NJ = DH * DV // P

    def __init__(self, nc, k, ctx, sems, gate, o_all):
        self.nc, self.k, self.gate, self.o_all = nc, k, gate, o_all
        (self.w_in, self.n_in, self.sq_done, self.sum_done, self.root_done, self.w_done, self.og_done, self.t_full,
         self.t_used, self.y_full, self.y_used) = sems

        def sb(name, shape):
            return ctx.enter_context(sbuf(nc, name, shape, F32))

        self.wo = sb("wo1", [P, self.NJ, D])
        self.nw = sb("nw", [P, 1])
        self.sq = sb("osq", [P, NT, DH * DV])
        self.ms = sb("ms", [P, NT, DH])
        self.ogT = sb("ogT", [P, 2, self.NJ, P])
        self.y = sb("y1", [P, 2, D])

    def sync_loads(self, sp):
        sp.dma_start(self.wo[:], self.k.ins["w_o1"]).then_inc(self.w_in, 16)
        for i in range(P // DV):
            sp.dma_start(self.nw[i * DV:(i + 1) * DV, :], self.k.ins["norm_w"].unsqueeze(1)).then_inc(self.n_in, 16)

    def gpsimd_before(self, pool):
        g_ = self.nc.gpsimd
        for t in range(NT):
            g_.tensor_tensor(self.o_all[:, t], self.o_all[:, t], self.gate[:, t], ALU.mult).then_inc(self.sq_done, 1)
            pool.wait_ge(self.sq_done, 2 * t + 1)
            g_.tensor_tensor(self.sq[:, t], self.o_all[:, t], self.o_all[:, t], ALU.mult).then_inc(self.sq_done, 1)

    def vector_before(self, dve, step, half):
        v, ms = self.nc.vector, self.ms[:, half * TB:(half + 1) * TB]
        if half == 0:
            dve.wait_ge(self.w_in, 16)
            dve.wait_ge(self.n_in, 32)
            v.tensor_scalar(self.wo[:], self.wo[:], self.nw[:, 0:1], None, ALU.mult).then_inc(self.w_done, 1)
        dve.wait_ge(self.sq_done, 2 * TB * (half + 1))
        step(v.tensor_reduce(ms, self.sq[:, half * TB:(half + 1) * TB].rearrange("p t (h d) -> p t h d", d=DV),
                             axis=X, op=ALU.add))
        v.tensor_scalar(ms, ms, 1.0 / DV, 1e-5, ALU.mult, ALU.add).then_inc(self.sum_done, 1)
        dve.wait_ge(self.root_done, half + 1)
        step(v.reciprocal(ms, ms))
        for t in range(half * TB, (half + 1) * TB):
            o = self.o_all[:, t].rearrange("p (h d) -> p h d", d=DV)
            v.tensor_tensor(o, o, self.ms[:, t].unsqueeze(2).broadcast_to([P, DH, DV]), ALU.mult
                            ).then_inc(self.og_done, 1)

    def scalar_before(self, act, half):
        ms = self.ms[:, half * TB:(half + 1) * TB]
        act.wait_ge(self.sum_done, half + 1)
        self.nc.scalar.activation(ms, ms, ACT.Sqrt).then_inc(self.root_done, 1)

    def scalar_tile(self, act, t):
        act.wait_ge(self.t_full, t + 1)
        if t >= 2:
            act.wait_ge(self.y_full, t - 1)
        self.nc.scalar.copy(self.ogT[:, t % 2].rearrange("p j t -> p (j t)"),
                            self.k.ps[:, 2 + t % 2, 0:self.NJ * P]).then_inc(self.t_used, 1)

    def transpose(self, pe, t):
        pe.wait_ge(self.og_done, t + 1)
        if t >= 2:
            pe.wait_ge(self.t_used, t - 1)
        for j in range(self.NJ):
            last = self.nc.tensor.transpose(self.k.ps[:, 2 + t % 2, j * P:(j + 1) * P],
                                            self.o_all[:, t, j * P:(j + 1) * P], self.k.identf)
        last.then_inc(self.t_full, 1)

    def tensor_tile(self, pe, t, bank):
        if t == 0:
            pe.wait_ge(self.w_done, 1)
            self.transpose(pe, 0)
        if t + 1 < NT:
            self.transpose(pe, t + 1)
        pe.wait_ge(self.t_used, t + 1)
        if t >= 2:
            pe.wait_ge(self.y_used, t - 1)
        for j in range(self.NJ):
            last = self.nc.tensor.matmul(self.k.ps[:, bank, 0:D], self.ogT[:, t % 2, j], self.wo[:, j],
                                         start=j == 0, stop=j == self.NJ - 1)
        last.then_inc(self.y_full, 1)

    def vector_tile(self, dve, step, t, bank):
        v, k, y = self.nc.vector, self.k, self.y[:, t % 2]
        dve.wait_ge(self.y_full, t + 1)
        step(v.tensor_tensor(y, k.ps[:, bank, 0:D], k.mod[:, 1, t // TB, 2 * D:3 * D], ALU.mult))
        dve.sem_inc(self.y_used, 1)
        step(v.tensor_tensor(k.x[:, t], k.x[:, t], y, ALU.add))


def route_stage(nc, k, n, h_dram, Residual, *residual_buffers):
    cap, trash, na = CAP[n], E * CAP[n], E * CAP[n] // P
    HIT, OUT = 10.0, -1.0e4
    TAKEN, NONE = 3.0e38, -3.0e38
    names = ["w_in", "logits_full", "key_done", "exp_done", "sel_done", "place_full", "hot_b_done", "hot_a_done",
             "rhs_done", "hot_used", "dve_step", "ws_in", "gu_full", "gate_done", "act_done",
             "y_full", "y_done", "h_out"]
    with stage(nc, *names) as sems, stage(nc, *Norm.NAMES) as norm_sems, \
            stage(nc, *Residual.NAMES) as residual_sems, ExitStack() as ctx:
        (w_in, logits_full, key_done, exp_done, sel_done, place_full, hot_b_done, hot_a_done, rhs_done,
         hot_used, dve_step, ws_in, gu_full, gate_done, act_done, y_full, y_done, h_out) = sems

        def sb(name, shape, dt=F32):
            return ctx.enter_context(sbuf(nc, name, shape, dt))

        wr = sb("wr", [P, KT, E])
        lg = sb("lg", [P, NT, E])
        gx = sb("gx", [P, NT, GROUPS + 8 - GTOP])
        gm = sb("gm", [P, NT, 8])
        mx = sb("mx", [P, NT])
        key = sb("key", [P, NT, E + 2])
        rep = sb("rep", [P, NT, E + 2])
        m8 = sb("m8", [P, NT, 8])
        ex = sb("ex", [P, NT, E])
        z = sb("z", [P, NT])
        sel = sb("sel", [P, NT, E])
        selb = sb("selb", [P, NT, E], BF16)
        valid = sb("valid", [P, NT, E])
        sv = sb("sv", [P, NT, E])
        s8 = sb("s8", [P, NT, 8])
        eq = sb("eq", [P, NT, TOPK, E])
        ai = sb("ai", [P, NT, TOPK], I32)
        af = sb("af", [P, NT, TOPK])
        bf = sb("bf", [P, NT, TOPK])
        hot_b = sb("hot_b", [P, HOTS, TOPK, P], F16)
        hot_a = sb("hot_a", [P, HOTS, TOPK, na], F16)
        rhs = sb("rhs", [P, HOTS, TOPK, na], F16)
        wgu = sb("wsgu", [P, KT, 2, FS])
        wd = sb("wsd", [P, 3, D])
        gate = sb("sgate", [P, 2, T])
        up = sb("sup", [P, 2, T])
        ac = sb("sact", [P, 3, TOK])
        iota = k.cb[:, slice(*CB["iota"])]
        before, ones = k.cb[:, slice(*CB["before"])], k.cb[:, slice(*CB["ones"])]
        LOGITS, TABLE, GUB, YB = 0, 1, 2, 6
        units = [(half, c, at, w) for half in range(2) for c, (at, w) in enumerate(FS_CHUNKS)]
        norm = Norm(nc, k, ctx, norm_sems, n, 3, (LOGITS, TABLE))
        residual = Residual(nc, k, ctx, residual_sems, *residual_buffers)

        with nc.Block() as block:
            @block.sync
            def _(sp):
                residual.sync_loads(sp)
                sp.dma_start(wr[:], k.ins[f"router{n}"]).then_inc(w_in, 16)
                sp.dma_start(wgu[:], k.ins[f"ws_gu{n}"]).then_inc(ws_in, 16)
                for c, (at, w) in enumerate(FS_CHUNKS):
                    sp.dma_start(wd[0:w, c], k.ins[f"ws_down{n}"][at:at + w, :]).then_inc(ws_in, 16)
                sp.wait_ge(norm.scaled, NT)
                sp.dma_start(h_dram.rearrange("(t p) d -> p t d", p=P), k.h[:]).then_inc(h_out, 16)
                sp.wait_ge(h_out, 16)

            @block.tensor
            def _(pe):
                def shared_gate_up(m):
                    half, c, at, w = units[m]
                    if m >= 2:
                        pe.wait_ge(gate_done, m - 1)
                    for gu in range(2):
                        for kt in range(KT):
                            last = nc.tensor.matmul(k.ps[0:w, GUB + 2 * (m % 2) + gu, :], wgu[:, kt, gu, at:at + w],
                                                    k.hT[:, kt, half * T:(half + 1) * T],
                                                    start=kt == 0, stop=kt == KT - 1)
                    last.then_inc(gu_full, 1)

                def shared_down(t):
                    pe.wait_ge(act_done, 3 * (t // TB + 1))
                    if t < 2:
                        pe.wait_ge(residual.y_used, NT)
                    else:
                        pe.wait_ge(y_done, t - 1)
                    for c, (at, w) in enumerate(FS_CHUNKS):
                        last = nc.tensor.matmul(k.ps[:, YB + t % 2, 0:D], ac[0:w, c, t * P:(t + 1) * P], wd[0:w, c],
                                                start=c == 0, stop=c == 2)
                    last.then_inc(y_full, 1)

                for t in range(NT):
                    residual.tensor_tile(pe, t, YB + t % 2)
                    if t == TB + 1:
                        norm.tensor_transpose(pe, 0)
                pe.wait_ge(ws_in, 64)
                pe.wait_ge(norm.hT_used, KT)
                for m in range(EARLY):
                    shared_gate_up(m)
                norm.tensor_transpose(pe, 1)
                pe.wait_ge(norm.hT_used, 2 * KT)
                pe.wait_ge(w_in, 16)
                for t in range(NT):
                    for kt in range(KT):
                        last = nc.tensor.matmul(k.ps[:, LOGITS, t * E:(t + 1) * E], k.hT[:, kt, t * P:(t + 1) * P],
                                                wr[:, kt], start=kt == 0, stop=kt == KT - 1)
                last.then_inc(logits_full, 1)
                for m in range(EARLY, len(units)):
                    shared_gate_up(m)
                pe.wait_ge(sel_done, 1)
                for t in range(NT):
                    last = nc.tensor.matmul(k.ps[:, LOGITS, t * E:(t + 1) * E], before, selb[:, t],
                                            start=True, stop=t == 0)
                    for u in range(t):
                        last = nc.tensor.matmul(k.ps[:, LOGITS, t * E:(t + 1) * E], ones, selb[:, u],
                                                start=False, stop=u == t - 1)
                last.then_inc(place_full, 1)
                for t in range(NT):
                    shared_down(t)
                for t in range(NT):
                    pe.wait_ge(hot_b_done, t + 1)
                    pe.wait_ge(rhs_done, t + 1)
                    for c in range(TOPK):
                        last = nc.tensor.matmul(k.ps[:, TABLE, 0:na], hot_b[:, t % HOTS, c], rhs[:, t % HOTS, c],
                                                start=t + c == 0, stop=t == NT - 1 and c == TOPK - 1)
                    last.then_inc(hot_used, 1)

            @block.scalar
            def _(act):
                def shared_act(m):
                    half, c, at, w = units[m]
                    act.wait_ge(gu_full, m + 1)
                    if m >= 2:
                        act.wait_ge(act_done, m - 1)
                    nc.scalar.copy(up[0:w, m % 2], k.ps[0:w, GUB + 2 * (m % 2) + 1, :])
                    nc.scalar.activation(gate[0:w, m % 2], k.ps[0:w, GUB + 2 * (m % 2), :], ACT.Silu
                                         ).then_inc(gate_done, 1)

                for half in range(2):
                    residual.scalar_before(act, half)
                for t in range(NT):
                    residual.scalar_tile(act, t)
                    if t == TB:
                        norm.scalar_root(act, 0)
                norm.scalar_evacuate(act, 0)
                norm.scalar_root(act, 1)
                for m in range(EARLY):
                    shared_act(m)
                norm.scalar_evacuate(act, 1)
                act.wait_ge(key_done, 1)
                nc.scalar.activation(ex[:], key[:, :, 0:E], ACT.Exp).then_inc(exp_done, 1)
                for m in range(EARLY, len(units)):
                    shared_act(m)
                for t in range(NT):
                    act.wait_ge(y_full, t + 1)
                    nc.scalar.copy(k.sh[:, t], k.ps[:, YB + t % 2, 0:D]).then_inc(y_done, 1)
                for t in range(NT):
                    act.wait_ge(hot_a_done, t + 1)
                    if t >= HOTS:
                        act.wait_ge(hot_used, t - HOTS + 1)
                    nc.scalar.activation(rhs[:, t % HOTS], hot_a[:, t % HOTS], ACT.Copy,
                                         scale=k.cf[:, CF["token"][0] + t:CF["token"][0] + t + 1]).then_inc(rhs_done, 1)

            @block.gpsimd
            def _(pool):
                residual.gpsimd_before(pool)
                norm.gpsimd_shift(pool, 0)
                norm.gpsimd_shift(pool, 1)
                for m, (half, c, at, w) in enumerate(units):
                    pool.wait_ge(gate_done, m + 1)
                    nc.gpsimd.tensor_tensor(ac[0:w, c, half * T:(half + 1) * T], gate[0:w, m % 2], up[0:w, m % 2],
                                            ALU.mult).then_inc(act_done, 1)

            @block.vector
            def _(dve):
                step = Steps(dve, dve_step)
                v = nc.vector
                step(v.memset(gx[:], NONE))
                step(v.memset(key[:], OUT))
                for half in range(2):
                    residual.vector_before(dve, step, half)
                for half in range(2):
                    for t in range(half * TB, (half + 1) * TB):
                        residual.vector_tile(dve, step, t, YB + t % 2)
                    norm.vector_moments(step, half)
                    norm.vector_scale(dve, step, half)
                dve.wait_ge(logits_full, 1)
                step(v.tensor_copy(lg[:], k.ps[:, LOGITS, 0:NT * E].rearrange("p (t e) -> p t e", e=E)))
                if n == 1:
                    step(v.tensor_reduce(gx[:, :, 0:GROUPS], lg[:].rearrange("p t (g e) -> p t g e", g=GROUPS),
                                         axis=X, op=ALU.max))
                    for t in range(NT):
                        last = v.max(gm[:, t], gx[:, t, 0:GROUPS])
                    step(last)
                    step(v.memset(gm[:, :, GTOP:8], NONE))
                    for t in range(NT):
                        last = v.match_replace(gx[:, t], gm[:, t], gx[:, t], TAKEN)
                    step(last)
                    step(v.tensor_scalar(gx[:], gx[:], 1.0e38, None, ALU.is_ge))
                    step(v.tensor_tensor(lg[:].rearrange("p t (g e) -> p t g e", g=GROUPS),
                                         lg[:].rearrange("p t (g e) -> p t g e", g=GROUPS),
                                         gx[:, :, 0:GROUPS].unsqueeze(3).broadcast_to([P, NT, GROUPS, E // GROUPS]),
                                         ALU.mult))
                step(v.tensor_reduce(mx[:], lg[:], axis=X, op=ALU.max))
                step(v.tensor_tensor(lg[:], lg[:], mx[:].unsqueeze(2).broadcast_to([P, NT, E]), ALU.subtract))
                v.tensor_scalar_max(key[:, :, 0:E], lg[:], -88.0).then_inc(key_done, 1)
                dve.wait_ge(key_done, 1)
                for t in range(NT):
                    last = v.max(m8[:, t], key[:, t, 0:E])
                step(last)
                step(v.memset(m8[:, :, TOPK:8], OUT))
                for t in range(NT):
                    last = v.match_replace(rep[:, t], m8[:, t], key[:, t], HIT)
                step(last)
                step(v.tensor_scalar(sel[:], rep[:, :, 0:E], HIT / 2, None, ALU.is_ge))
                v.tensor_copy(selb[:], sel[:]).then_inc(sel_done, 1)
                dve.wait_ge(exp_done, 1)
                step(v.tensor_reduce(z[:], ex[:], axis=X, op=ALU.add))
                step(v.reciprocal(z[:], z[:]))
                step(v.tensor_tensor(ex[:], ex[:], z[:].unsqueeze(2).broadcast_to([P, NT, E]), ALU.mult))
                step(v.tensor_tensor(ex[:], ex[:], sel[:], ALU.mult))
                if n == 0:
                    step(v.tensor_reduce(z[:], ex[:], axis=X, op=ALU.add))
                    step(v.tensor_scalar_add(z[:], z[:], 1e-20))
                    step(v.reciprocal(z[:], z[:]))
                    step(v.tensor_tensor(ex[:], ex[:], z[:].unsqueeze(2).broadcast_to([P, NT, E]), ALU.mult))
                else:
                    step(v.tensor_scalar(ex[:], ex[:], ROUTE_SCALE, None, ALU.mult))
                dve.wait_ge(place_full, 1)
                place = k.ps[:, LOGITS, 0:NT * E].rearrange("p (t e) -> p t e", e=E)
                base = k.cf[:, slice(*CF[f"base{n}"])].unsqueeze(1).broadcast_to([P, NT, E])
                step(v.tensor_scalar(valid[:], place, float(cap), None, ALU.is_lt))
                step(v.tensor_tensor(ex[:], ex[:], valid[:], ALU.mult))
                step(v.tensor_tensor(sv[:], place, base, ALU.add))
                step(v.tensor_tensor(sv[:], sv[:], valid[:], ALU.mult))
                step(v.scalar_tensor_tensor(sv[:], sv[:], float(trash + 1), sel[:], ALU.add, ALU.mult))
                step(v.tensor_scalar_add(sv[:], sv[:], -1.0))
                for t in range(NT):
                    last = v.max(s8[:, t], sv[:, t])
                step(last)
                top = s8[:, :, 0:TOPK]
                step(v.tensor_scalar(ai[:], top, -63.5, 1.0 / P, ALU.add, ALU.mult))
                step(v.tensor_copy(af[:], ai[:]))
                step(v.scalar_tensor_tensor(bf[:], af[:], -float(P), top, ALU.mult, ALU.add))
                for t in range(NT):
                    if t >= HOTS:
                        dve.wait_ge(hot_used, t - HOTS + 1)
                        dve.wait_ge(rhs_done, t - HOTS + 1)
                    v.tensor_tensor(hot_a[:, t % HOTS], iota[:, 0:na].unsqueeze(1).broadcast_to([P, TOPK, na]),
                                    af[:, t].unsqueeze(2).broadcast_to([P, TOPK, na]), ALU.is_equal
                                    ).then_inc(hot_a_done, 1)
                    v.tensor_tensor(hot_b[:, t % HOTS], iota.unsqueeze(1).broadcast_to([P, TOPK, P]),
                                    bf[:, t].unsqueeze(2).broadcast_to([P, TOPK, P]), ALU.is_equal
                                    ).then_inc(hot_b_done, 1)
                step(v.tensor_copy(k.slot[:], top))
                step(v.tensor_tensor(eq[:], sv[:].unsqueeze(2).broadcast_to([P, NT, TOPK, E]),
                                     top.unsqueeze(3).broadcast_to([P, NT, TOPK, E]), ALU.is_equal))
                step(v.tensor_tensor(eq[:], eq[:], ex[:].unsqueeze(2).broadcast_to([P, NT, TOPK, E]), ALU.mult))
                step(v.tensor_reduce(k.wk[:], eq[:], axis=X, op=ALU.add))
                dve.wait_ge(hot_used, NT)
                step(v.tensor_copy(k.table[:, 0:na], k.ps[:, TABLE, 0:na]))


def expert_stage(nc, k, n, h_dram, y_dram):
    cap = CAP[n]
    per = SLOTS // cap
    U = max(4, per)
    GU = U // per
    XS = min(2, GU)
    WS = 4
    nb = -(-cap // P)
    rows = min(cap, P)
    turns = E // U
    names = ["x0_in", "x1_in", "w0_in", "w1_in", "w2_in", "w3_in", "ids_done", "xT0_full", "xT1_full", "xT0_used",
             "xT1_used", "gu_full", "gate_done", "act_done", "y_full", "y_done", "y0_out", "y1_out", "zero_done", "zero_out",
             "ids_seen"]
    with stage(nc, *names, gathers=2) as sems, ExitStack() as ctx:
        (x0_in, x1_in, w0_in, w1_in, w2_in, w3_in, ids_done, xT0_full, xT1_full, xT0_used, xT1_used, gu_full,
         gate_done, act_done, y_full, y_done, y0_out, y1_out, zero_done, zero_out, ids_seen) = sems
        w_in, x_in, y_out = [w0_in, w1_in, w2_in, w3_in], [x0_in, x1_in], [y0_out, y1_out]
        xT_full, xT_used = [xT0_full, xT1_full], [xT0_used, xT1_used]

        def sb(name, shape, dt=F32):
            return ctx.enter_context(sbuf(nc, name, shape, dt))

        wgu = sb("wgu", [P, WS, KT, 2, F])
        wd = sb("wd", [FH, WS, 2, D])
        ids = sb("ids", [P, XS, SB], I32)
        xe = sb("xe", [P, XS, SB, D])
        xT = sb("xT", [P, XS, KT, SLOTS])
        gate = sb("gate", [FH, 2, cap])
        ac = sb("ac", [FH, 2, 2, cap])
        ye = sb("ye", [P, 2, nb, D])
        zero = sb("zero", [1, D])
        XT, GUB, YB = 0, 2, 6

        with nc.Block() as block:
            @block.sync
            def _(sp):
                def load(e, slot):
                    sp.dma_start(wgu[:, slot], k.ins[f"w_gu{n}"][bass.ds(e, 1)]
                                 .rearrange("o p a b c -> (o p) a b c")).then_inc(w_in[slot], 16)
                    sp.dma_start(wd[:, slot], k.ins[f"w_down{n}"][bass.ds(e, 1)]
                                 .rearrange("o p a b -> (o p) a b")).then_inc(w_in[slot], 16)

                for e in range(WS):
                    load(e, e)
                with sp.Fori(1, E // WS) as turn:
                    for s in range(WS):
                        sp.wait_ge(y_full, WS * turn + (s - WS + 1))
                        load(WS * turn + s, s)

            @block.gpsimd
            def _(pool):
                nc.gpsimd.memset(zero[:], 0.0).then_inc(zero_done, 1)
                def gather(g, slot):
                    nc.gpsimd.tensor_copy(ids[:, slot], k.table[:, bass.ds(g * SB, SB)]).then_inc(ids_done, 1)
                    pool.wait_ge(ids_done, g + 1)
                    pool.sem_inc(ids_seen, 1)
                    for s in range(SB):
                        nc.gpsimd.indirect_dma_start(
                            out=xe[:, slot, s], out_offset=None, in_=h_dram,
                            in_offset=bass.IndirectOffsetOnAxis(ap=ids[:, slot, s:s + 1], axis=0),
                        ).then_inc(x_in[slot], 16)

                for g in range(XS):
                    gather(g, g)
                with pool.Fori(1, E // per // XS) as turn:
                    for s in range(XS):
                        pool.wait_ge(xT_full[1], XS * turn + (s - XS + 1))
                        gather(XS * turn + s, s)

            @block.tensor
            def _(pe):
                def transpose(turn, j):
                    g, slot = turn * GU + j, j % XS
                    pe.wait_ge(x_in[slot], turn * (16 * SB * GU // XS) + 16 * SB * (j // XS + 1))
                    for kt in range(KT):
                        pe.wait_ge(xT_used[kt], g + 1)
                        for s in range(SB):
                            last = nc.tensor.transpose(k.ps[:, XT + kt, s * P:(s + 1) * P],
                                                       xe[:, slot, s, kt * P:(kt + 1) * P], k.identf)
                        last.then_inc(xT_full[kt], 1)

                def gate_up(turn, i):
                    g, slot, col = turn * GU + i // per, (i // per) % XS, (i % per) * cap
                    pe.wait_ge(w_in[i % WS], turn * (32 * U // WS) + 32 * (i // WS + 1))
                    for kt in range(KT):
                        pe.wait_ge(xT_used[kt], g + 2)
                    pe.wait_ge(act_done, turn * U + i + 1)
                    for gu in range(2):
                        for f in range(2):
                            for kt in range(KT):
                                last = nc.tensor.matmul(k.ps[0:FH, GUB + 2 * gu + f, 0:cap],
                                                        wgu[:, i % WS, kt, gu, f * FH:(f + 1) * FH],
                                                        xT[:, slot, kt, col:col + cap],
                                                        start=kt == 0, stop=kt == KT - 1)
                    last.then_inc(gu_full, 1)

                def down(turn, i):
                    pe.wait_ge(act_done, turn * U + i + 2)
                    pe.wait_ge(y_done, turn * U + i + 1)
                    for s in range(nb):
                        for f in range(2):
                            last = nc.tensor.matmul(k.ps[0:rows, YB + s // 2, (s % 2) * D:(s % 2 + 1) * D],
                                                    ac[:, i % 2, f, s * P:s * P + rows], wd[:, i % WS, f],
                                                    start=f == 0, stop=f == 1)
                    last.then_inc(y_full, 1)

                def step(turn, i, last):
                    if per == 1 and not (last and i + 2 >= U):
                        transpose(turn, i + 2)
                    if per > 1 and i == U - 1:
                        if not last:
                            transpose(turn, GU)
                        down(turn, i)
                    if not (last and i == U - 1):
                        gate_up(turn, i + 1)
                    if not (per > 1 and i == U - 1):
                        down(turn, i)

                for j in range(XS):
                    transpose(0, j)
                gate_up(0, 0)
                with pe.Fori(0, turns - 1) as turn:
                    for i in range(U):
                        step(turn, i, False)
                for i in range(U):
                    step(turns - 1, i, True)

            @block.scalar
            def _(act):
                def output(turn, i):
                    e, slot = turn * U + i, i % 2
                    act.wait_ge(y_out[slot], turn * (8 * U) + 16 * (i // 2 + 1))
                    act.wait_ge(y_full, e + 1)
                    yf = ye[0:rows, slot].rearrange("p b d -> p (b d)")
                    pf = k.ps[0:rows, YB:YB + 2, :].rearrange("p b d -> p (b d)")
                    nc.scalar.copy(yf, pf[:, 0:nb * D]).then_inc(y_done, 1)
                    act.wait_ge(y_done, e + 2)
                    act.dma_start(y_dram[bass.ds(e * cap, cap), :].rearrange("(s p) d -> p s d", p=rows),
                                  ye[0:rows, slot]).then_inc(y_out[slot], 16)

                act.wait_ge(zero_done, 1)
                act.dma_start(y_dram[E * cap:E * cap + 1, :], zero[:]).then_inc(zero_out, 16)
                act.sem_inc(xT_used[1], 1)
                act.sem_inc(y_done, 1)
                for s in y_out:
                    act.sem_inc(s, 16)
                def slots_on_chip(turn, j):
                    act.wait_ge(xT_full[1], turn * GU + j + 1)
                    nc.scalar.copy(xT[:, j % XS, 1], k.ps[:, XT + 1, 0:SLOTS]).then_inc(xT_used[1], 1)

                def gate_of(turn, i):
                    act.wait_ge(gu_full, turn * U + i + 1)
                    nc.scalar.activation(gate[:], k.ps[0:FH, GUB:GUB + 2, 0:cap], ACT.Silu).then_inc(gate_done, 1)

                def step(turn, i, last):
                    if per == 1 and not (last and i + 2 >= U):
                        slots_on_chip(turn, i + 2)
                    if per > 1 and i == U - 1 and not last:
                        slots_on_chip(turn, GU)
                    if not (last and i == U - 1):
                        gate_of(turn, i + 1)
                    output(turn, i)

                for j in range(XS):
                    slots_on_chip(0, j)
                gate_of(0, 0)
                with act.Fori(0, turns - 1) as turn:
                    for i in range(U):
                        step(turn, i, False)
                for i in range(U):
                    step(turns - 1, i, True)
                for s in y_out:
                    act.wait_ge(s, 16 + 16 * E // 2)
                act.wait_ge(zero_out, 16)

            @block.vector
            def _(dve):
                dve.sem_inc(xT_used[0], 1)
                dve.sem_inc(act_done, 1)
                def slots_on_chip(turn, j):
                    dve.wait_ge(xT_full[0], turn * GU + j + 1)
                    nc.vector.tensor_copy(xT[:, j % XS, 0], k.ps[:, XT, 0:SLOTS]).then_inc(xT_used[0], 1)

                def act_of(turn, i):
                    dve.wait_ge(gate_done, turn * U + i + 1)
                    nc.vector.tensor_tensor(ac[:, i % 2], gate[:], k.ps[0:FH, GUB + 2:GUB + 4, 0:cap],
                                            ALU.mult).then_inc(act_done, 1)

                def step(turn, i, last):
                    if per == 1 and not (last and i + 2 >= U):
                        slots_on_chip(turn, i + 2)
                    if per > 1 and i == U - 1 and not last:
                        slots_on_chip(turn, GU)
                    if not (last and i == U - 1):
                        act_of(turn, i + 1)

                for j in range(XS):
                    slots_on_chip(0, j)
                act_of(0, 0)
                with dve.Fori(0, turns - 1) as turn:
                    for i in range(U):
                        step(turn, i, False)
                for i in range(U):
                    step(turns - 1, i, True)


class Combine:
    NAMES = ["g0_in", "g1_in", "g2_in", "g3_in", "tile_done"]
    BUFS = 4

    def __init__(self, nc, k, ctx, sems, n, y_dram):
        self.nc, self.k, self.n, self.y_dram = nc, k, n, y_dram
        self.g_in, self.tile_done = sems[:self.BUFS], sems[self.BUFS]
        self.rows = ctx.enter_context(sbuf(nc, "rows", [P, self.BUFS, TOPK, D], F32))
        self.acc = ctx.enter_context(sbuf(nc, "acc", [P, 2, D], F32))

    def gpsimd_tile(self, pool, t):
        if t >= self.BUFS:
            pool.wait_ge(self.tile_done, t - self.BUFS + 1)
        for c in range(TOPK):
            self.nc.gpsimd.indirect_dma_start(
                out=self.rows[:, t % self.BUFS, c], out_offset=None, in_=self.y_dram,
                in_offset=bass.IndirectOffsetOnAxis(ap=self.k.slot[:, t, c:c + 1], axis=0),
            ).then_inc(self.g_in[t % self.BUFS], 16)

    def vector_tile(self, dve, step, t):
        v, k, acc = self.nc.vector, self.k, self.acc[:, t % 2]
        dve.wait_ge(self.g_in[t % self.BUFS], 16 * TOPK * (t // self.BUFS + 1))
        for c in range(TOPK):
            step(v.scalar_tensor_tensor(acc, self.rows[:, t % self.BUFS, c], k.wk[:, t, c:c + 1],
                                        k.sh[:, t] if c == 0 else acc, ALU.mult, ALU.add))
        step(v.tensor_tensor(acc, acc, k.mod[:, self.n, t // TB, 5 * D:6 * D], ALU.mult))
        step(v.tensor_tensor(k.x[:, t], k.x[:, t], acc, ALU.add))
        dve.sem_inc(self.tile_done, 1)


def last_stage(nc, k, y_dram, out):
    with stage(nc, *Combine.NAMES, gathers=Combine.BUFS) as sems, stage(nc, "dve_step", "out_done") as (
            dve_step, out_done), ExitStack() as ctx:
        combine = Combine(nc, k, ctx, sems, 1, y_dram)
        with nc.Block() as block:
            @block.gpsimd
            def _(pool):
                for t in range(NT):
                    combine.gpsimd_tile(pool, t)

            @block.vector
            def _(dve):
                step = Steps(dve, dve_step)
                for t in range(NT):
                    combine.vector_tile(dve, step, t)

            @block.sync
            def _(sp):
                for t in range(NT):
                    sp.wait_ge(combine.tile_done, t + 1)
                    sp.dma_start(out[:, t], k.x[:, t]).then_inc(out_done, 16)
                sp.wait_ge(out_done, 16 * NT)


SK, SKB, SQ, SQG, SKBG, SKE, SVB = range(7)


def delta_project_stage(nc, k, y_dram, qkv, gate, g, scl, tot):
    names = ["w_in", "v_in", "ab_full", "x0_full", "x1_full", "x0_used", "x1_used", "tap_done", "conv_done", "t_full", "t_used",
             "gate_full", "gate_used", "abs_done", "exp_done", "sig_done", "sq_done", "root_done", "g_done",
             "cum_full", "cum_done", "dve_step"]
    with stage(nc, *names) as sems, stage(nc, *Combine.NAMES, gathers=Combine.BUFS) as combine_sems, \
            stage(nc, *Modulation.NAMES) as mod_sems, stage(nc, *Norm.NAMES) as norm_sems, ExitStack() as ctx:
        (w_in, v_in, ab_full, x0_full, x1_full, x0_used, x1_used, tap_done, conv_done, t_full, t_used, gate_full, gate_used,
         abs_done, exp_done, sig_done, sq_done, root_done, g_done, cum_full, cum_done, dve_step) = sems
        x_full, x_used = [x0_full, x1_full], [x0_used, x1_used]

        def sb(name, shape, dt=F32):
            return ctx.enter_context(sbuf(nc, name, shape, dt))

        NGAB = DH * DV + 2 * DH
        wq = sb("wq", [P, KT, QKV])
        wg = sb("wg", [P, KT, NGAB])
        cw = sb("cw", [CH, NCH, TAPS])
        al = sb("al", [P, 2, DH])
        cv = sb("cv", [CH, 2, T])
        ab = sb("ab", [P, NT, 2 * DH])
        xa = sb("xa", [P, NT, DH])
        u = sb("u", [P, NT, DH])
        s = sb("s", [P, NT, DH])
        s2 = sb("s2", [P, NT, DH])
        pl = sb("pl", [P, NT, DH])
        sq = sb("sq", [P, NT, 2 * DH * DK])
        ss = sb("ss", [P, NT, 2 * DH])
        cum = sb("cum", [P, 2, NT, DH])
        XB, TBK, GB, AB, CUM = 0, 2, 4, 6, 7
        combine = Combine(nc, k, ctx, combine_sems, 0, y_dram)
        mod = Modulation(nc, k, ctx, mod_sems, 1)
        norm = Norm(nc, k, ctx, norm_sems, 1, 0, (AB, CUM))

        with nc.Block() as block:
            @block.sync
            def _(sp):
                sp.dma_start(wg[:], k.ins["w_gab"]).then_inc(w_in, 16)
                sp.dma_start(wq[:], k.ins["w_qkv1"]).then_inc(w_in, 16)
                sp.dma_start(cw[:], k.ins["conv"]).then_inc(v_in, 16)
                sp.dma_start(al[:, 0], k.ins["A_log"].partition_broadcast(P)).then_inc(v_in, 16)
                sp.dma_start(al[:, 1], k.ins["dt_bias"].partition_broadcast(P)).then_inc(v_in, 16)

            @block.tensor
            def _(pe):
                def project(m):
                    b, c = divmod(m, NCH)
                    if m >= 2:
                        pe.wait_ge(x_used[m % 2], m // 2)
                    for kt in range(KT):
                        last = nc.tensor.matmul(k.ps[0:CH, XB + m % 2, :], wq[:, kt, c * CH:(c + 1) * CH],
                                                k.hT[:, kt, b * T:(b + 1) * T], start=kt == 0, stop=kt == KT - 1)
                    last.then_inc(x_full[m % 2], 1)

                def transpose(m):
                    pe.wait_ge(conv_done, m + 1)
                    if m >= 2:
                        pe.wait_ge(t_used, m - 1)
                    for q in range(TB):
                        last = nc.tensor.transpose(k.ps[:, TBK + m % 2, q * CH:(q + 1) * CH], cv[:, m % 2, q * P:(q + 1) * P],
                                                   k.identf[0:CH, 0:CH])
                    last.then_inc(t_full, 1)

                def gates(t):
                    if t >= 2:
                        pe.wait_ge(gate_used, t - 1)
                    for kt in range(KT):
                        last = nc.tensor.matmul(k.ps[:, GB + t % 2, 0:DH * DV], k.hT[:, kt, t * P:(t + 1) * P],
                                                wg[:, kt, 0:DH * DV], start=kt == 0, stop=kt == KT - 1)
                    last.then_inc(gate_full, 1)

                mod.tensor_rows(pe)
                pe.wait_ge(w_in, 32)
                for half in range(2):
                    norm.tensor_transpose(pe, half)
                    pe.wait_ge(norm.hT_used, KT * (half + 1))
                    if half == 0:
                        pe.wait_ge(mod.rows_used, len(mod.FILLS))
                    if half == 1:
                        for t in range(NT):
                            for kt in range(KT):
                                last = nc.tensor.matmul(k.ps[:, AB, t * 2 * DH:(t + 1) * 2 * DH],
                                                        k.hT[:, kt, t * P:(t + 1) * P], wg[:, kt, DH * DV:],
                                                        start=kt == 0, stop=kt == KT - 1)
                        last.then_inc(ab_full, 1)
                    for m in range(half * NCH, (half + 1) * NCH):
                        project(m)
                        if m % 2:
                            gates(m // 2)
                        if m > half * NCH:
                            transpose(m - 1)
                    transpose((half + 1) * NCH - 1)
                pe.wait_ge(g_done, 1)
                gf = g[:].rearrange("p t h -> p (t h)")
                n = NT * DH
                nc.tensor.matmul(k.ps[:, CUM, 0:n], k.cf[:, slice(*CF["upto"])], gf, start=True, stop=True)
                nc.tensor.matmul(k.ps[:, CUM, n:2 * n], k.cf[:, slice(*CF["after"])], gf, start=True, stop=True)
                nc.tensor.matmul(k.ps[0:DK, CUM, 2 * n:3 * n], k.cf[:, slice(*CF["ones"])], gf,
                                 start=True, stop=True).then_inc(cum_full, 1)

            @block.gpsimd
            def _(pool):
                for t in range(NT):
                    combine.gpsimd_tile(pool, t)
                    if t == TB + 1:
                        norm.gpsimd_shift(pool, 0)
                norm.gpsimd_shift(pool, 1)

            @block.scalar
            def _(act):
                def first_tap(m):
                    b, c = divmod(m, NCH)
                    act.wait_ge(x_full[m % 2], m // 2 + 1)
                    if m >= 2:
                        act.wait_ge(t_full, m - 1)
                    nc.scalar.activation(cv[:, m % 2], k.ps[0:CH, XB + m % 2, :], ACT.Copy,
                                         scale=cw[:, c, TAPS - 1:TAPS]).then_inc(tap_done, 1)

                def convolved(m):
                    b, c = divmod(m, NCH)
                    act.wait_ge(t_full, m + 1)
                    nc.scalar.activation(qkv[:, b * TB:(b + 1) * TB, c * CH:(c + 1) * CH],
                                         k.ps[:, TBK + m % 2, 0:TB * CH].rearrange("p (t c) -> p t c", c=CH),
                                         ACT.Silu).then_inc(t_used, 1)

                mod.scalar_loads(act)
                mod.scalar_silu(act)
                mod.scalar_rows(act)
                act.wait_ge(v_in, 48)
                for half in range(2):
                    if half == 0:
                        norm.scalar_root(act, 0)
                    norm.scalar_evacuate(act, half)
                    for m in range(half * NCH, (half + 1) * NCH):
                        if m == NCH - 2:
                            norm.scalar_root(act, 1)
                        first_tap(m)
                        if m % 2:
                            t = m // 2
                            act.wait_ge(gate_full, t + 1)
                            nc.scalar.activation(gate[:, t], k.ps[:, GB + t % 2, 0:DH * DV], ACT.Silu
                                                 ).then_inc(gate_used, 1)
                        if m > half * NCH:
                            convolved(m - 1)
                    convolved((half + 1) * NCH - 1)
                act.wait_ge(abs_done, 1)
                nc.scalar.activation(al[:, 0], al[:, 0], ACT.Exp)
                nc.scalar.activation(u[:], u[:], ACT.Exp).then_inc(exp_done, 1)
                nc.scalar.activation(scl[:, :, SVB], ab[:, :, DH:2 * DH], ACT.Sigmoid).then_inc(sig_done, 1)
                act.wait_ge(sq_done, 1)
                nc.scalar.activation(ss[:], ss[:], ACT.Sqrt).then_inc(root_done, 1)
                act.wait_ge(cum_full, 1)
                n = NT * DH
                nc.scalar.activation(cum[:].rearrange("p a t h -> p (a t h)"), k.ps[:, CUM, 0:2 * n], ACT.Exp)
                nc.scalar.activation(tot[:].rearrange("p t h -> p (t h)"), k.ps[0:DK, CUM, 2 * n:3 * n],
                                     ACT.Exp).then_inc(cum_done, 1)

            @block.vector
            def _(dve):
                step = Steps(dve, dve_step)
                v = nc.vector
                def convolve(m):
                    b, c = divmod(m, NCH)
                    y, x = cv[:, m % 2], k.ps[0:CH, XB + m % 2, :]
                    dve.wait_ge(tap_done, m + 1)
                    for back in range(1, TAPS):
                        ins = v.scalar_tensor_tensor(y[:, back:], x[:, 0:T - back], cw[:, c, TAPS - 1 - back:TAPS - back],
                                                     y[:, back:], ALU.mult, ALU.add)
                        if back < TAPS - 1:
                            step(ins)
                    ins.then_inc(conv_done, 1)
                    dve.wait_ge(conv_done, m + 1)
                    dve.sem_inc(x_used[m % 2], 1)

                mod.vector_repeat(dve)
                for t in range(TB):
                    combine.vector_tile(dve, step, t)
                norm.vector_moments(step, 0)
                mod.vector_scales(dve, step)
                norm.vector_scale(dve, step, 0)
                dve.wait_ge(v_in, 48)
                for t in range(TB, NT):
                    combine.vector_tile(dve, step, t)
                    for m in range(2 * (t - TB), 2 * (t - TB) + 2):
                        if t < NT - 1:
                            convolve(m)
                norm.vector_moments(step, 1)
                norm.vector_scale(dve, step, 1)
                for m in range(NCH - 2, NCH):
                    convolve(m)
                dve.wait_ge(ab_full, 1)
                step(v.tensor_copy(ab[:], k.ps[:, AB, 0:NT * 2 * DH].rearrange("p (t c) -> p t c", c=2 * DH)))
                step(v.tensor_tensor(xa[:], ab[:, :, 0:DH], al[:, 1].unsqueeze(1).broadcast_to([P, NT, DH]), ALU.add))
                v.scalar_tensor_tensor(u[:], xa[:], -1.0, xa[:], ALU.mult, ALU.min).then_inc(abs_done, 1)
                for m in range(NCH, B * NCH):
                    convolve(m)
                mod.vector_gates(step)
                dve.wait_ge(exp_done, 1)
                step(v.tensor_scalar_add(s[:], u[:], 2.0))
                step(v.reciprocal(s[:], s[:]))
                step(v.tensor_tensor(s[:], s[:], u[:], ALU.mult))
                step(v.tensor_tensor(s2[:], s[:], s[:], ALU.mult))
                step(v.tensor_scalar(pl[:], s2[:], 1.0 / 17, None, ALU.mult))
                for d in (15, 13, 11, 9, 7, 5, 3):
                    step(v.scalar_tensor_tensor(pl[:], pl[:], 1.0 / d, s2[:], ALU.add, ALU.mult))
                step(v.scalar_tensor_tensor(pl[:], pl[:], 1.0, s[:], ALU.add, ALU.mult))
                step(v.tensor_scalar(xa[:], xa[:], 0.0, None, ALU.max))
                step(v.scalar_tensor_tensor(xa[:], pl[:], 2.0, xa[:], ALU.mult, ALU.add))
                v.scalar_tensor_tensor(g[:], xa[:], -1.0, al[:, 0].unsqueeze(1).broadcast_to([P, NT, DH]),
                                       ALU.mult, ALU.mult).then_inc(g_done, 1)
                dve.wait_ge(t_used, B * NCH)
                qk = qkv[:, :, 0:2 * DH * DK]
                step(v.tensor_tensor(sq[:], qk, qk, ALU.mult))
                step(v.tensor_reduce(ss[:], sq[:].rearrange("p t (h d) -> p t h d", d=DK), axis=X, op=ALU.add))
                v.tensor_scalar_add(ss[:], ss[:], 1e-6).then_inc(sq_done, 1)
                dve.wait_ge(root_done, 1)
                step(v.reciprocal(ss[:], ss[:]))
                dve.wait_ge(sig_done, 1)
                dve.wait_ge(cum_done, 1)
                rq, rk, beta = ss[:, :, 0:DH], ss[:, :, DH:2 * DH], scl[:, :, SVB]
                step(v.tensor_copy(scl[:, :, SK], rk))
                step(v.tensor_tensor(scl[:, :, SKB], rk, beta, ALU.mult))
                step(v.tensor_scalar(scl[:, :, SQ], rq, float(DK) ** -0.5, None, ALU.mult))
                step(v.tensor_tensor(scl[:, :, SQG], scl[:, :, SQ], cum[:, 0], ALU.mult))
                step(v.tensor_tensor(scl[:, :, SKBG], scl[:, :, SKB], cum[:, 0], ALU.mult))
                step(v.tensor_tensor(scl[:, :, SKE], rk, cum[:, 1], ALU.mult))


def delta_stage(nc, k, qkv, g, scl, tot, o_all):
    HP = DH * P
    HB = HP // 2
    NL = len(LEVELS)
    L_KT, L_QT, L_D, L_KQ, L_P, L_W1T, L_O, NLF = 0, 1, 2, 3, 4, 4 + 2 * NL, 5 + 2 * NL, 6 + 2 * NL
    R_KBT, R_QGT, R_KK, R_X0, R_XP, R_W1, R_DELTA, R_S, NRF = 0, 1, 2, 3, 4, 3 + NL, 4 + NL, 5 + NL, 6 + NL
    names = []
    for b in range(B):
        names += [f"l{b}_full", f"l{b}_used", f"r{b}_full", f"r{b}_used", f"prep{b}_done", f"decay{b}_done",
                  f"y{b}_done", f"lev{b}_done", f"pool{b}_step", f"s{b}_step", f"state{b}_zero"]
    with stage(nc, *names) as sems, ExitStack() as ctx:
        per = len(names) // B
        (l_full, l_used, r_full, r_used, prep_done, decay_done, y_done, lev_done, pool_step, s_step, s_zero) = (
            [sems[b * per + i] for b in range(B)] for i in range(per))

        def sb(name, shape, dt=F32):
            return [ctx.enter_context(sbuf(nc, f"{name}{b}", shape, dt)) for b in range(B)]

        mats = sb("mats", [P, 4, DH, DK])
        ke = sb("ke", [P, DH, DK])
        wr = sb("wr", [P, DH, DV + DK])
        matT = sb("matT", [DK, 4, 2, HB])
        ex = sb("ex", [P, 2, HB])
        spare = [[buf[:].rearrange("p t d -> p (t d)")[:, i * HP:(i + 1) * HP].rearrange("p (a n) -> p a n", a=2)
                  for i in range(2)] for buf in (k.h, k.sh)]
        at, mt = [spare[b][0] for b in range(B)], [spare[b][1] for b in range(B)]
        RING = 2
        lev = sb("lev", [P, RING, 2, HB])
        xx = sb("xx", [P, 2, HB])
        yy = sb("yy", [P, 2, HB])
        pp = sb("pp", [P, 2, HB])
        gs = [x[:].rearrange("p a (h j) -> p (a h) j", j=P) for x in pp]
        w1 = sb("w1", [P, 2, DH // 2, DV + DK])
        w1t = sb("w1t", [DK, 2, HB])
        de = sb("de", [P, DH, DV])
        state = sb("state", [DK, DH, DV])
        base = CF["lev"][0]

        def bank(b, side):
            return 4 * b + 2 * side

        def pair(b, side, p=P, w=HB):
            return k.ps[0:p, bank(b, side):bank(b, side) + 2, 0:w]

        def at_head(b, side, h, p=P, w=P):
            c = (h % 3) * w
            return k.ps[0:p, bank(b, side) + h // 3, c:c + w]

        def head(t, h, w=P):
            return t[:, h // 3, (h % 3) * w:(h % 3 + 1) * w]

        with nc.Block() as block:
            @block.gpsimd
            def _(pool):
                g_ = nc.gpsimd
                for b in range(B):
                    g_.memset(state[b][:], 0.0).then_inc(s_zero[b], 1)

                def prepare(c, b):
                    t = c + b * TB
                    pool.wait_ge(r_used[b], c * NRF + 1)

                    def scaled(out, at_, width, m):
                        src = qkv[:, bass.ds(t, 1), at_:at_ + DH * width].rearrange("p o (h d) -> p (o h) d", d=width)
                        sc = scl[:, bass.ds(t, 1), m].rearrange("p o h -> p (o h)").unsqueeze(2)
                        return g_.tensor_tensor(out, src, sc.broadcast_to([P, DH, width]), ALU.mult)

                    q_at, k_at, v_at = 0, DH * DK, 2 * DH * DK
                    scaled(mats[b][:, 0], k_at, DK, SK)
                    scaled(mats[b][:, 1], k_at, DK, SKB)
                    scaled(mats[b][:, 2], q_at, DK, SQ)
                    scaled(mats[b][:, 3], q_at, DK, SQG)
                    scaled(ke[b][:], k_at, DK, SKE)
                    scaled(wr[b][:, :, 0:DV], v_at, DV, SVB)
                    scaled(wr[b][:, :, DV:], k_at, DK, SKBG).then_inc(prep_done[b], 1)

                def mask(i):
                    return k.cf[:, base + i * P:base + (i + 1) * P].unsqueeze(1).broadcast_to([P, DH, P])

                def heads_of(t):
                    return t.rearrange("p a (h i) -> p (a h) i", i=P)

                def first(c, b):
                    y = heads_of(yy[b][:])
                    pool.wait_ge(r_used[b], c * NRF + R_KK + 2)
                    g_.tensor_tensor(y, heads_of(at[b]), mask(0), ALU.mult).then_inc(pool_step[b], 1)
                    pool.wait_ge(pool_step[b], c + 1)
                    g_.tensor_tensor(y, k.identf.unsqueeze(1).broadcast_to([P, DH, P]), y,
                                     ALU.subtract).then_inc(y_done[b], 1)

                def level(c, b, i):
                    if i >= RING:
                        pool.wait_ge(l_full[b], c * NLF + (L_P + 2 * (i - RING) + 1))
                    g_.tensor_tensor(heads_of(lev[b][:, i % RING]), heads_of(at[b]), mask(i + 1),
                                     ALU.mult).then_inc(lev_done[b], 1)

                with pool.Fori(0, TB) as c:
                    for b in range(B):
                        prepare(c, b)
                    for b in range(B):
                        first(c, b)
                    for i in range(NL):
                        for b in range(B):
                            level(c, b, i)

            @block.tensor
            def _(pe):
                def left_free(c, b, i):
                    pe.wait_ge(l_used[b], c * NLF + i + 1)

                def left_there(c, b, i):
                    pe.wait_ge(l_used[b], c * NLF + i + 2)

                def right_free(c, b, i):
                    pe.wait_ge(r_used[b], c * NRF + i + 1)

                def right_there(c, b, i):
                    pe.wait_ge(r_used[b], c * NRF + i + 2)

                def transposes(c, b, side, m, i):
                    (right_free if side else left_free)(c, b, i)
                    for h in range(DH):
                        last = nc.tensor.transpose(at_head(b, side, h, DK), mats[b][:, m, h], k.identf)
                    last.then_inc((r_full if side else l_full)[b], 1)

                for b in range(B):
                    pe.wait_ge(s_zero[b], 1)
                with pe.Fori(0, TB) as c:
                    for b in range(B):
                        pe.wait_ge(prep_done[b], c + 1)
                        transposes(c, b, 0, 0, L_KT)
                        transposes(c, b, 1, 1, R_KBT)
                        transposes(c, b, 0, 2, L_QT)
                        transposes(c, b, 1, 3, R_QGT)
                    for b in range(B):
                        pe.wait_ge(decay_done[b], c + 1)
                        left_free(c, b, L_D)
                        for h in range(DH):
                            nc.tensor.matmul(at_head(b, 0, h), gs[b][:, h], k.cf[:, slice(*CF["upto"])],
                                             start=True, stop=False)
                            last = nc.tensor.matmul(at_head(b, 0, h), k.identb, k.cb[:, slice(*CB["past"])],
                                                    start=False, stop=True)
                        last.then_inc(l_full[b], 1)
                    for b in range(B):
                        right_free(c, b, R_KK)
                        left_there(c, b, L_KT)
                        for h in range(DH):
                            last = nc.tensor.matmul(at_head(b, 1, h), head(matT[b][:, 0], h), head(matT[b][:, 1], h),
                                                    start=True, stop=True)
                        last.then_inc(r_full[b], 1)
                    for b in range(B):
                        left_free(c, b, L_KQ)
                        for h in range(DH):
                            last = nc.tensor.matmul(at_head(b, 0, h), head(matT[b][:, 0], h), head(matT[b][:, 2], h),
                                                    start=True, stop=True)
                        last.then_inc(l_full[b], 1)
                    for b in range(B):
                        right_free(c, b, R_X0)
                        pe.wait_ge(y_done[b], c + 1)
                        for h in range(DH):
                            last = nc.tensor.transpose(at_head(b, 1, h), head(yy[b], h), k.identf)
                        last.then_inc(r_full[b], 1)
                    for i in range(NL):
                        for b in range(B):
                            left_free(c, b, L_P + 2 * i)
                            pe.wait_ge(lev_done[b], c * NL + i + 1)
                            right_there(c, b, R_X0 + i)
                            for h in range(DH):
                                last = nc.tensor.matmul(at_head(b, 0, h), head(lev[b][:, i % RING], h), head(xx[b], h),
                                                        start=True, stop=True)
                            last.then_inc(l_full[b], 1)
                        for b in range(B):
                            left_there(c, b, L_P + 2 * i)
                            if i < NL - 1:
                                right_free(c, b, R_XP + i)
                                for h in range(DH):
                                    last = nc.tensor.matmul(at_head(b, 1, h), head(yy[b], h), head(pp[b], h),
                                                            start=True, stop=True)
                                last.then_inc(r_full[b], 1)
                            for h in range(DH):
                                last = nc.tensor.matmul(at_head(b, 0, h), head(pp[b], h), head(yy[b], h),
                                                        start=True, stop=True)
                            last.then_inc(l_full[b], 1)
                    for b in range(B):
                        left_there(c, b, L_P + 2 * NL - 1)
                        right_free(c, b, R_W1)
                        for h in range(DH):
                            last = nc.tensor.matmul(at_head(b, 1, h, P, DV + DK), head(yy[b], h), wr[b][:, h],
                                                    start=True, stop=True)
                        last.then_inc(r_full[b], 1)
                        for h in range(DH):
                            last = nc.tensor.matmul(at_head(b, 0, h, DK), wr[b][:, h, DV:], head(yy[b], h),
                                                    start=True, stop=True)
                        last.then_inc(l_full[b], 1)
                    for b in range(B):
                        left_there(c, b, L_W1T)
                        right_free(c, b, R_DELTA)
                        for h in range(DH):
                            last = nc.tensor.matmul(k.ps[:, bank(b, 1), h * DV:(h + 1) * DV], head(w1t[b], h),
                                                    state[b][:, h], start=True, stop=True)
                        last.then_inc(r_full[b], 1)
                    for b in range(B):
                        right_there(c, b, R_DELTA)
                        left_free(c, b, L_O)
                        for h in range(DH):
                            o = k.ps[:, bank(b, 0), h * DV:(h + 1) * DV]
                            nc.tensor.matmul(o, head(matT[b][:, 3], h), state[b][:, h], start=True, stop=False)
                            last = nc.tensor.matmul(o, head(mt[b], h), de[b][:, h], start=False, stop=True)
                        last.then_inc(l_full[b], 1)
                        for h in range(DH):
                            last = nc.tensor.matmul(k.ps[0:DK, bank(b, 1), h * DV:(h + 1) * DV], ke[b][:, h],
                                                    de[b][:, h], start=True, stop=True)
                        last.then_inc(r_full[b], 1)

            @block.scalar
            def _(act):
                def left(c, b, i, out, src, func=ACT.Copy):
                    act.wait_ge(l_full[b], c * NLF + i + 1)
                    nc.scalar.activation(out, src, func).then_inc(l_used[b], 1)

                def right(c, b, i, out, src):
                    act.wait_ge(r_full[b], c * NRF + i + 1)
                    nc.scalar.activation(out, src, ACT.Copy).then_inc(r_used[b], 1)

                for b in range(B):
                    act.sem_inc(l_used[b], 1)
                    act.sem_inc(r_used[b], 1)
                with act.Fori(0, TB) as c:
                    for b in range(B):
                        left(c, b, L_KT, matT[b][:, 0], pair(b, 0, DK))
                        right(c, b, R_KBT, matT[b][:, 1], pair(b, 1, DK))
                        left(c, b, L_QT, matT[b][:, 2], pair(b, 0, DK))
                        right(c, b, R_QGT, matT[b][:, 3], pair(b, 1, DK))
                    for b in range(B):
                        left(c, b, L_D, ex[b][:], pair(b, 0), ACT.Exp)
                    for b in range(B):
                        right(c, b, R_X0, xx[b][:], pair(b, 1))
                    for i in range(NL):
                        for b in range(B):
                            left(c, b, L_P + 2 * i, pp[b][:], pair(b, 0))
                    for b in range(B):
                        right(c, b, R_W1, w1[b][:].rearrange("p a h d -> p a (h d)"), pair(b, 1, P, 3 * (DV + DK)))
                        left(c, b, L_W1T, w1t[b][:], pair(b, 0, DK))
                    for b in range(B):
                        left(c, b, L_O, o_all[:, bass.ds(c + b * TB, 1)].rearrange("p o n -> p (o n)"),
                             k.ps[:, bank(b, 0), 0:DH * DV])

            @block.vector
            def _(dve):
                v = nc.vector
                with dve.Fori(0, TB) as c:
                    for b in range(B):
                        dve.wait_ge(l_used[b], c * NLF + 1)
                        gt = g[:, bass.ds(c + b * TB, 1)].rearrange("p o h -> p (o h)").unsqueeze(2)
                        v.tensor_tensor(gs[b], k.cf[:, slice(*CF["after"])].unsqueeze(1).broadcast_to([P, DH, P]),
                                        gt.broadcast_to([P, DH, P]), ALU.mult).then_inc(decay_done[b], 1)
                    for b in range(B):
                        dve.wait_ge(r_full[b], c * NRF + R_KK + 1)
                        dve.wait_ge(l_used[b], c * NLF + L_D + 2)
                        v.tensor_tensor(at[b], pair(b, 1), ex[b][:], ALU.mult).then_inc(r_used[b], 1)
                    for b in range(B):
                        dve.wait_ge(l_full[b], c * NLF + L_KQ + 1)
                        v.tensor_tensor(mt[b], pair(b, 0), ex[b][:], ALU.mult).then_inc(l_used[b], 1)
                    for i in range(NL):
                        for b in range(B):
                            if i < NL - 1:
                                dve.wait_ge(r_full[b], c * NRF + R_XP + i + 1)
                                v.tensor_tensor(xx[b][:], xx[b][:], pair(b, 1), ALU.subtract).then_inc(r_used[b], 1)
                            dve.wait_ge(l_full[b], c * NLF + L_P + 2 * i + 2)
                            v.tensor_tensor(yy[b][:], yy[b][:], pair(b, 0), ALU.subtract).then_inc(l_used[b], 1)
                    for b in range(B):
                        dve.wait_ge(r_full[b], c * NRF + R_DELTA + 1)
                        v.tensor_tensor(de[b][:].rearrange("p (a h) d -> p a h d", a=2), w1[b][:, :, :, 0:DV],
                                        k.ps[:, bank(b, 1), 0:DH * DV].rearrange("p (a h d) -> p a h d", a=2, d=DV),
                                        ALU.subtract).then_inc(r_used[b], 1)
                    for b in range(B):
                        dve.wait_ge(r_full[b], c * NRF + R_S + 1)
                        tt = tot[:, bass.ds(c + b * TB, 1)].rearrange("p o h -> p (o h)").unsqueeze(2)
                        v.tensor_tensor(state[b][:], state[b][:], tt.broadcast_to([DK, DH, DV]),
                                        ALU.mult).then_inc(s_step[b], 1)
                        dve.wait_ge(s_step[b], c + 1)
                        v.tensor_tensor(state[b][:], state[b][:],
                                        k.ps[0:DK, bank(b, 1), 0:DH * DV].rearrange("p (h d) -> p h d", d=DV),
                                        ALU.add).then_inc(r_used[b], 1)


class Kernel:
    pass


def build(nc, ins, out):
    NAMES.clear()
    SEMS.clear()
    k = Kernel()
    k.ins = ins
    ctx = ExitStack()
    with ctx:
        def sb(name, shape, dt=F32):
            return ctx.enter_context(sbuf(nc, name, shape, dt))

        k.ps = ctx.enter_context(nc.psum_tensor("ps", [P, 8, 512], F32))
        k.x = sb("x", [P, NT, D])
        k.h = sb("h", [P, NT, D])
        k.hT = sb("hT", [P, KT, TOK])
        k.mod = sb("mod", [P, 2, B, NMOD])
        k.cf = sb("cf", [P, CF_W])
        k.cb = sb("cb", [P, CB_W], BF16)
        k.identf = k.cf[:, slice(*CF["ident"])]
        k.identb = k.cb[:, slice(*CB["ident"])]
        k.future = k.cb[:, slice(*CB["future"])]
        k.sh = sb("sh", [P, NT, D])
        k.slot = sb("slot", [P, NT, TOPK], I32)
        k.wk = sb("wk", [P, NT, TOPK])
        k.table = sb("table", [P, E * CAP[0] // P], I32)
        h_dram = nc.dram_tensor("h_rows", [TOK, D], F32).ap()
        y_dram = [nc.dram_tensor(f"y_rows{n}", [E * CAP[n] + 1, D], F32).ap() for n in (0, 1)]
        k.wo_in = ctx.enter_context(nc.semaphore("wo_in"))

        first_stage(nc, k)
        with ExitStack() as scope:
            attn = scope.enter_context(sbuf(nc, "attn", [P, HEADS * B, T], F32))
            wo = scope.enter_context(sbuf(nc, "wo", [P, HEADS, D], F32))
            with nc.Block() as block:
                @block.sync
                def _(sp):
                    sp.dma_start(wo[:], ins["w_o"]).then_inc(k.wo_in, 16)
            attention_stage(nc, k, attn)
            route_stage(nc, k, 0, h_dram, AttentionOut, attn, wo)
        expert_stage(nc, k, 0, h_dram, y_dram[0])
        renew(nc)
        with ExitStack() as scope:
            def buf(name, shape):
                return scope.enter_context(sbuf(nc, name, shape))

            gate = buf("gate_act", [P, NT, DH * DV])
            g = buf("g", [P, NT, DH])
            tot = buf("tot", [DK, NT, DH])
            o_all = buf("o_all", [P, NT, DH * DV])
            scl = buf("scl", [P, NT, 7, DH])
            with sbuf(nc, "qkv", [P, NT, QKV]) as qkv:
                delta_project_stage(nc, k, y_dram[0], qkv, gate, g, scl, tot)
                delta_stage(nc, k, qkv, g, scl, tot, o_all)
            route_stage(nc, k, 1, h_dram, DeltaOut, gate, o_all)
        expert_stage(nc, k, 1, h_dram, y_dram[1])
        last_stage(nc, k, y_dram[1], out)
        return k


def layouts(a):
    g = {name: np.asarray(v) for name, v in a.items()}

    def rows(m, p=P):
        return np.ascontiguousarray(m.reshape(m.shape[0] // p, p, *m.shape[1:]).swapaxes(0, 1))

    o = {}
    o["cf"], o["cb"] = constants()
    o["x"] = rows(g["L0_attn_query"].reshape(TOK, D))
    for n in (0, 1):
        o[f"c{n}"] = rows(g[f"L{n}_c"].T)
        o[f"wmod{n}"] = rows(g[f"L{n}_wmod"])
    qkv = np.stack([g[f"L0_attn_w_{c}"].reshape(KT, P, HEADS, HD) for c in "qkv"])
    o["w_qkv"] = np.ascontiguousarray(qkv.transpose(3, 2, 0, 1, 4))
    o["b_qkv"] = np.ascontiguousarray(np.stack([g[f"L0_attn_b_{c}"].reshape(HEADS, HD) for c in "qkv"]).transpose(2, 0, 1))
    o["w_o"] = rows(g["L0_attn_w_o"])
    o["b_o"] = g["L0_attn_b_o"]
    o["router0"] = rows(g["L0_ffn_wg_router"].T)
    o["router1"] = rows(g["L1_ffn_gate_w"].T)
    gu0 = np.stack([g["L0_ffn_w_gate"], g["L0_ffn_w_up"]], 2)
    gu1 = g["L1_ffn_w_gate_up"].reshape(E, D, 2, F)
    for n, gu in ((0, gu0), (1, gu1)):
        o[f"w_gu{n}"] = np.ascontiguousarray(gu.reshape(E, KT, P, 2, F).transpose(0, 2, 1, 3, 4))
        wd = g[f"L{n}_ffn_w_down"]
        o[f"w_down{n}"] = np.ascontiguousarray(wd.reshape(E, 2, FH, D).transpose(0, 2, 1, 3))
        o[f"ws_down{n}"] = g[f"L{n}_ffn_ws_down"]
    o["ws_gu0"] = rows(np.stack([g["L0_ffn_ws_gate"], g["L0_ffn_ws_up"]], 1))
    o["ws_gu1"] = rows(g["L1_ffn_ws_gate_up"].reshape(D, 2, FS))
    o["w_qkv1"] = rows(np.concatenate([g["L1_attn_Wq"], g["L1_attn_Wk"], g["L1_attn_Wv"]]).T)
    o["w_gab"] = rows(np.concatenate([g["L1_attn_Wg"], g["L1_attn_Wa"], g["L1_attn_Wb"]]).T)
    conv = np.concatenate([g["L1_attn_conv_q_w"], g["L1_attn_conv_k_w"], g["L1_attn_conv_v_w"]])[:, 0]
    o["conv"] = rows(conv, CH)
    o["A_log"], o["dt_bias"], o["norm_w"] = g["L1_attn_A_log"], g["L1_attn_dt_bias"], g["L1_attn_norm_w"]
    o["w_o1"] = rows(g["L1_attn_Wo"].T)
    return {n: np.ascontiguousarray(v) for n, v in o.items()}


def kernel(**inputs):
    import concourse.bacc as bacc
    from concourse.bass_utils import run_bass_kernel_spmd

    nc = bacc.Bacc("TRN2", target_bir_lowering=False, num_devices=1)
    arrays = {f"in_{n}": v for n, v in layouts(inputs).items()}
    ins = {n[3:]: nc.dram_tensor(n, v.shape, mybir.dt.from_np(v.dtype), kind="ExternalInput").ap()
           for n, v in arrays.items()}
    out = nc.dram_tensor("out", [P, NT, D], F32, kind="ExternalOutput").ap()
    build(nc, ins, out)
    r = run_bass_kernel_spmd(nc, [arrays], core_ids=[0])
    y = r.results[0]["out"]
    return np.ascontiguousarray(y.swapaxes(0, 1)).reshape(B, T, D)
```

```python
from contextlib import ExitStack, contextmanager

import numpy as np

import concourse.bass as bass
import concourse.mybir as mybir

F32 = mybir.dt.float32
BF16 = mybir.dt.bfloat16
F16 = mybir.dt.float16
I32 = mybir.dt.int32
F32R = mybir.dt.float32r
ALU = mybir.AluOpType
ACT = mybir.ActivationFunctionType
X = mybir.AxisListType.X

P = 128
B, T, D = 2, 512, 256
TOK = B * T
NT = TOK // P
TB = T // P
KT = D // P
NMOD = 6 * D

HEADS, HD = 16, 128
SCALE = float(HD) ** -0.5

E, TOPK, F = 32, 6, 176
FH = F // 2
FS = 2 * F
HOTS = 4
EARLY = 3
FS_CHUNKS = [(0, 128), (128, 128), (256, 96)]
CAP = [2 * (TOK * TOPK // E), 48]
GROUPS, GTOP = 8, 3
ROUTE_SCALE = 16.0

DH, DK, DV = 6, 32, 64
QKV = DH * (2 * DK + DV)
CH = 96
NCH = QKV // CH
TAPS = 4
LEVELS = [2, 4, 8, 16, 32, 64]
NEG = -1.0e30

CF = {}
_at = 0
for _n, _w in (("ident", P), ("after", P), ("upto", P), ("ones", DK), ("base0", E), ("base1", E),
               ("token", NT), ("lev", (len(LEVELS) + 1) * P)):
    CF[_n] = (_at, _at + _w)
    _at += _w
CF_W = _at
CB = {}
_at = 0
for _n, _w in (("ident", P), ("future", P), ("past", P), ("before", P), ("ones", P), ("iota", P)):
    CB[_n] = (_at, _at + _w)
    _at += _w
CB_W = _at


def constants():
    i = np.arange(P)
    cf = np.zeros((P, CF_W), np.float32)
    cf[:, slice(*CF["ident"])] = np.eye(P)
    cf[:, slice(*CF["after"])] = i[:, None] > i[None, :]
    cf[:, slice(*CF["upto"])] = i[:, None] <= i[None, :]
    cf[:, slice(*CF["ones"])] = 1.0
    for n in (0, 1):
        cf[:, slice(*CF[f"base{n}"])] = (np.arange(E) * CAP[n] - E * CAP[n])[None, :]
    cf[:, slice(*CF["token"])] = i[:, None] + P * np.arange(NT)[None, :]
    at = CF["lev"][0]
    for s in [1] + LEVELS:
        j, k = i[:, None], i[None, :]
        cf[:, at:at + P] = (j // (2 * s) == k // (2 * s)) & (j // s % 2 == 0) & (k // s % 2 == 1)
        at += P
    cb = np.zeros((P, CB_W), np.float32)
    cb[:, slice(*CB["ident"])] = np.eye(P)
    cb[:, slice(*CB["future"])] = np.where(i[None, :] > i[:, None], NEG, 0.0)
    cb[:, slice(*CB["past"])] = np.where(i[None, :] < i[:, None], NEG, 0.0)
    cb[:, slice(*CB["before"])] = i[:, None] < i[None, :]
    cb[:, slice(*CB["ones"])] = 1.0
    cb[:, slice(*CB["iota"])] = i[None, :]
    return cf, cb.astype(mybir.dt.np(BF16))


SEMS = []


@contextmanager
def stage(nc, *names, gathers=0):
    NAMES["stage"] = NAMES.get("stage", 0) + 1
    guards = [nc.semaphore(f"{n}_s{NAMES['stage']}") for n in names]
    sems = [g.__enter__() for g in guards]
    SEMS.append((gathers, guards, sems))
    yield sems


def renew(nc):
    with nc.Block() as block:
        @block.sync
        def _(sp):
            for n, _, sems in SEMS:
                for s in sems[n:]:
                    sp.sem_clear(s)
    for n, guards, _ in reversed(SEMS):
        for g in reversed(guards[n:]):
            g.__exit__(None, None, None)
    SEMS.clear()


class Steps:

    def __init__(self, engine, sem, base=0):
        self.engine, self.sem, self.base, self.n = engine, sem, base, 0

    def __call__(self, ins):
        ins.then_inc(self.sem, 1)
        self.n += 1
        self.engine.wait_ge(self.sem, self.base + self.n)


NAMES = {}


def sbuf(nc, name, shape, dt=F32):
    NAMES[name] = NAMES.get(name, -1) + 1
    return nc.sbuf_tensor(f"{name}_{NAMES[name]}" if NAMES[name] else name, shape, dt)


class Modulation:
    NAMES = ["c_in", "w0_in", "w1_in", "w2_in", "silu_done", "rep_done", "rows_full", "rows_used"]
    FILLS = [(b, c) for c in range(NMOD // 512) for b in range(B)]

    def __init__(self, nc, k, ctx, sems, layer):
        self.nc, self.k, self.layer = nc, k, layer
        self.c_in, *self.w_in, self.silu_done, self.rep_done, self.rows_full, self.rows_used = sems
        self.ct = ctx.enter_context(sbuf(nc, "ct", [P, KT, B], F32))
        self.rep = ctx.enter_context(sbuf(nc, "rep", [P, KT * B, P], F32))
        self.wm = ctx.enter_context(sbuf(nc, "wm", [P, KT, NMOD], F32))
        self.sign = ctx.enter_context(sbuf(nc, "sign", [P, B, 2, D], F32))

    def scalar_loads(self, act):
        act.dma_start(self.ct[:], self.k.ins[f"c{self.layer}"]).then_inc(self.c_in, 16)
        for c in range(NMOD // 512):
            act.dma_start(self.wm[:, :, 512 * c:512 * c + 512],
                          self.k.ins[f"wmod{self.layer}"][:, :, 512 * c:512 * c + 512]).then_inc(self.w_in[c], 16)

    def scalar_silu(self, act):
        act.wait_ge(self.c_in, 16)
        self.nc.scalar.activation(self.ct[:], self.ct[:], ACT.Silu).then_inc(self.silu_done, 1)

    def vector_repeat(self, dve):
        dve.wait_ge(self.silu_done, 1)
        self.nc.vector.tensor_copy(self.rep[:], self.ct[:].rearrange("p k b -> p (k b)").unsqueeze(2)
                                   .broadcast_to([P, KT * B, P])).then_inc(self.rep_done, 1)

    def tensor_rows(self, pe):
        pe.wait_ge(self.rep_done, 1)
        for n, (b, c) in enumerate(self.FILLS):
            pe.wait_ge(self.w_in[c], 16)
            for kt in range(KT):
                last = self.nc.tensor.matmul(self.k.ps[:, n, :], self.rep[:, kt * B + b, :],
                                             self.wm[:, kt, 512 * c:512 * c + 512], start=kt == 0, stop=kt == KT - 1)
            last.then_inc(self.rows_full, 1)

    def scalar_rows(self, act, chunks=range(NMOD // 512)):
        for n, (b, c) in enumerate(self.FILLS):
            if c not in chunks:
                continue
            act.wait_ge(self.rows_full, n + 1)
            self.nc.scalar.copy(self.k.mod[:, self.layer, b, 512 * c:512 * c + 512],
                                self.k.ps[:, n, :]).then_inc(self.rows_used, 1)

    def vector_scale(self, dve, step, row):
        dve.wait_ge(self.rows_used, B * (row // 2 + 1))
        m = self.k.mod[:, self.layer, :, row * D:(row + 1) * D]
        step(self.nc.vector.tensor_scalar_add(m, m, 1.0))

    def vector_rest(self, dve, step):
        self.vector_scale(dve, step, 4)
        v, sg = self.nc.vector, self.sign[:]
        m = self.k.mod[:, self.layer].rearrange("p b (s d) -> p b s d", d=D)[:, :, 2:6:3]
        step(v.tensor_scalar(sg, m, 0.0, 2.0, ALU.is_ge, ALU.mult))
        step(v.tensor_scalar_add(sg, sg, -1.0))
        step(v.tensor_tensor(m, m, sg, ALU.mult))
        step(v.scalar_tensor_tensor(m, m, 0.25, sg, ALU.max, ALU.mult))


class Norm:
    NAMES = ["moments", "root", "shaped", "scaled", "hT_full", "hT_used"]

    def __init__(self, nc, k, ctx, sems, layer, shift, banks):
        self.nc, self.k, self.layer, self.shift, self.banks = nc, k, layer, shift, banks
        self.moments, self.root, self.shaped, self.scaled, self.hT_full, self.hT_used = sems
        self.st = ctx.enter_context(sbuf(nc, "st", [P, NT, 6], F32))
        self.mv = ctx.enter_context(sbuf(nc, "mv", [P, NT, 2], F32))
        self.rt = ctx.enter_context(sbuf(nc, "rt", [P, NT], F32))

    def vector_moments(self, step, half):
        v, tiles = self.nc.vector, range(half * TB, (half + 1) * TB)
        for t in tiles:
            last = v.bn_stats(self.st[:, t], self.k.x[:, t])
        step(last)
        for t in tiles:
            last = v.bn_aggr(self.mv[:, t], self.st[:, t])
        step(last)
        s = slice(half * TB, (half + 1) * TB)
        v.tensor_scalar_add(self.rt[:, s], self.mv[:, s, 1], 1e-5).then_inc(self.moments, 1)

    def scalar_root(self, act, half):
        s = slice(half * TB, (half + 1) * TB)
        act.wait_ge(self.moments, half + 1)
        self.nc.scalar.activation(self.rt[:, s], self.rt[:, s], ACT.Sqrt).then_inc(self.root, 1)

    def vector_scale(self, dve, step, half):
        v, k = self.nc.vector, self.k
        s = slice(half * TB, (half + 1) * TB)
        dve.wait_ge(self.root, half + 1)
        step(v.reciprocal(self.rt[:, s], self.rt[:, s]))
        tiles = range(half * TB, (half + 1) * TB)
        for t in tiles:
            last = v.tensor_scalar(k.h[:, t], k.x[:, t], self.mv[:, t, 0:1], self.rt[:, t:t + 1],
                                   ALU.subtract, ALU.mult)
            if t % 2:
                step(last)
                for u in (t - 1, t):
                    v.tensor_tensor(k.h[:, u], k.h[:, u], k.mod[:, self.layer, half, (self.shift + 1) * D:
                                                                (self.shift + 2) * D], ALU.mult).then_inc(self.shaped, 1)

    def gpsimd_shift(self, pool, half):
        k = self.k
        for t in range(half * TB, (half + 1) * TB):
            pool.wait_ge(self.shaped, t + 1)
            self.nc.gpsimd.tensor_tensor(k.h[:, t], k.h[:, t], k.mod[:, self.layer, half, self.shift * D:
                                                                     (self.shift + 1) * D], ALU.add
                                         ).then_inc(self.scaled, 1)

    def tensor_transpose(self, pe, half):
        if half:
            pe.wait_ge(self.hT_used, KT)
        for kt in range(KT):
            for q in range(TB):
                t = half * TB + q
                if kt == 0:
                    pe.wait_ge(self.scaled, t + 1)
                last = self.nc.tensor.transpose(self.k.ps[:, self.banks[kt], q * P:(q + 1) * P],
                                                self.k.h[:, t, kt * P:(kt + 1) * P], self.k.identf)
            last.then_inc(self.hT_full, 1)

    def scalar_evacuate(self, act, half):
        for kt in range(KT):
            act.wait_ge(self.hT_full, half * KT + kt + 1)
            self.nc.scalar.copy(self.k.hT[:, kt, half * T:(half + 1) * T],
                                self.k.ps[:, self.banks[kt], :]).then_inc(self.hT_used, 1)


def first_stage(nc, k, w, bias):
    with stage(nc, "x_in", "const_in", "dve_step") as (x_in, const_in, dve_step), \
            stage(nc, *Modulation.NAMES) as mod_sems, stage(nc, *Norm.NAMES) as norm_sems, ExitStack() as ctx:
        mod = Modulation(nc, k, ctx, mod_sems, 0)
        norm = Norm(nc, k, ctx, norm_sems, 0, 0, (6, 7))
        with nc.Block() as block:
            @block.sync
            def _(sp):
                sp.dma_start(k.x[:], k.ins["x"]).then_inc(x_in, 16)
                sp.dma_start(k.cf[:], k.ins["cf"]).then_inc(const_in, 16)
                sp.dma_start(k.cb[:], k.ins["cb"]).then_inc(const_in, 16)
                sp.wait_ge(mod.w_in[-1], 16)
                sp.dma_start(bias[:], k.ins["b_qkv"]).then_inc(k.bias_in, 16)
                for h in range(2):
                    sp.dma_start(w[:, h], k.ins["w_qkv"][h]).then_inc(k.w_in[h], 16)

            @block.scalar
            def _(act):
                mod.scalar_loads(act)
                mod.scalar_silu(act)
                for half in range(2):
                    norm.scalar_root(act, half)
                mod.scalar_rows(act)
                for half in range(2):
                    norm.scalar_evacuate(act, half)

            @block.tensor
            def _(pe):
                mod.tensor_rows(pe)
                pe.wait_ge(const_in, 32)
                for half in range(2):
                    norm.tensor_transpose(pe, half)

            @block.vector
            def _(dve):
                step = Steps(dve, dve_step)
                dve.wait_ge(x_in, 16)
                norm.vector_moments(step, 0)
                mod.vector_repeat(dve)
                norm.vector_moments(step, 1)
                mod.vector_scale(dve, step, 1)
                for half in range(2):
                    norm.vector_scale(dve, step, half)
                mod.vector_rest(dve, step)

            @block.gpsimd
            def _(pool):
                for half in range(2):
                    norm.gpsimd_shift(pool, half)


def split_product(nc, out, lhsT, rhs, start, stop):
    nc.tensor.matmul(out, lhsT[0], rhs[0], start=start, stop=False)
    nc.tensor.matmul(out, lhsT[0], rhs[1], start=False, stop=False)
    return nc.tensor.matmul(out, lhsT[1], rhs[0], start=False, stop=stop)


def attention_stage(nc, k, attn, w, bias):
    names = ["hT_high", "hT_low", "w_high", "w_low", "pj0_full", "pj1_full", "pj0_used", "pj1_used", "s_full", "max_done",
             "p_done", "sums_inv", "p_scaled", "t0_full", "t1_full", "t0_used", "t1_used", "o_full", "o_used"]
    with stage(nc, *names) as sems, ExitStack() as ctx:
        (hT_high, hT_low, w_high, w_low, pj0_full, pj1_full, pj0_used, pj1_used, s_full, max_done, p_done, sums_inv,
         p_scaled, t0_full, t1_full, t0_used, t1_used, o_full, o_used) = sems
        w_in, bias_in = k.w_in, k.bias_in
        pj_full, pj_used = [pj0_full, pj1_full], [pj0_used, pj1_used]

        def sb(name, shape, dt=F32):
            return ctx.enter_context(sbuf(nc, name, shape, dt))

        w_s = sb("w_s", [P, 2, 2, 2, KT, HD], F32R)
        hT_s = [sb(f"hT_{part}", [P, KT, TOK], F32R) for part in ("high", "low")]
        qT = sb("qT", [P, 2, TOK])
        kT = sb("kT", [P, 2, TOK])
        v = k.h[:].rearrange("p t d -> p (t d)").rearrange("p (s t d) -> p s t d", s=2, d=HD)
        at = {3: (0, 512), 2: (512, 896), 0: (896, 1024), 1: (1024, 1280)}
        pr = sb("pr", [P, 2, 1280])
        nmax = sb("nmax", [P, 2, TB])
        sums = sb("sums", [P, 2, TB])
        inv = sb("inv", [P, 2, TB])
        pt = sb("pt", [P, 2, 1280])
        pt_at = [0, 512, 1024, 896]
        PJ, S0, T0, O = 0, 2, 5, 7
        s_banks = [[(3, 0)], [(2, 0), (0, 384)], [(1, 0)]]

        with nc.Block() as block:
            @block.sync
            def _(sp):
                def load(h, slot):
                    sp.wait_ge(pj_full[1], 3 * (h - 1))
                    sp.dma_start(w[:, slot], k.ins["w_qkv"][bass.ds(h, 1)].rearrange("o p a b c -> (o p) a b c")
                                 ).then_inc(w_in[slot], 16)

                with sp.Fori(1, HEADS // 2) as pair:
                    load(2 * pair, 0)
                    load(2 * pair + 1, 1)

            @block.tensor
            def _(pe):
                pe.wait_ge(bias_in, 16)
                fill = [0, 0]

                def project(h, slot, parts, banks=(0, 1)):
                    if "q" in parts:
                        pe.wait_ge(w_in[slot], 8 * (h - slot) + 16)
                        pe.wait_ge(w_low, h + 1)
                    for i, what in enumerate("qkv"):
                        if what not in parts:
                            continue
                        for bank in banks:
                            if not (isinstance(h, int) and h == 0 and i == 0):
                                pe.wait_ge(pj_used[bank], 3 * h + i)
                            if what == "v":
                                for q in range(TB):
                                    t = bank * TB + q
                                    for kt in range(KT):
                                        last = nc.tensor.matmul(k.ps[:, PJ + bank, q * HD:(q + 1) * HD],
                                                                k.hT[:, kt, t * P:(t + 1) * P], w[:, slot, i, kt],
                                                                start=kt == 0, stop=kt == KT - 1)
                            else:
                                for kt in range(KT):
                                    last = split_product(nc, k.ps[:, PJ + bank, :],
                                                         [w_s[:, slot, part, i, kt] for part in range(2)],
                                                         [hT_s[part][:, kt, bank * T:(bank + 1) * T]
                                                          for part in range(2)], kt == 0, kt == KT - 1)
                            last.then_inc(pj_full[bank], 1)

                def scores(h, slot, b):
                    u = 2 * h + b
                    pe.wait_ge(pj_used[b], 3 * h + 2)
                    for n, tiles in enumerate(s_banks):
                        if not (isinstance(u, int) and u == 0):
                            pe.wait_ge(p_done, 3 * u + n - 2)
                        for q, col in tiles:
                            nk = (q + 1) * P
                            nc.tensor.matmul(k.ps[:, S0 + n, col:col + nk],
                                             qT[:, slot, b * T + q * P:b * T + (q + 1) * P],
                                             kT[:, slot, b * T:b * T + nk], start=True, stop=False)
                            last = nc.tensor.matmul(k.ps[:, S0 + n, col + nk - P:col + nk], k.identb, k.future,
                                                    start=False, stop=True)
                        last.then_inc(s_full, 1)

                def weights(h, slot, b, ns):
                    u = 2 * h + b
                    for n in ns:
                        js, bank = ([0], [1, 3], [2])[n], n % 2
                        if n == 0:
                            pe.wait_ge(p_scaled, u + 1)
                        if n == 1:
                            pe.wait_ge(t1_used, u + 1)
                        else:
                            pe.wait_ge(t0_used, 2 * u + n // 2 + 1)
                        for j in js:
                            for q in range(j, TB):
                                c = pt_at[j] - pt_at[js[0]] + (q - j) * P
                                last = nc.tensor.transpose(k.ps[:, T0 + bank, c:c + P],
                                                           pr[:, b, at[q][0] + j * P:at[q][0] + (j + 1) * P],
                                                           k.identf)
                        last.then_inc(t1_full if bank else t0_full, 1)

                def values(h, slot, b):
                    u = 2 * h + b
                    pe.wait_ge(pj_used[b], 3 * h + 3)
                    pe.wait_ge(t0_used, 2 * u + 3)
                    pe.wait_ge(t1_used, u + 2)
                    pe.wait_ge(o_used, u + 1)
                    for j in range(TB):
                        nq = (TB - j) * P
                        last = nc.tensor.matmul(k.ps[:, O, j * P:], v[:, slot, b * TB + j],
                                                pt[:, b, pt_at[j]:pt_at[j] + nq], start=j == 0, stop=j == TB - 1)
                    last.then_inc(o_full, 1)

                def head(h, slot, last=False):
                    nxt = not last
                    if nxt:
                        project(h + 1, 1 - slot, "q", (0, 1))
                    scores(h, slot, 1)
                    weights(h, slot, 0, (0, 1))
                    if nxt:
                        project(h + 1, 1 - slot, "k", (0,))
                    weights(h, slot, 0, (2,))
                    if nxt:
                        project(h + 1, 1 - slot, "k", (1,))
                    values(h, slot, 0)
                    if nxt:
                        project(h + 1, 1 - slot, "v", (0,))
                        scores(h + 1, 1 - slot, 0)
                    weights(h, slot, 1, (0, 1))
                    if nxt:
                        project(h + 1, 1 - slot, "v", (1,))
                    weights(h, slot, 1, (2,))
                    values(h, slot, 1)

                pe.wait_ge(hT_low, KT)
                project(0, 0, "qkv")
                scores(0, 0, 0)
                with pe.Fori(0, HEADS // 2 - 1) as pair:
                    head(2 * pair, 0)
                    head(2 * pair + 1, 1)
                head(HEADS - 2, 0)
                head(HEADS - 1, 1, last=True)

            @block.vector
            def _(dve):
                def evac_q(h, slot):
                    for b in range(B):
                        dve.wait_ge(pj_full[b], 3 * h + 1)
                        nc.vector.tensor_scalar(qT[:, slot, b * T:(b + 1) * T], k.ps[:, PJ + b, :],
                                                bias[:, 0, bass.ds(h, 1)], SCALE, ALU.add, ALU.mult
                                                ).then_inc(pj_used[b], 1)

                def maxima(h, b):
                    u = 2 * h + b
                    for n, tiles in enumerate(s_banks):
                        dve.wait_ge(s_full, 3 * u + n + 1)
                        for q, col in tiles:
                            last = nc.vector.tensor_reduce(nmax[:, b, q:q + 1], k.ps[:, S0 + n, col:col + (q + 1) * P],
                                                           axis=X, op=ALU.max, negate=True)
                        last.then_inc(max_done, 1)

                def invert(h, b):
                    dve.wait_ge(p_done, 3 * (2 * h + b) + 3)
                    nc.vector.reciprocal(inv[:, b], sums[:, b]).then_inc(sums_inv, 1)

                def evac_t(h, b):
                    u = 2 * h + b
                    dve.wait_ge(t0_full, 2 * u + 1)
                    nc.vector.tensor_copy(pt[:, b, 0:512], k.ps[:, T0, :]).then_inc(t0_used, 1)
                    dve.wait_ge(t0_full, 2 * u + 2)
                    nc.vector.tensor_copy(pt[:, b, 1024:1280], k.ps[:, T0, 0:256]).then_inc(t0_used, 1)

                def head(h, slot, last=False):
                    if not last:
                        evac_q(h + 1, 1 - slot)
                    maxima(h, 1)
                    invert(h, 1)
                    evac_t(h, 0)
                    if not last:
                        maxima(h + 1, 0)
                        invert(h + 1, 0)
                    evac_t(h, 1)

                for kt in range(KT):
                    dve.wait_ge(hT_high, kt + 1)
                    nc.vector.tensor_tensor(hT_s[1][:, kt], k.hT[:, kt], hT_s[0][:, kt].bitcast(F32), ALU.subtract
                                            ).then_inc(hT_low, 1)
                dve.wait_ge(bias_in, 16)
                dve.sem_inc(t0_used, 1)
                evac_q(0, 0)
                maxima(0, 0)
                invert(0, 0)
                with dve.Fori(0, HEADS // 2 - 1) as pair:
                    head(2 * pair, 0)
                    head(2 * pair + 1, 1)
                head(HEADS - 2, 0)
                head(HEADS - 1, 1, last=True)

            @block.gpsimd
            def _(pool):
                def scale(h, b):
                    pool.wait_ge(sums_inv, 2 * h + b + 1)
                    for q in range(TB):
                        s = pr[:, b, at[q][0]:at[q][1]]
                        last = nc.gpsimd.tensor_tensor(s, s, inv[:, b, q:q + 1].broadcast_to([P, (q + 1) * P]), ALU.mult)
                    last.then_inc(p_scaled, 1)

                def weights_low(h, slot):
                    pool.wait_ge(w_high, h + 1)
                    nc.gpsimd.tensor_tensor(w_s[:, slot, 1], w[:, slot, 0:2], w_s[:, slot, 0].bitcast(F32),
                                            ALU.subtract).then_inc(w_low, 1)

                for h in range(2):
                    weights_low(h, h)
                scale(0, 0)
                with pool.Fori(0, HEADS // 2 - 1) as pair:
                    for s in range(2):
                        scale(2 * pair + s, 1)
                        weights_low(2 * pair + (s + 2), s)
                        scale(2 * pair + (s + 1), 0)
                scale(HEADS - 2, 1)
                scale(HEADS - 1, 0)
                scale(HEADS - 1, 1)

            @block.scalar
            def _(act):
                def weights_high(h, slot):
                    act.wait_ge(w_in[slot], 8 * (h - slot) + 16)
                    nc.scalar.copy(w_s[:, slot, 0], w[:, slot, 0:2]).then_inc(w_high, 1)

                def evac_k(h, slot):
                    for b in range(B):
                        act.wait_ge(pj_full[b], 3 * h + 2)
                    for b in range(B):
                        nc.scalar.activation(kT[:, slot, b * T:(b + 1) * T], k.ps[:, PJ + b, :], ACT.Identity,
                                             bias=bias[:, 1, bass.ds(h, 1)]).then_inc(pj_used[b], 1)

                def evac_v(h, slot, b):
                    act.wait_ge(pj_full[b], 3 * h + 3)
                    nc.scalar.copy(v[:, slot, b * TB:(b + 1) * TB].rearrange("p t d -> p (t d)"),
                                   k.ps[:, PJ + b, :]).then_inc(pj_used[b], 1)

                def exponentials(h, b):
                    u = 2 * h + b
                    if not (isinstance(u, int) and u < 2):
                        act.wait_ge(t0_full, 2 * u - 2)
                    for n, tiles in enumerate(s_banks):
                        act.wait_ge(max_done, 3 * u + n + 1)
                        for q, col in tiles:
                            last = nc.scalar.activation(pr[:, b, at[q][0]:at[q][1]],
                                                        k.ps[:, S0 + n, col:col + (q + 1) * P], ACT.Exp,
                                                        bias=nmax[:, b, q:q + 1], accum_out=sums[:, b, q:q + 1])
                        last.then_inc(p_done, 1)

                def evac_t1(h, b):
                    act.wait_ge(t1_full, 2 * h + b + 1)
                    nc.scalar.copy(pt[:, b, 512:1024], k.ps[:, T0 + 1, :]).then_inc(t1_used, 1)

                def evac_o(h, b):
                    act.wait_ge(o_full, 2 * h + b + 1)
                    nc.scalar.activation(attn[:, bass.ds(2 * h + b, 1)].rearrange("p o t -> p (o t)"), k.ps[:, O, :],
                                         ACT.Identity, bias=bias[:, 2, bass.ds(h, 1)]).then_inc(o_used, 1)

                def head(h, slot, last=False, split_next=True):
                    exponentials(h, 1)
                    evac_t1(h, 0)
                    if not last:
                        evac_k(h + 1, 1 - slot)
                    if split_next:
                        weights_high(h + 2, slot)
                    evac_o(h, 0)
                    if not last:
                        evac_v(h + 1, 1 - slot, 0)
                        exponentials(h + 1, 0)
                    evac_t1(h, 1)
                    if not last:
                        evac_v(h + 1, 1 - slot, 1)
                    evac_o(h, 1)

                for kt in range(KT):
                    nc.scalar.copy(hT_s[0][:, kt], k.hT[:, kt]).then_inc(hT_high, 1)
                for h in range(2):
                    weights_high(h, h)
                act.wait_ge(bias_in, 16)
                act.sem_inc(t1_used, 1)
                act.sem_inc(o_used, 1)
                evac_k(0, 0)
                for b in range(B):
                    evac_v(0, 0, b)
                exponentials(0, 0)
                head(0, 0)
                with act.Fori(0, HEADS // 2 - 2) as pair:
                    head(2 * pair + 1, 1)
                    head(2 * pair + 2, 0)
                head(HEADS - 3, 1)
                head(HEADS - 2, 0, split_next=False)
                head(HEADS - 1, 1, last=True, split_next=False)


class AttentionOut:
    NAMES = ["b_in", "y_full", "y_used"]

    def __init__(self, nc, k, ctx, sems, attn, wo):
        self.nc, self.k, self.attn, self.wo = nc, k, attn, wo
        self.b_in, self.y_full, self.y_used = sems
        self.bo = ctx.enter_context(sbuf(nc, "bo", [P, D], F32))
        self.y = ctx.enter_context(sbuf(nc, "y", [P, 2, D], F32))

    def sync_loads(self, sp):
        sp.dma_start(self.bo[:], self.k.ins["b_o"].partition_broadcast(P)).then_inc(self.b_in, 16)

    def tensor_tile(self, pe, t, bank):
        b, q = divmod(t, TB)
        if t == 0:
            pe.wait_ge(self.k.wo_in, 32)
        if t >= 2:
            pe.wait_ge(self.y_used, t - 1)
        for h in range(HEADS):
            last = self.nc.tensor.matmul(self.k.ps[:, bank, 0:D], self.attn[:, 2 * h + b, q * P:(q + 1) * P],
                                         self.wo[:, h] if h < HEADS // 2 else self.k.sh[:, h - HEADS // 2],
                                         start=h == 0, stop=h == HEADS - 1)
        last.then_inc(self.y_full, 1)

    def vector_tile(self, dve, step, t, bank):
        v, k, y = self.nc.vector, self.k, self.y[:, t % 2]
        if t == 0:
            dve.wait_ge(self.b_in, 16)
        dve.wait_ge(self.y_full, t + 1)
        step(v.tensor_tensor(y, k.ps[:, bank, 0:D], self.bo[:], ALU.add))
        dve.sem_inc(self.y_used, 1)
        step(v.tensor_tensor(y, y, k.mod[:, 0, t // TB, 2 * D:3 * D], ALU.mult))
        step(v.tensor_tensor(k.x[:, t], k.x[:, t], y, ALU.add))

    def vector_before(self, dve, step, half):
        pass

    def scalar_before(self, act, half):
        pass

    def scalar_tile(self, act, t):
        pass


class DeltaOut:
    NAMES = ["w_in", "n_in", "sum_done", "root_done", "w_done", "og_done", "t_full", "t_used", "y_full",
             "y_used"]
    NJ = DH * DV // P

    def __init__(self, nc, k, ctx, sems, o_all, sq):
        self.nc, self.k, self.o_all, self.sq = nc, k, o_all, sq
        (self.w_in, self.n_in, self.sum_done, self.root_done, self.w_done, self.og_done, self.t_full,
         self.t_used, self.y_full, self.y_used) = sems

        def sb(name, shape):
            return ctx.enter_context(sbuf(nc, name, shape, F32))

        self.wo = sb("wo1", [P, self.NJ, D])
        self.nw = sb("nw", [P, 1])
        self.ms = sb("ms", [P, NT, DH])
        self.ogT = sb("ogT", [P, 2, self.NJ, P])
        self.y = sb("y1", [P, 2, D])

    def sync_loads(self, sp):
        sp.dma_start(self.wo[:], self.k.ins["w_o1"]).then_inc(self.w_in, 16)
        for i in range(P // DV):
            sp.dma_start(self.nw[i * DV:(i + 1) * DV, :], self.k.ins["norm_w"].unsqueeze(1)).then_inc(self.n_in, 16)

    def vector_before(self, dve, step, half):
        v, ms = self.nc.vector, self.ms[:, half * TB:(half + 1) * TB]
        if half == 0:
            dve.wait_ge(self.w_in, 16)
            dve.wait_ge(self.n_in, 32)
            v.tensor_scalar(self.wo[:], self.wo[:], self.nw[:, 0:1], None, ALU.mult).then_inc(self.w_done, 1)
        step(v.tensor_reduce(ms, self.sq[:, half * TB:(half + 1) * TB].rearrange("p t (h d) -> p t h d", d=DV),
                             axis=X, op=ALU.add))
        v.tensor_scalar(ms, ms, 1.0 / DV, 1e-5, ALU.mult, ALU.add).then_inc(self.sum_done, 1)
        dve.wait_ge(self.root_done, half + 1)
        step(v.reciprocal(ms, ms))
        for t in range(half * TB, (half + 1) * TB):
            o = self.o_all[:, t].rearrange("p (h d) -> p h d", d=DV)
            v.tensor_tensor(o, o, self.ms[:, t].unsqueeze(2).broadcast_to([P, DH, DV]), ALU.mult
                            ).then_inc(self.og_done, 1)

    def scalar_before(self, act, half):
        ms = self.ms[:, half * TB:(half + 1) * TB]
        act.wait_ge(self.sum_done, half + 1)
        self.nc.scalar.activation(ms, ms, ACT.Sqrt).then_inc(self.root_done, 1)

    def scalar_tile(self, act, t):
        act.wait_ge(self.t_full, t + 1)
        if t >= 2:
            act.wait_ge(self.y_full, t - 1)
        self.nc.scalar.copy(self.ogT[:, t % 2].rearrange("p j t -> p (j t)"),
                            self.k.ps[:, 2 + t % 2, 0:self.NJ * P]).then_inc(self.t_used, 1)

    def transpose(self, pe, t):
        pe.wait_ge(self.og_done, t + 1)
        if t >= 2:
            pe.wait_ge(self.t_used, t - 1)
        for j in range(self.NJ):
            last = self.nc.tensor.transpose(self.k.ps[:, 2 + t % 2, j * P:(j + 1) * P],
                                            self.o_all[:, t, j * P:(j + 1) * P], self.k.identf)
        last.then_inc(self.t_full, 1)

    def tensor_tile(self, pe, t, bank):
        if t == 0:
            pe.wait_ge(self.w_done, 1)
            self.transpose(pe, 0)
        if t + 1 < NT:
            self.transpose(pe, t + 1)
        pe.wait_ge(self.t_used, t + 1)
        if t >= 2:
            pe.wait_ge(self.y_used, t - 1)
        for j in range(self.NJ):
            last = self.nc.tensor.matmul(self.k.ps[:, bank, 0:D], self.ogT[:, t % 2, j], self.wo[:, j],
                                         start=j == 0, stop=j == self.NJ - 1)
        last.then_inc(self.y_full, 1)

    def vector_tile(self, dve, step, t, bank):
        v, k, y = self.nc.vector, self.k, self.y[:, t % 2]
        dve.wait_ge(self.y_full, t + 1)
        step(v.tensor_tensor(y, k.ps[:, bank, 0:D], k.mod[:, 1, t // TB, 2 * D:3 * D], ALU.mult))
        dve.sem_inc(self.y_used, 1)
        step(v.tensor_tensor(k.x[:, t], k.x[:, t], y, ALU.add))


def route_stage(nc, k, n, h_dram, Residual, *residual_buffers):
    cap, trash, na = CAP[n], E * CAP[n], E * CAP[n] // P
    HIT, OUT = 10.0, -1.0e4
    TAKEN, NONE = 3.0e38, -3.0e38
    names = ["w_in", "logits_full", "key_done", "exp_done", "sel_done", "place_full", "hot_b_done", "hot_a_done",
             "rhs_done", "hot_used", "dve_step", "ws_in", "gu_full", "gate_done", "act_done",
             "y_full", "y_done", "h_out"]
    with stage(nc, *names) as sems, stage(nc, *Norm.NAMES) as norm_sems, \
            stage(nc, *Residual.NAMES) as residual_sems, ExitStack() as ctx:
        (w_in, logits_full, key_done, exp_done, sel_done, place_full, hot_b_done, hot_a_done, rhs_done,
         hot_used, dve_step, ws_in, gu_full, gate_done, act_done, y_full, y_done, h_out) = sems

        def sb(name, shape, dt=F32):
            return ctx.enter_context(sbuf(nc, name, shape, dt))

        wr = sb("wr", [P, KT, E])
        lg = sb("lg", [P, NT, E])
        gx = sb("gx", [P, NT, GROUPS + 8 - GTOP])
        gm = sb("gm", [P, NT, 8])
        mx = sb("mx", [P, NT])
        key = sb("key", [P, NT, E + 2])
        rep = sb("rep", [P, NT, E + 2])
        m8 = sb("m8", [P, NT, 8])
        ex = k.probs
        z = sb("z", [P, NT])
        sel = sb("sel", [P, NT, E])
        selb = sb("selb", [P, NT, E], BF16)
        valid = sb("valid", [P, NT, E])
        sv, s8 = k.sv, k.s8
        ai = sb("ai", [P, NT, TOPK], I32)
        af = sb("af", [P, NT, TOPK], BF16)
        bf = sb("bf", [P, NT, TOPK], BF16)
        hot_b = sb("hot_b", [P, HOTS, TOPK, P], F16)
        hot_a = sb("hot_a", [P, HOTS, TOPK, na], F16)
        rhs = sb("rhs", [P, HOTS, TOPK, na], F16)
        wgu = sb("wsgu", [P, KT, 2, FS])
        wd = sb("wsd", [P, 3, D])
        gate = sb("sgate", [P, 2, T])
        up = sb("sup", [P, 2, T])
        ac = sb("sact", [P, 3, TOK])
        iota = k.cb[:, slice(*CB["iota"])]
        before, ones = k.cb[:, slice(*CB["before"])], k.cb[:, slice(*CB["ones"])]
        LOGITS, TABLE, GUB, YB = 0, 1, 2, 6
        units = [(half, c, at, w) for half in range(2) for c, (at, w) in enumerate(FS_CHUNKS)]
        norm = Norm(nc, k, ctx, norm_sems, n, 3, (LOGITS, TABLE))
        residual = Residual(nc, k, ctx, residual_sems, *residual_buffers)

        with nc.Block() as block:
            @block.sync
            def _(sp):
                residual.sync_loads(sp)
                sp.dma_start(wr[:], k.ins[f"router{n}"]).then_inc(w_in, 16)
                sp.dma_start(wgu[:], k.ins[f"ws_gu{n}"]).then_inc(ws_in, 16)
                for c, (at, w) in enumerate(FS_CHUNKS):
                    sp.dma_start(wd[0:w, c], k.ins[f"ws_down{n}"][at:at + w, :]).then_inc(ws_in, 16)
                sp.wait_ge(norm.scaled, NT)
                sp.dma_start(h_dram.rearrange("(t p) d -> p t d", p=P), k.h[:]).then_inc(h_out, 16)
                sp.wait_ge(h_out, 16)

            @block.tensor
            def _(pe):
                def shared_gate_up(m):
                    half, c, at, w = units[m]
                    if m >= 2:
                        pe.wait_ge(gate_done, m - 1)
                    for gu in range(2):
                        for kt in range(KT):
                            last = nc.tensor.matmul(k.ps[0:w, GUB + 2 * (m % 2) + gu, :], wgu[:, kt, gu, at:at + w],
                                                    k.hT[:, kt, half * T:(half + 1) * T],
                                                    start=kt == 0, stop=kt == KT - 1)
                    last.then_inc(gu_full, 1)

                def shared_down(t):
                    pe.wait_ge(act_done, 3 * (t // TB + 1))
                    if t < 2:
                        pe.wait_ge(residual.y_used, NT)
                    else:
                        pe.wait_ge(y_done, t - 1)
                    for c, (at, w) in enumerate(FS_CHUNKS):
                        last = nc.tensor.matmul(k.ps[:, YB + t % 2, 0:D], ac[0:w, c, t * P:(t + 1) * P], wd[0:w, c],
                                                start=c == 0, stop=c == 2)
                    last.then_inc(y_full, 1)

                for t in range(NT):
                    residual.tensor_tile(pe, t, YB + t % 2)
                    if t == TB + 1:
                        norm.tensor_transpose(pe, 0)
                pe.wait_ge(ws_in, 64)
                pe.wait_ge(norm.hT_used, KT)
                for m in range(EARLY):
                    shared_gate_up(m)
                norm.tensor_transpose(pe, 1)
                pe.wait_ge(norm.hT_used, 2 * KT)
                pe.wait_ge(w_in, 16)
                for t in range(NT):
                    for kt in range(KT):
                        last = nc.tensor.matmul(k.ps[:, LOGITS, t * E:(t + 1) * E], k.hT[:, kt, t * P:(t + 1) * P],
                                                wr[:, kt], start=kt == 0, stop=kt == KT - 1)
                last.then_inc(logits_full, 1)
                for m in range(EARLY, len(units)):
                    shared_gate_up(m)
                pe.wait_ge(sel_done, 1)
                for t in range(NT):
                    last = nc.tensor.matmul(k.ps[:, LOGITS, t * E:(t + 1) * E], before, selb[:, t],
                                            start=True, stop=t == 0)
                    for u in range(t):
                        last = nc.tensor.matmul(k.ps[:, LOGITS, t * E:(t + 1) * E], ones, selb[:, u],
                                                start=False, stop=u == t - 1)
                last.then_inc(place_full, 1)
                for t in range(NT):
                    shared_down(t)
                for t in range(NT):
                    pe.wait_ge(hot_b_done, t + 1)
                    pe.wait_ge(rhs_done, t + 1)
                    for c in range(TOPK):
                        last = nc.tensor.matmul(k.ps[:, TABLE, 0:na], hot_b[:, t % HOTS, c], rhs[:, t % HOTS, c],
                                                start=t + c == 0, stop=t == NT - 1 and c == TOPK - 1)
                    last.then_inc(hot_used, 1)

            @block.scalar
            def _(act):
                def shared_act(m):
                    half, c, at, w = units[m]
                    act.wait_ge(gu_full, m + 1)
                    if m >= 2:
                        act.wait_ge(act_done, m - 1)
                    nc.scalar.copy(up[0:w, m % 2], k.ps[0:w, GUB + 2 * (m % 2) + 1, :])
                    nc.scalar.activation(gate[0:w, m % 2], k.ps[0:w, GUB + 2 * (m % 2), :], ACT.Silu
                                         ).then_inc(gate_done, 1)

                for half in range(2):
                    residual.scalar_before(act, half)
                for t in range(NT):
                    residual.scalar_tile(act, t)
                    if t == TB:
                        norm.scalar_root(act, 0)
                norm.scalar_evacuate(act, 0)
                norm.scalar_root(act, 1)
                for m in range(EARLY):
                    shared_act(m)
                norm.scalar_evacuate(act, 1)
                act.wait_ge(key_done, 1)
                nc.scalar.activation(ex[:], key[:, :, 0:E], ACT.Exp).then_inc(exp_done, 1)
                for m in range(EARLY, len(units)):
                    shared_act(m)
                for t in range(NT):
                    act.wait_ge(y_full, t + 1)
                    nc.scalar.copy(k.sh[:, t], k.ps[:, YB + t % 2, 0:D]).then_inc(y_done, 1)
                for t in range(NT):
                    act.wait_ge(hot_a_done, t + 1)
                    if t >= HOTS:
                        act.wait_ge(hot_used, t - HOTS + 1)
                    nc.scalar.activation(rhs[:, t % HOTS], hot_a[:, t % HOTS], ACT.Copy,
                                         scale=k.cf[:, CF["token"][0] + t:CF["token"][0] + t + 1]).then_inc(rhs_done, 1)

            @block.gpsimd
            def _(pool):
                norm.gpsimd_shift(pool, 0)
                norm.gpsimd_shift(pool, 1)
                for m, (half, c, at, w) in enumerate(units):
                    pool.wait_ge(gate_done, m + 1)
                    nc.gpsimd.tensor_tensor(ac[0:w, c, half * T:(half + 1) * T], gate[0:w, m % 2], up[0:w, m % 2],
                                            ALU.mult).then_inc(act_done, 1)

            @block.vector
            def _(dve):
                step = Steps(dve, dve_step)
                v = nc.vector
                step(v.memset(gx[:], NONE))
                step(v.memset(key[:], OUT))
                for half in range(2):
                    residual.vector_before(dve, step, half)
                for half in range(2):
                    for t in range(half * TB, (half + 1) * TB):
                        residual.vector_tile(dve, step, t, YB + t % 2)
                    norm.vector_moments(step, half)
                    norm.vector_scale(dve, step, half)
                dve.wait_ge(logits_full, 1)
                step(v.tensor_copy(lg[:], k.ps[:, LOGITS, 0:NT * E].rearrange("p (t e) -> p t e", e=E)))
                if n == 1:
                    step(v.tensor_reduce(gx[:, :, 0:GROUPS], lg[:].rearrange("p t (g e) -> p t g e", g=GROUPS),
                                         axis=X, op=ALU.max))
                    for t in range(NT):
                        last = v.max(gm[:, t], gx[:, t, 0:GROUPS])
                    step(last)
                    step(v.memset(gm[:, :, GTOP:8], NONE))
                    for t in range(NT):
                        last = v.match_replace(gx[:, t], gm[:, t], gx[:, t], TAKEN)
                    step(last)
                    step(v.tensor_scalar(gx[:], gx[:], 1.0e38, None, ALU.is_ge))
                    step(v.tensor_tensor(lg[:].rearrange("p t (g e) -> p t g e", g=GROUPS),
                                         lg[:].rearrange("p t (g e) -> p t g e", g=GROUPS),
                                         gx[:, :, 0:GROUPS].unsqueeze(3).broadcast_to([P, NT, GROUPS, E // GROUPS]),
                                         ALU.mult))
                step(v.tensor_reduce(mx[:], lg[:], axis=X, op=ALU.max))
                step(v.tensor_tensor(lg[:], lg[:], mx[:].unsqueeze(2).broadcast_to([P, NT, E]), ALU.subtract))
                v.tensor_scalar_max(key[:, :, 0:E], lg[:], -88.0).then_inc(key_done, 1)
                dve.wait_ge(key_done, 1)
                for t in range(NT):
                    last = v.max(m8[:, t], key[:, t, 0:E])
                step(last)
                step(v.memset(m8[:, :, TOPK:8], OUT))
                for t in range(NT):
                    last = v.match_replace(rep[:, t], m8[:, t], key[:, t], HIT)
                step(last)
                step(v.tensor_scalar(sel[:], rep[:, :, 0:E], HIT / 2, None, ALU.is_ge))
                v.tensor_copy(selb[:], sel[:]).then_inc(sel_done, 1)
                dve.wait_ge(exp_done, 1)
                step(v.tensor_reduce(z[:], ex[:], axis=X, op=ALU.add))
                step(v.reciprocal(z[:], z[:]))
                step(v.tensor_tensor(ex[:], ex[:], z[:].unsqueeze(2).broadcast_to([P, NT, E]), ALU.mult))
                step(v.tensor_tensor(ex[:], ex[:], sel[:], ALU.mult))
                if n == 0:
                    step(v.tensor_reduce(z[:], ex[:], axis=X, op=ALU.add))
                    step(v.tensor_scalar_add(z[:], z[:], 1e-20))
                    step(v.reciprocal(z[:], z[:]))
                    step(v.tensor_tensor(ex[:], ex[:], z[:].unsqueeze(2).broadcast_to([P, NT, E]), ALU.mult))
                else:
                    step(v.tensor_scalar(ex[:], ex[:], ROUTE_SCALE, None, ALU.mult))
                dve.wait_ge(place_full, 1)
                place = k.ps[:, LOGITS, 0:NT * E].rearrange("p (t e) -> p t e", e=E)
                base = k.cf[:, slice(*CF[f"base{n}"])].unsqueeze(1).broadcast_to([P, NT, E])
                step(v.tensor_scalar(valid[:], place, float(cap), None, ALU.is_lt))
                step(v.tensor_tensor(ex[:], ex[:], valid[:], ALU.mult))
                step(v.tensor_tensor(sv[:], place, base, ALU.add))
                step(v.tensor_tensor(sv[:], sv[:], valid[:], ALU.mult))
                step(v.scalar_tensor_tensor(sv[:], sv[:], float(trash + 1), sel[:], ALU.add, ALU.mult))
                step(v.tensor_scalar_add(sv[:], sv[:], -1.0))
                for t in range(NT):
                    last = v.max(s8[:, t], sv[:, t])
                step(last)
                top = s8[:, :, 0:TOPK]
                step(v.tensor_scalar(ai[:], top, -63.5, 1.0 / P, ALU.add, ALU.mult))
                step(v.tensor_copy(af[:], ai[:]))
                step(v.scalar_tensor_tensor(bf[:], af[:], -float(P), top, ALU.mult, ALU.add))
                for t in range(NT):
                    if t >= HOTS:
                        dve.wait_ge(hot_used, t - HOTS + 1)
                        dve.wait_ge(rhs_done, t - HOTS + 1)
                    v.tensor_tensor(hot_a[:, t % HOTS], iota[:, 0:na].unsqueeze(1).broadcast_to([P, TOPK, na]),
                                    af[:, t].unsqueeze(2).broadcast_to([P, TOPK, na]), ALU.is_equal
                                    ).then_inc(hot_a_done, 1)
                    v.tensor_tensor(hot_b[:, t % HOTS], iota.unsqueeze(1).broadcast_to([P, TOPK, P]),
                                    bf[:, t].unsqueeze(2).broadcast_to([P, TOPK, P]), ALU.is_equal
                                    ).then_inc(hot_b_done, 1)
                step(v.tensor_copy(k.slot[:], top))
                dve.wait_ge(hot_used, NT)
                step(v.tensor_copy(k.table[:, 0:na], k.ps[:, TABLE, 0:na]))


def slot_weights(nc, k, dve, eq, dve_step):
    v, step = nc.vector, Steps(dve, dve_step)
    shape = [P, NT, TOPK, E]
    step(v.tensor_tensor(eq[:], k.sv[:].unsqueeze(2).broadcast_to(shape),
                         k.s8[:, :, 0:TOPK].unsqueeze(3).broadcast_to(shape), ALU.is_equal))
    step(v.tensor_tensor(eq[:], eq[:], k.probs[:].unsqueeze(2).broadcast_to(shape), ALU.mult))
    step(v.tensor_reduce(k.wk[:], eq[:], axis=X, op=ALU.add))


def wide_expert_stage(nc, k, h_dram, y_dram):
    cap = CAP[0]
    nb = cap // P
    U = 4
    XS = 2
    WS = 4
    turns = E // U
    names = ["x0_in", "x1_in", "w0_in", "w1_in", "w2_in", "w3_in", "ids_done", "ids_seen", "xT_full", "xT_high",
             "xT_used", "w_high", "w_used", "gu_full", "gate_done", "prod_done", "ac_high", "act_done",
             "y_full", "y_done", "y0_out", "y1_out", "zero_done", "zero_out", "dve_step"]
    with stage(nc, *names, gathers=2) as sems, ExitStack() as ctx:
        (x0_in, x1_in, w0_in, w1_in, w2_in, w3_in, ids_done, ids_seen, xT_full, xT_high, xT_used, w_high,
         w_used, gu_full, gate_done, prod_done, ac_high, act_done, y_full, y_done, y0_out, y1_out, zero_done,
         zero_out, dve_step) = sems
        w_in, x_in, y_out = [w0_in, w1_in, w2_in, w3_in], [x0_in, x1_in], [y0_out, y1_out]

        def sb(name, shape, dt=F32):
            return ctx.enter_context(sbuf(nc, name, shape, dt))

        wgu = sb("wgu", [P, WS, KT, 2, F])
        wd = sb("wd", [FH, WS, 2, D])
        ids = sb("ids", [P, XS, nb], I32)
        xe = sb("xe", [P, XS, nb, D])
        gate = sb("gate", [FH, 2, 2, cap])
        wgu_s = sb("wgu_s", [P, 2, 2, KT, 2, F], F32R)
        wd_s = sb("wd_s", [FH, WS, 2, 2, D], F32R)
        xT_s = sb("xT_s", [P, XS, 2, KT, cap], F32R)
        prod = sb("prod", [FH, 2, cap])
        ac_s = sb("ac_s", [FH, 2, 2, 2, cap], F32R)
        ye = sb("ye", [P, 2, nb, D])
        zero = sb("zero", [1, D])
        eq = sb("eq", [P, NT, TOPK, E])
        XT, GUB, YB = 0, 2, 6

        def gate_up_at(gu):
            return k.ps[0:FH, GUB + 2 * gu:GUB + 2 * gu + 2, 0:cap]

        with nc.Block() as block:
            @block.sync
            def _(sp):
                def load(e, slot):
                    sp.dma_start(wgu[:, slot], k.ins["w_gu0"][bass.ds(e, 1)]
                                 .rearrange("o p a b c -> (o p) a b c")).then_inc(w_in[slot], 16)
                    sp.dma_start(wd[:, slot], k.ins["w_down0"][bass.ds(e, 1)]
                                 .rearrange("o p a b -> (o p) a b")).then_inc(w_in[slot], 16)

                for e in range(WS):
                    load(e, e)
                with sp.Fori(1, E // WS) as turn:
                    for s in range(WS):
                        sp.wait_ge(w_used, WS * turn + (s - WS + 1))
                        load(WS * turn + s, s)

            @block.gpsimd
            def _(pool):
                nc.gpsimd.memset(zero[:], 0.0).then_inc(zero_done, 1)

                def gather(g, slot):
                    nc.gpsimd.tensor_copy(ids[:, slot], k.table[:, bass.ds(g * nb, nb)]).then_inc(ids_done, 1)
                    pool.wait_ge(ids_done, g + 1)
                    pool.sem_inc(ids_seen, 1)
                    for s in range(nb):
                        nc.gpsimd.indirect_dma_start(
                            out=xe[:, slot, s], out_offset=None, in_=h_dram,
                            in_offset=bass.IndirectOffsetOnAxis(ap=ids[:, slot, s:s + 1], axis=0),
                        ).then_inc(x_in[slot], 16)

                for g in range(XS):
                    gather(g, g)
                with pool.Fori(1, E // XS) as turn:
                    for s in range(XS):
                        pool.wait_ge(xT_full, XS * turn + (s - XS + 1))
                        gather(XS * turn + s, s)

            @block.tensor
            def _(pe):
                def transpose(turn, j):
                    slot = j % XS
                    pe.wait_ge(x_in[slot], turn * (16 * nb * U // XS) + 16 * nb * (j // XS + 1))
                    pe.wait_ge(xT_used, turn * U + j + 1)
                    for kt in range(KT):
                        for s in range(nb):
                            last = nc.tensor.transpose(k.ps[:, XT + kt, s * P:(s + 1) * P],
                                                       xe[:, slot, s, kt * P:(kt + 1) * P], k.identf)
                    last.then_inc(xT_full, 1)

                def gate_up(turn, i):
                    pe.wait_ge(w_used, turn * U + i + 1)
                    pe.wait_ge(prod_done, turn * U + i + 1)
                    pe.wait_ge(xT_used, turn * U + i + 2)
                    for gu in range(2):
                        for f in range(2):
                            out, fs = gate_up_at(gu)[:, f], slice(f * FH, (f + 1) * FH)
                            for kt in range(KT):
                                last = split_product(nc, out, [wgu_s[:, i % 2, part, kt, gu, fs] for part in range(2)],
                                                     [xT_s[:, i % XS, part, kt] for part in range(2)],
                                                     kt == 0, kt == KT - 1)
                    last.then_inc(gu_full, 1)

                def down(turn, i):
                    pe.wait_ge(act_done, turn * U + i + 2)
                    pe.wait_ge(y_done, turn * U + i + 1)
                    for s in range(nb):
                        out, cs = k.ps[:, YB + s // 2, (s % 2) * D:(s % 2 + 1) * D], slice(s * P, (s + 1) * P)
                        for f in range(2):
                            last = split_product(nc, out, [ac_s[:, i % 2, part, f, cs] for part in range(2)],
                                                 [wd_s[:, i % WS, part, f] for part in range(2)], f == 0, f == 1)
                    last.then_inc(y_full, 1)

                def step(turn, i, last):
                    if not (last and i + 2 >= U):
                        transpose(turn, i + 2)
                    if not (last and i == U - 1):
                        gate_up(turn, i + 1)
                    down(turn, i)

                for j in range(XS):
                    transpose(0, j)
                gate_up(0, 0)
                with pe.Fori(0, turns - 1) as turn:
                    for i in range(U):
                        step(turn, i, False)
                for i in range(U):
                    step(turns - 1, i, True)

            @block.scalar
            def _(act):
                def output(turn, i):
                    e, slot = turn * U + i, i % 2
                    act.wait_ge(y_out[slot], turn * (8 * U) + 16 * (i // 2 + 1))
                    act.wait_ge(y_full, e + 1)
                    nc.scalar.copy(ye[:, slot].rearrange("p b d -> p (b d)"),
                                   k.ps[:, YB:YB + 2, :].rearrange("p b d -> p (b d)")[:, 0:nb * D]).then_inc(y_done, 1)
                    act.wait_ge(y_done, e + 2)
                    act.dma_start(y_dram[bass.ds(e * cap, cap), :].rearrange("(s p) d -> p s d", p=P),
                                  ye[:, slot]).then_inc(y_out[slot], 16)

                act.wait_ge(zero_done, 1)
                act.dma_start(y_dram[E * cap:E * cap + 1, :], zero[:]).then_inc(zero_out, 16)
                act.sem_inc(y_done, 1)
                for s in y_out:
                    act.sem_inc(s, 16)

                def slots_on_chip(turn, j):
                    act.wait_ge(xT_full, turn * U + j + 1)
                    nc.scalar.copy(xT_s[:, j % XS, 0], k.ps[:, XT:XT + 2, 0:cap]).then_inc(xT_high, 1)

                def weights_high(turn, i):
                    act.wait_ge(w_in[i % WS], turn * (32 * U // WS) + 32 * (i // WS + 1))
                    nc.scalar.copy(wgu_s[:, i % 2, 0], wgu[:, i % WS])
                    nc.scalar.copy(wd_s[:, i % WS, 0], wd[:, i % WS]).then_inc(w_high, 1)

                def gate_of(turn, i):
                    act.wait_ge(gu_full, turn * U + i + 1)
                    nc.scalar.activation(gate[:, i % 2], gate_up_at(0), ACT.Silu).then_inc(gate_done, 1)
                    act.wait_ge(prod_done, turn * U + i + 2)
                    nc.scalar.copy(ac_s[:, i % 2, 0], prod[:]).then_inc(ac_high, 1)

                def step(turn, i, last):
                    if not (last and i + 2 >= U):
                        weights_high(turn, i + 2)
                        slots_on_chip(turn, i + 2)
                    if not (last and i == U - 1):
                        gate_of(turn, i + 1)
                    output(turn, i)

                for j in range(XS):
                    weights_high(0, j)
                    slots_on_chip(0, j)
                gate_of(0, 0)
                with act.Fori(0, turns - 1) as turn:
                    for i in range(U):
                        step(turn, i, False)
                for i in range(U):
                    step(turns - 1, i, True)
                for s in y_out:
                    act.wait_ge(s, 16 + 16 * E // 2)
                act.wait_ge(zero_out, 16)

            @block.vector
            def _(dve):
                v = nc.vector
                dve.sem_inc(xT_used, 1)
                dve.sem_inc(prod_done, 1)
                dve.sem_inc(act_done, 1)
                slot_weights(nc, k, dve, eq, dve_step)

                def low(out, whole, high):
                    return v.tensor_tensor(out, whole, high.bitcast(F32), ALU.subtract)

                def slots_on_chip(turn, j):
                    dve.wait_ge(xT_high, turn * U + j + 1)
                    low(xT_s[:, j % XS, 1], k.ps[:, XT:XT + 2, 0:cap], xT_s[:, j % XS, 0]).then_inc(xT_used, 1)

                def weights_low(turn, i):
                    dve.wait_ge(w_high, turn * U + i + 1)
                    low(wgu_s[:, i % 2, 1], wgu[:, i % WS], wgu_s[:, i % 2, 0])
                    low(wd_s[:, i % WS, 1], wd[:, i % WS], wd_s[:, i % WS, 0]).then_inc(w_used, 1)

                def act_of(turn, i):
                    dve.wait_ge(gate_done, turn * U + i + 1)
                    dve.wait_ge(act_done, turn * U + i + 1)
                    v.tensor_tensor(prod[:], gate[:, i % 2], gate_up_at(1), ALU.mult).then_inc(prod_done, 1)
                    dve.wait_ge(ac_high, turn * U + i + 1)
                    low(ac_s[:, i % 2, 1], prod[:], ac_s[:, i % 2, 0]).then_inc(act_done, 1)

                def step(turn, i, last):
                    if not (last and i + 2 >= U):
                        weights_low(turn, i + 2)
                        slots_on_chip(turn, i + 2)
                    if not (last and i == U - 1):
                        act_of(turn, i + 1)

                for j in range(XS):
                    weights_low(0, j)
                    slots_on_chip(0, j)
                act_of(0, 0)
                with dve.Fori(0, turns - 1) as turn:
                    for i in range(U):
                        step(turn, i, False)
                for i in range(U):
                    step(turns - 1, i, True)


def narrow_expert_stage(nc, k, h_dram, y_dram):
    cap = CAP[1]
    U = 8
    SLOTS = U * cap
    SB = SLOTS // P
    WS = 8
    turns = E // U
    names = ["x_in", *[f"w{s}_in" for s in range(WS)], "ids_done", "ids_seen", "xT_full", "xT0_used", "xT1_used",
             "gu_full", "gate_done", "prod_done", "acT_full", "act_done", "y_full", "y_done", "y0_out", "y1_out",
             "zero_done", "zero_out", "turns_seen", "dve_step"]
    with stage(nc, *names, gathers=1) as sems, ExitStack() as ctx:
        (x_in, *w_in, ids_done, ids_seen, xT_full, xT0_used, xT1_used, gu_full, gate_done, prod_done, acT_full,
         act_done, y_full, y_done, y0_out, y1_out, zero_done, zero_out, turns_seen,
         dve_step) = sems
        y_out, xT_used = [y0_out, y1_out], [xT0_used, xT1_used]

        def sb(name, shape, dt=F32):
            return ctx.enter_context(sbuf(nc, name, shape, dt))

        wgu = sb("wgu", [P, WS, KT, 2 * F])
        wd = sb("wd", [FH, WS, 2, D])
        ids = sb("ids", [P, SB], I32)
        xe = sb("xe", [P, SB, D])
        xT = sb("xT", [P, KT, SLOTS])
        gate = sb("gate", [cap, 2, F])
        prod = sb("prod", [cap, 2, F])
        ac = sb("ac", [FH, 2, 2, cap])
        ye = sb("ye", [cap, 2, D])
        zero = sb("zero", [1, D])
        eq = sb("eq", [P, NT, TOPK, E])
        XT, GUB, ACB, YB = 0, 2, 4, 6

        with nc.Block() as block:
            @block.sync
            def _(sp):
                def load(e, slot):
                    sp.dma_start(wgu[:, slot], k.ins["w_gu1"][bass.ds(e, 1)]
                                 .rearrange("o p a b c -> (o p) a (b c)")).then_inc(w_in[slot], 16)
                    sp.dma_start(wd[:, slot], k.ins["w_down1"][bass.ds(e, 1)]
                                 .rearrange("o p a b -> (o p) a b")).then_inc(w_in[slot], 16)

                for e in range(WS):
                    load(e, e)
                with sp.Fori(1, E // WS) as turn:
                    for s in range(WS):
                        sp.wait_ge(y_full, WS * turn + (s - WS + 1))
                        load(WS * turn + s, s)

            @block.gpsimd
            def _(pool):
                nc.gpsimd.memset(zero[:], 0.0).then_inc(zero_done, 1)

                def gather(g):
                    nc.gpsimd.tensor_copy(ids[:], k.table[:, bass.ds(g * SB, SB)]).then_inc(ids_done, 1)
                    pool.wait_ge(ids_done, g + 1)
                    pool.sem_inc(ids_seen, 1)
                    for s in range(SB):
                        nc.gpsimd.indirect_dma_start(
                            out=xe[:, s], out_offset=None, in_=h_dram,
                            in_offset=bass.IndirectOffsetOnAxis(ap=ids[:, s:s + 1], axis=0),
                        ).then_inc(x_in, 16)

                gather(0)
                with pool.Fori(1, turns) as turn:
                    pool.wait_ge(xT_full, turn)
                    gather(turn)

            @block.tensor
            def _(pe):
                def transpose(turn):
                    pe.wait_ge(x_in, turn * (16 * SB) + 16 * SB)
                    for kt in range(KT):
                        for s in range(SB):
                            last = nc.tensor.transpose(k.ps[:, XT + kt, s * P:(s + 1) * P],
                                                       xe[:, s, kt * P:(kt + 1) * P], k.identf)
                    last.then_inc(xT_full, 1)

                def gate_up(turn, i):
                    pe.wait_ge(w_in[i % WS], turn * (32 * U // WS) + 32 * (i // WS + 1))
                    pe.wait_ge(prod_done, turn * U + i + 1)
                    for used in xT_used:
                        pe.wait_ge(used, turn + (i // U + 1))
                    col = (i % U) * cap
                    for kt in range(KT):
                        last = nc.tensor.matmul(k.ps[0:cap, GUB + i % 2, 0:2 * F], xT[:, kt, col:col + cap],
                                                wgu[:, i % WS, kt], start=kt == 0, stop=kt == KT - 1)
                    last.then_inc(gu_full, 1)

                def act_transpose(turn, i):
                    pe.wait_ge(prod_done, turn * U + i + 3)
                    pe.wait_ge(act_done, turn * U + i + 1)
                    pe.sem_inc(turns_seen, 1)
                    for f in range(2):
                        last = nc.tensor.transpose(k.ps[0:FH, ACB + i % 2, f * cap:(f + 1) * cap],
                                                   prod[:, i % 2, f * FH:(f + 1) * FH], k.identf[0:cap, 0:cap])
                    last.then_inc(acT_full, 1)

                def down(turn, i):
                    pe.wait_ge(act_done, turn * U + i + 3)
                    pe.wait_ge(y_done, turn * U + i + 1)
                    for f in range(2):
                        last = nc.tensor.matmul(k.ps[0:cap, YB + i % 2, 0:D], ac[:, i % 2, f], wd[:, i % WS, f],
                                                start=f == 0, stop=f == 1)
                    last.then_inc(y_full, 1)

                def step(turn, i, last):
                    more = not (last and i + 2 >= U)
                    if i == U - 2 and not last:
                        transpose(turn + 1)
                    if i != U - 2 and more:
                        gate_up(turn, i + 2)
                    if not (last and i == U - 1):
                        act_transpose(turn, i + 1)
                    down(turn, i)
                    if i == U - 2 and more:
                        gate_up(turn, i + 2)

                transpose(0)
                gate_up(0, 0)
                gate_up(0, 1)
                act_transpose(0, 0)
                with pe.Fori(0, turns - 1) as turn:
                    for i in range(U):
                        step(turn, i, False)
                for i in range(U):
                    step(turns - 1, i, True)

            @block.scalar
            def _(act):
                def output(turn, i):
                    e, slot = turn * U + i, i % 2
                    act.wait_ge(y_out[slot], turn * (8 * U) + 16 * (i // 2 + 1))
                    act.wait_ge(y_full, e + 1)
                    nc.scalar.copy(ye[:, slot], k.ps[0:cap, YB + slot, 0:D]).then_inc(y_done, 1)
                    act.wait_ge(y_done, e + 3)
                    act.dma_start(y_dram[bass.ds(e * cap, cap), :], ye[:, slot]).then_inc(y_out[slot], 16)

                def slots_on_chip(turn):
                    act.wait_ge(xT_full, turn + 1)
                    nc.scalar.copy(xT[:, 1], k.ps[:, XT + 1, 0:SLOTS]).then_inc(xT1_used, 1)

                def gate_of(turn, i):
                    act.wait_ge(gu_full, turn * U + i + 1)
                    nc.scalar.activation(gate[:, i % 2], k.ps[0:cap, GUB + i % 2, 0:F], ACT.Silu).then_inc(gate_done, 1)

                def step(turn, i, last):
                    more = not (last and i + 2 >= U)
                    if i == U - 2 and not last:
                        slots_on_chip(turn + 1)
                    if i != U - 2 and more:
                        gate_of(turn, i + 2)
                    output(turn, i)
                    if i == U - 2 and more:
                        gate_of(turn, i + 2)

                act.wait_ge(zero_done, 1)
                act.dma_start(y_dram[E * cap:E * cap + 1, :], zero[:]).then_inc(zero_out, 16)
                act.sem_inc(y_done, 2)
                for s in y_out:
                    act.sem_inc(s, 16)
                slots_on_chip(0)
                gate_of(0, 0)
                gate_of(0, 1)
                with act.Fori(0, turns - 1) as turn:
                    for i in range(U):
                        step(turn, i, False)
                for i in range(U):
                    step(turns - 1, i, True)
                for s in y_out:
                    act.wait_ge(s, 16 + 16 * E // 2)
                act.wait_ge(zero_out, 16)

            @block.vector
            def _(dve):
                v = nc.vector
                dve.sem_inc(prod_done, 2)
                dve.sem_inc(act_done, 2)
                slot_weights(nc, k, dve, eq, dve_step)

                def slots_on_chip(turn):
                    dve.wait_ge(xT_full, turn + 1)
                    v.tensor_copy(xT[:, 0], k.ps[:, XT, 0:SLOTS]).then_inc(xT0_used, 1)

                def product(turn, i):
                    dve.wait_ge(gate_done, turn * U + i + 1)
                    v.tensor_tensor(prod[:, i % 2], gate[:, i % 2], k.ps[0:cap, GUB + i % 2, F:2 * F],
                                    ALU.mult).then_inc(prod_done, 1)

                def act_of(turn, i):
                    dve.wait_ge(acT_full, turn * U + i + 1)
                    v.tensor_copy(ac[:, i % 2].rearrange("p f c -> p (f c)"), k.ps[0:FH, ACB + i % 2, 0:2 * cap]
                                  ).then_inc(act_done, 1)

                def step(turn, i, last):
                    more = not (last and i + 2 >= U)
                    if i == U - 2 and not last:
                        slots_on_chip(turn + 1)
                    if i != U - 2 and more:
                        product(turn, i + 2)
                    if not (last and i == U - 1):
                        act_of(turn, i + 1)
                    if i == U - 2 and more:
                        product(turn, i + 2)

                slots_on_chip(0)
                product(0, 0)
                product(0, 1)
                act_of(0, 0)
                with dve.Fori(0, turns - 1) as turn:
                    for i in range(U):
                        step(turn, i, False)
                for i in range(U):
                    step(turns - 1, i, True)


class Combine:
    NAMES = ["g0_in", "g1_in", "g2_in", "g3_in", "tile_done"]
    BUFS = 4

    def __init__(self, nc, k, ctx, sems, n, y_dram):
        self.nc, self.k, self.n, self.y_dram = nc, k, n, y_dram
        self.g_in, self.tile_done = sems[:self.BUFS], sems[self.BUFS]
        self.rows = ctx.enter_context(sbuf(nc, "rows", [P, self.BUFS, TOPK, D], F32))
        self.acc = ctx.enter_context(sbuf(nc, "acc", [P, 2, D], F32))

    def gpsimd_tile(self, pool, t):
        if t >= self.BUFS:
            pool.wait_ge(self.tile_done, t - self.BUFS + 1)
        for c in range(TOPK):
            self.nc.gpsimd.indirect_dma_start(
                out=self.rows[:, t % self.BUFS, c], out_offset=None, in_=self.y_dram,
                in_offset=bass.IndirectOffsetOnAxis(ap=self.k.slot[:, t, c:c + 1], axis=0),
            ).then_inc(self.g_in[t % self.BUFS], 16)

    def vector_tile(self, dve, step, t):
        v, k, acc = self.nc.vector, self.k, self.acc[:, t % 2]
        dve.wait_ge(self.g_in[t % self.BUFS], 16 * TOPK * (t // self.BUFS + 1))
        for c in range(TOPK):
            step(v.scalar_tensor_tensor(acc, self.rows[:, t % self.BUFS, c], k.wk[:, t, c:c + 1],
                                        k.sh[:, t] if c == 0 else acc, ALU.mult, ALU.add))
        step(v.tensor_tensor(acc, acc, k.mod[:, self.n, t // TB, 5 * D:6 * D], ALU.mult))
        step(v.tensor_tensor(k.x[:, t], k.x[:, t], acc, ALU.add))
        dve.sem_inc(self.tile_done, 1)


def last_stage(nc, k, y_dram, out):
    with stage(nc, *Combine.NAMES, gathers=Combine.BUFS) as sems, stage(nc, "dve_step", "out_done") as (
            dve_step, out_done), ExitStack() as ctx:
        combine = Combine(nc, k, ctx, sems, 1, y_dram)
        with nc.Block() as block:
            @block.gpsimd
            def _(pool):
                for t in range(NT):
                    combine.gpsimd_tile(pool, t)

            @block.vector
            def _(dve):
                step = Steps(dve, dve_step)
                for t in range(NT):
                    combine.vector_tile(dve, step, t)

            @block.sync
            def _(sp):
                for t in range(NT):
                    sp.wait_ge(combine.tile_done, t + 1)
                    sp.dma_start(out[:, t], k.x[:, t]).then_inc(out_done, 16)
                sp.wait_ge(out_done, 16 * NT)


SK, SKB, SQ, SQG, SKBG, SKE, SVB = range(7)


def delta_project_stage(nc, k, y_dram, qkv, gate, g, scl, tot):
    names = ["w_in", "v_in", "squared", "x0_full", "x1_full", "x0_used", "x1_used", "tap_done", "conv_done", "t_full", "t_used",
             "gate_full", "gate_used", "abs_done", "exp_done", "sig_done", "sq_done", "root_done", "g_done",
             "cum_full", "cum_done", "dve_step"]
    with stage(nc, *names) as sems, stage(nc, *Combine.NAMES, gathers=Combine.BUFS) as combine_sems, \
            stage(nc, *Modulation.NAMES) as mod_sems, stage(nc, *Norm.NAMES) as norm_sems, ExitStack() as ctx:
        (w_in, v_in, squared, x0_full, x1_full, x0_used, x1_used, tap_done, conv_done, t_full, t_used, gate_full, gate_used,
         abs_done, exp_done, sig_done, sq_done, root_done, g_done, cum_full, cum_done, dve_step) = sems
        x_full, x_used = [x0_full, x1_full], [x0_used, x1_used]

        def sb(name, shape, dt=F32):
            return ctx.enter_context(sbuf(nc, name, shape, dt))

        NGAB = DH * DV + 2 * DH
        wq = sb("wq", [P, KT, QKV])
        wg = sb("wg", [P, KT, NGAB])
        cw = sb("cw", [CH, NCH, TAPS])
        al = sb("al", [P, 2, DH])
        cv = sb("cv", [CH, 2, T])
        ab = sb("ab", [P, NT, 2 * DH])
        xa = sb("xa", [P, NT, DH])
        u = sb("u", [P, NT, DH])
        s = sb("s", [P, NT, DH])
        s2 = sb("s2", [P, NT, DH])
        pl = sb("pl", [P, NT, DH])
        sq = sb("sq", [P, NT, 2 * DH * DK])
        ss = sb("ss", [P, NT, 2 * DH])
        cum = sb("cum", [P, 2, NT, DH])
        XB, TBK, GB, NB, CUM = 0, 2, 4, 6, 7
        combine = Combine(nc, k, ctx, combine_sems, 0, y_dram)
        mod = Modulation(nc, k, ctx, mod_sems, 1)
        norm = Norm(nc, k, ctx, norm_sems, 1, 0, (NB, CUM))

        with nc.Block() as block:
            @block.sync
            def _(sp):
                sp.dma_start(wg[:], k.ins["w_gab"]).then_inc(w_in, 16)
                sp.dma_start(wq[:], k.ins["w_qkv1"]).then_inc(w_in, 16)
                sp.dma_start(cw[:], k.ins["conv"]).then_inc(v_in, 16)
                sp.dma_start(al[:, 0], k.ins["A_log"].partition_broadcast(P)).then_inc(v_in, 16)
                sp.dma_start(al[:, 1], k.ins["dt_bias"].partition_broadcast(P)).then_inc(v_in, 16)

            @block.tensor
            def _(pe):
                def project(m):
                    b, c = divmod(m, NCH)
                    if m >= 2:
                        pe.wait_ge(x_used[m % 2], m // 2)
                    for kt in range(KT):
                        last = nc.tensor.matmul(k.ps[0:CH, XB + m % 2, :], wq[:, kt, c * CH:(c + 1) * CH],
                                                k.hT[:, kt, b * T:(b + 1) * T], start=kt == 0, stop=kt == KT - 1)
                    last.then_inc(x_full[m % 2], 1)

                def transpose(m):
                    pe.wait_ge(conv_done, m + 1)
                    if m >= 2:
                        pe.wait_ge(t_used, m - 1)
                    for q in range(TB):
                        last = nc.tensor.transpose(k.ps[:, TBK + m % 2, q * CH:(q + 1) * CH], cv[:, m % 2, q * P:(q + 1) * P],
                                                   k.identf[0:CH, 0:CH])
                    last.then_inc(t_full, 1)

                def gates(t):
                    if t >= 2:
                        pe.wait_ge(gate_used, t - 1)
                    for kt in range(KT):
                        last = nc.tensor.matmul(k.ps[:, GB + t % 2, 0:NGAB], k.hT[:, kt, t * P:(t + 1) * P],
                                                wg[:, kt], start=kt == 0, stop=kt == KT - 1)
                    last.then_inc(gate_full, 1)

                mod.tensor_rows(pe)
                pe.wait_ge(w_in, 32)
                for half in range(2):
                    norm.tensor_transpose(pe, half)
                    pe.wait_ge(norm.hT_used, KT * (half + 1))
                    if half == 0:
                        pe.wait_ge(mod.rows_used, len(mod.FILLS))
                    for m in range(half * NCH, (half + 1) * NCH):
                        project(m)
                        if m % NCH < TB:
                            gates(half * TB + m % NCH)
                        if m > half * NCH:
                            transpose(m - 1)
                    transpose((half + 1) * NCH - 1)
                pe.wait_ge(g_done, 1)
                gf = g[:].rearrange("p t h -> p (t h)")
                n = NT * DH
                nc.tensor.matmul(k.ps[:, CUM, 0:n], k.cf[:, slice(*CF["upto"])], gf, start=True, stop=True)
                nc.tensor.matmul(k.ps[:, CUM, n:2 * n], k.cf[:, slice(*CF["after"])], gf, start=True, stop=True)
                nc.tensor.matmul(k.ps[0:DK, CUM, 2 * n:3 * n], k.cf[:, slice(*CF["ones"])], gf,
                                 start=True, stop=True).then_inc(cum_full, 1)

            @block.gpsimd
            def _(pool):
                for t in range(NT):
                    combine.gpsimd_tile(pool, t)
                    if t == TB + 1:
                        norm.gpsimd_shift(pool, 0)
                norm.gpsimd_shift(pool, 1)
                for half in range(2):
                    pool.wait_ge(t_used, half * NCH + 2 * DH * DK // CH)
                    qk = qkv[:, half * TB:(half + 1) * TB, 0:2 * DH * DK]
                    nc.gpsimd.tensor_tensor(sq[:, half * TB:(half + 1) * TB], qk, qk, ALU.mult).then_inc(squared, 1)

            @block.scalar
            def _(act):
                def first_tap(m):
                    b, c = divmod(m, NCH)
                    act.wait_ge(x_full[m % 2], m // 2 + 1)
                    if m >= 2:
                        act.wait_ge(t_full, m - 1)
                    nc.scalar.activation(cv[:, m % 2], k.ps[0:CH, XB + m % 2, :], ACT.Copy,
                                         scale=cw[:, c, TAPS - 1:TAPS]).then_inc(tap_done, 1)

                def convolved(m):
                    b, c = divmod(m, NCH)
                    act.wait_ge(t_full, m + 1)
                    nc.scalar.activation(qkv[:, b * TB:(b + 1) * TB, c * CH:(c + 1) * CH],
                                         k.ps[:, TBK + m % 2, 0:TB * CH].rearrange("p (t c) -> p t c", c=CH),
                                         ACT.Silu).then_inc(t_used, 1)

                mod.scalar_loads(act)
                mod.scalar_silu(act)
                mod.scalar_rows(act)
                act.wait_ge(v_in, 48)
                for half in range(2):
                    if half == 0:
                        norm.scalar_root(act, 0)
                    norm.scalar_evacuate(act, half)
                    for m in range(half * NCH, (half + 1) * NCH):
                        if m == 4:
                            norm.scalar_root(act, 1)
                        first_tap(m)
                        if m % NCH < TB:
                            t = half * TB + m % NCH
                            act.wait_ge(gate_full, t + 1)
                            nc.scalar.activation(gate[:, t], k.ps[:, GB + t % 2, 0:DH * DV], ACT.Silu)
                            nc.scalar.copy(ab[:, t], k.ps[:, GB + t % 2, DH * DV:NGAB]).then_inc(gate_used, 1)
                        if m > half * NCH:
                            convolved(m - 1)
                        if m == NCH + TB:
                            act.wait_ge(abs_done, 1)
                            nc.scalar.activation(al[:, 0], al[:, 0], ACT.Exp)
                            nc.scalar.activation(u[:], u[:], ACT.Exp).then_inc(exp_done, 1)
                            nc.scalar.activation(scl[:, :, SVB], ab[:, :, DH:2 * DH], ACT.Sigmoid).then_inc(sig_done, 1)
                    convolved((half + 1) * NCH - 1)
                act.wait_ge(sq_done, 1)
                nc.scalar.activation(ss[:], ss[:], ACT.Sqrt).then_inc(root_done, 1)
                act.wait_ge(cum_full, 1)
                n = NT * DH
                nc.scalar.activation(cum[:].rearrange("p a t h -> p (a t h)"), k.ps[:, CUM, 0:2 * n], ACT.Exp)
                nc.scalar.activation(tot[:].rearrange("p t h -> p (t h)"), k.ps[0:DK, CUM, 2 * n:3 * n],
                                     ACT.Exp).then_inc(cum_done, 1)

            @block.vector
            def _(dve):
                step = Steps(dve, dve_step)
                v = nc.vector
                def norms(half):
                    tiles = slice(half * TB, (half + 1) * TB)
                    dve.wait_ge(squared, half + 1)
                    step(v.tensor_reduce(ss[:, tiles], sq[:, tiles].rearrange("p t (h d) -> p t h d", d=DK),
                                         axis=X, op=ALU.add))

                def convolve(m):
                    b, c = divmod(m, NCH)
                    y, x = cv[:, m % 2], k.ps[0:CH, XB + m % 2, :]
                    dve.wait_ge(tap_done, m + 1)
                    for back in range(1, TAPS):
                        ins = v.scalar_tensor_tensor(y[:, back:], x[:, 0:T - back], cw[:, c, TAPS - 1 - back:TAPS - back],
                                                     y[:, back:], ALU.mult, ALU.add)
                        if back < TAPS - 1:
                            step(ins)
                    ins.then_inc(conv_done, 1)
                    dve.wait_ge(conv_done, m + 1)
                    dve.sem_inc(x_used[m % 2], 1)

                mod.vector_repeat(dve)
                for t in range(TB):
                    combine.vector_tile(dve, step, t)
                    if t == 0:
                        mod.vector_rest(dve, step)
                norm.vector_moments(step, 0)
                mod.vector_scale(dve, step, 1)
                norm.vector_scale(dve, step, 0)
                dve.wait_ge(v_in, 48)
                for t in range(TB, NT):
                    combine.vector_tile(dve, step, t)
                    if t in (NT - 3, NT - 2):
                        for m in range(2 * (t - NT + 3), 2 * (t - NT + 3) + 2):
                            convolve(m)
                norm.vector_moments(step, 1)
                norm.vector_scale(dve, step, 1)
                for m in range(4, NCH):
                    convolve(m)
                for m in range(NCH, NCH + TB):
                    convolve(m)
                dve.wait_ge(gate_used, NT)
                step(v.tensor_tensor(xa[:], ab[:, :, 0:DH], al[:, 1].unsqueeze(1).broadcast_to([P, NT, DH]), ALU.add))
                v.scalar_tensor_tensor(u[:], xa[:], -1.0, xa[:], ALU.mult, ALU.min).then_inc(abs_done, 1)
                convolve(NCH + TB)
                norms(0)
                convolve(NCH + TB + 1)
                dve.wait_ge(exp_done, 1)
                step(v.tensor_scalar_add(s[:], u[:], 2.0))
                step(v.reciprocal(s[:], s[:]))
                step(v.tensor_tensor(s[:], s[:], u[:], ALU.mult))
                step(v.tensor_tensor(s2[:], s[:], s[:], ALU.mult))
                step(v.tensor_scalar(pl[:], s2[:], 1.0 / 17, None, ALU.mult))
                for d in (15, 13, 11, 9, 7, 5, 3):
                    step(v.scalar_tensor_tensor(pl[:], pl[:], 1.0 / d, s2[:], ALU.add, ALU.mult))
                step(v.scalar_tensor_tensor(pl[:], pl[:], 1.0, s[:], ALU.add, ALU.mult))
                step(v.tensor_scalar(xa[:], xa[:], 0.0, None, ALU.max))
                step(v.scalar_tensor_tensor(xa[:], pl[:], 2.0, xa[:], ALU.mult, ALU.add))
                v.scalar_tensor_tensor(g[:], xa[:], -1.0, al[:, 0].unsqueeze(1).broadcast_to([P, NT, DH]),
                                       ALU.mult, ALU.mult).then_inc(g_done, 1)
                for m in range(NCH + TB + 2, B * NCH):
                    convolve(m)
                norms(1)
                v.tensor_scalar_add(ss[:], ss[:], 1e-6).then_inc(sq_done, 1)
                dve.wait_ge(root_done, 1)
                step(v.reciprocal(ss[:], ss[:]))
                dve.wait_ge(sig_done, 1)
                dve.wait_ge(cum_done, 1)
                rq, rk, beta = ss[:, :, 0:DH], ss[:, :, DH:2 * DH], scl[:, :, SVB]
                step(v.tensor_copy(scl[:, :, SK], rk))
                step(v.tensor_tensor(scl[:, :, SKB], rk, beta, ALU.mult))
                step(v.tensor_scalar(scl[:, :, SQ], rq, float(DK) ** -0.5, None, ALU.mult))
                step(v.tensor_tensor(scl[:, :, SQG], scl[:, :, SQ], cum[:, 0], ALU.mult))
                step(v.tensor_tensor(scl[:, :, SKBG], scl[:, :, SKB], cum[:, 0], ALU.mult))
                step(v.tensor_tensor(scl[:, :, SKE], rk, cum[:, 1], ALU.mult))


def delta_stage(nc, k, qkv, g, scl, tot, gate, o_all, sq):
    HP = DH * P
    HB = HP // 2
    NL = len(LEVELS)
    fills = [["decay", "ksT", "kq"], ["qsT", "kk", "X"]]
    for i in range(NL):
        fills[i % 2] += [("P", i), ("Y", i)]
        if i < NL - 1:
            fills[1 - i % 2].append(("X", i))
    fills[0] += ["w1T", "out"]
    fills[1] += ["w1", "delta", "state"]
    AT = {name: (side, n) for side in range(2) for n, name in enumerate(fills[side])}
    names = []
    for b in range(B):
        names += [f"left{b}_full", f"left{b}_used", f"right{b}_full", f"right{b}_used", f"prep{b}_done", f"decay{b}_done",
                  f"y{b}_done", f"lev{b}_done", f"pool{b}_step", f"s{b}_step", f"state{b}_zero",
                  f"gated{b}_step"]
    with stage(nc, *names) as sems, ExitStack() as ctx:
        per = len(names) // B
        (l_full, l_used, r_full, r_used, prep_done, decay_done, y_done, lev_done, pool_step, s_step, s_zero,
         gated_step) = (
            [sems[b * per + i] for b in range(B)] for i in range(per))
        full, used = (l_full, r_full), (l_used, r_used)

        def sb(name, shape, dt=F32):
            return [ctx.enter_context(sbuf(nc, f"{name}{b}", shape, dt)) for b in range(B)]

        ks = sb("ks", [P, DH, 3, DK])
        qs = sb("qs", [P, DH, 3, DK])
        ke = sb("ke", [P, DH, DK])
        wr = sb("wr", [P, DH, DV + DK])
        ksT = sb("ksT", [3 * DK, 2, HB])
        qsT = sb("qsT", [3 * DK, 2, HB])
        ex = sb("ex", [P, 2, HB])
        spare = [[buf[:].rearrange("p t d -> p (t d)")[:, i * HP:(i + 1) * HP].rearrange("p (a n) -> p a n", a=2)
                  for i in range(2)] for buf in (k.h, k.sh)]
        at, mt = [spare[b][0] for b in range(B)], [spare[b][1] for b in range(B)]
        RING = 2
        lev = sb("lev", [P, RING, 2, HB])
        xx = sb("xx", [P, 2, HB])
        yy = sb("yy", [P, 2, HB])
        pp = sb("pp", [P, 2, HB])
        gs = [x[:].rearrange("p a (h j) -> p (a h) j", j=P) for x in pp]
        w1 = sb("w1", [P, 2, DH // 2, DV + DK])
        w1t = sb("w1t", [DK, 2, HB])
        de = sb("de", [P, DH, DV])
        state = sb("state", [DK, DH, DV])
        base = CF["lev"][0]

        def bank(b, name):
            return 4 * b + 2 * AT[name][0]

        def pair(b, name, p=P, w=HB):
            return k.ps[0:p, bank(b, name):bank(b, name) + 2, 0:w]

        def at_head(b, name, h, p=P, w=P):
            c = (h % 3) * w
            return k.ps[0:p, bank(b, name) + h // 3, c:c + w]

        def wait_full(engine, c, b, name):
            side, n = AT[name]
            engine.wait_ge(full[side][b], c * len(fills[side]) + n + 1)

        def wait_free(engine, c, b, name):
            side, n = AT[name]
            engine.wait_ge(used[side][b], c * len(fills[side]) + n + 1)

        def wait_used(engine, c, b, name):
            side, n = AT[name]
            engine.wait_ge(used[side][b], c * len(fills[side]) + n + 2)

        def is_full(last, b, name):
            last.then_inc(full[AT[name][0]][b], 1)

        def is_used(last, b, name):
            last.then_inc(used[AT[name][0]][b], 1)

        def head(t, h, w=P):
            return t[:, h // 3, (h % 3) * w:(h % 3 + 1) * w]

        def turns(engine, steps):
            def do(name, c, b, *i):
                if name in steps:
                    steps[name](c, b, *i)

            def levels(c, b, others):
                for name, oc, ob in others.get(-1, ()):
                    do(name, oc, ob)
                for i in range(NL):
                    for half, name in enumerate(("level_p", "level_xy")):
                        do(name, c, b, i)
                        for name, oc, ob in others.get(2 * i + half, ()):
                            do(name, oc, ob)

            def others(end, begin):
                at = {}
                if end is not None:
                    at = {-1: [("w1", *end)], 0: [("delta", *end)], 2: [("out", *end)], 4: [("gated", *end)]}
                if begin is not None:
                    at[2] = at.get(2, []) + [("prepare", *begin)]
                    at[4] = at.get(4, []) + [("decay", *begin)]
                    at[6] = [("transposes", *begin)]
                    at[8] = [("kk", *begin)]
                    at[10] = [("kq", *begin)]
                    at[11] = [("x0", *begin)]
                return at

            def chunk(c, first=False, last=False):
                levels(c, 0, others(None if first else (c - 1, 1), (c, 1)))
                levels(c, 1, others((c, 0), None if last else (c + 1, 0)))

            for name in ("prepare", "decay", "transposes", "kk", "kq", "x0"):
                do(name, 0, 0)
            chunk(0, first=True)
            with engine.Fori(1, TB - 1) as c:
                chunk(c)
            chunk(TB - 1, last=True)
            for name in ("w1", "delta", "out", "gated"):
                do(name, TB - 1, 1)

        with nc.Block() as block:
            @block.gpsimd
            def _(pool):
                g_ = nc.gpsimd
                for b in range(B):
                    g_.memset(state[b][:], 0.0).then_inc(s_zero[b], 1)

                def prepare(c, b):
                    t = c + b * TB
                    wait_free(pool, c, b, fills[1][0])

                    def scaled(out, at_, width, m, repeat=1):
                        src = qkv[:, bass.ds(t, 1), at_:at_ + DH * width].rearrange("p o (h d) -> p (o h) d", d=width)
                        sc = scl[:, bass.ds(t, 1), m].rearrange("p o h -> p (o h)").unsqueeze(2)
                        if repeat == 1:
                            return g_.tensor_tensor(out, src, sc.broadcast_to([P, DH, width]), ALU.mult)
                        return g_.tensor_tensor(out, src.unsqueeze(2).broadcast_to([P, DH, repeat, width]),
                                                sc.unsqueeze(3).broadcast_to([P, DH, repeat, width]), ALU.mult)

                    q_at, k_at, v_at = 0, DH * DK, 2 * DH * DK
                    scaled(ks[b][:], k_at, DK, SK, 3)
                    scaled(qs[b][:, :, 0], q_at, DK, SQG)
                    scaled(qs[b][:, :, 1], k_at, DK, SKB)
                    scaled(qs[b][:, :, 2], q_at, DK, SQ).then_inc(prep_done[b], 1)
                    scaled(ke[b][:], k_at, DK, SKE)
                    scaled(wr[b][:, :, 0:DV], v_at, DV, SVB)
                    scaled(wr[b][:, :, DV:], k_at, DK, SKBG).then_inc(prep_done[b], 1)

                def mask(i):
                    return k.cf[:, base + i * P:base + (i + 1) * P].unsqueeze(1).broadcast_to([P, DH, P])

                def heads_of(t):
                    return t.rearrange("p a (h i) -> p (a h) i", i=P)

                def first(c, b):
                    y = heads_of(yy[b][:])
                    wait_used(pool, c, b, "kk")
                    g_.tensor_tensor(y, heads_of(at[b]), mask(0), ALU.mult).then_inc(pool_step[b], 1)
                    pool.wait_ge(pool_step[b], c + 1)
                    g_.tensor_tensor(y, k.identf.unsqueeze(1).broadcast_to([P, DH, P]), y,
                                     ALU.subtract).then_inc(y_done[b], 1)
                    for i in range(RING):
                        blocks(c, b, i)

                def blocks(c, b, i):
                    if i >= RING:
                        wait_full(pool, c, b, ("P", i - RING))
                    g_.tensor_tensor(heads_of(lev[b][:, i % RING]), heads_of(at[b]), mask(i + 1),
                                     ALU.mult).then_inc(lev_done[b], 1)

                def next_blocks(c, b, i):
                    if i + RING < NL:
                        blocks(c, b, i + RING)

                def gated(c, b):
                    def tile(buf):
                        return buf[:, bass.ds(c + b * TB, 1)].rearrange("p o n -> p (o n)")

                    wait_used(pool, c, b, "out")
                    g_.tensor_tensor(tile(o_all), tile(o_all), tile(gate), ALU.mult).then_inc(gated_step[b], 1)
                    pool.wait_ge(gated_step[b], c + 1)
                    g_.tensor_tensor(tile(sq), tile(o_all), tile(o_all), ALU.mult)

                turns(pool, {"gated": gated, "prepare": prepare, "kk": first, "level_p": next_blocks})

            @block.tensor
            def _(pe):
                def transposes(c, b):
                    pe.wait_ge(prep_done[b], 2 * c + 1)
                    for src, name in ((ks, "ksT"), (qs, "qsT")):
                        wait_free(pe, c, b, name)
                        for h in range(DH):
                            last = nc.tensor.transpose(at_head(b, name, h, 3 * DK),
                                                       src[b][:, h].rearrange("p m d -> p (m d)"), k.identf)
                        is_full(last, b, name)

                def decay(c, b):
                    pe.wait_ge(decay_done[b], c + 1)
                    wait_free(pe, c, b, "decay")
                    for h in range(DH):
                        nc.tensor.matmul(at_head(b, "decay", h), gs[b][:, h], k.cf[:, slice(*CF["upto"])],
                                         start=True, stop=False)
                        last = nc.tensor.matmul(at_head(b, "decay", h), k.identb, k.cb[:, slice(*CB["past"])],
                                                start=False, stop=True)
                    is_full(last, b, "decay")

                def product(b, name, lhsT, rhs):
                    for h in range(DH):
                        last = nc.tensor.matmul(at_head(b, name, h), lhsT(h), rhs(h), start=True, stop=True)
                    is_full(last, b, name)

                def rows_of(t, m, h):
                    return t[m * DK:(m + 1) * DK, h // 3, (h % 3) * P:(h % 3 + 1) * P]

                def kk(c, b):
                    wait_free(pe, c, b, "kk")
                    wait_used(pe, c, b, "ksT")
                    product(b, "kk", lambda h: rows_of(ksT[b], 1, h), lambda h: rows_of(qsT[b], 1, h))

                def kq(c, b):
                    wait_free(pe, c, b, "kq")
                    product(b, "kq", lambda h: rows_of(ksT[b], 2, h), lambda h: rows_of(qsT[b], 2, h))

                def x0(c, b):
                    wait_free(pe, c, b, "X")
                    pe.wait_ge(y_done[b], c + 1)
                    for h in range(DH):
                        last = nc.tensor.transpose(at_head(b, "X", h), head(yy[b], h), k.identf)
                    is_full(last, b, "X")

                def level_p(c, b, i):
                    pe.wait_ge(lev_done[b], c * NL + i + 1)
                    wait_used(pe, c, b, ("X", i - 1) if i else "X")
                    wait_free(pe, c, b, ("P", i))
                    product(b, ("P", i), lambda h: head(lev[b][:, i % RING], h), lambda h: head(xx[b], h))

                def level_xy(c, b, i):
                    wait_used(pe, c, b, ("P", i))
                    if i < NL - 1:
                        wait_free(pe, c, b, ("X", i))
                        product(b, ("X", i), lambda h: head(yy[b], h), lambda h: head(pp[b], h))
                    elif NL > 1:
                        wait_used(pe, c, b, ("Y", i - 1))
                    product(b, ("Y", i), lambda h: head(pp[b], h), lambda h: head(yy[b], h))

                def w1_(c, b):
                    wait_used(pe, c, b, ("Y", NL - 1))
                    pe.wait_ge(prep_done[b], 2 * c + 2)
                    wait_free(pe, c, b, "w1T")
                    for h in range(DH):
                        last = nc.tensor.matmul(at_head(b, "w1T", h, DK), wr[b][:, h, DV:], head(yy[b], h),
                                                start=True, stop=True)
                    is_full(last, b, "w1T")
                    for h in range(DH):
                        last = nc.tensor.matmul(at_head(b, "w1", h, P, DV + DK), head(yy[b], h), wr[b][:, h],
                                                start=True, stop=True)
                    is_full(last, b, "w1")

                def delta(c, b):
                    wait_used(pe, c, b, "w1T")
                    wait_free(pe, c, b, "delta")
                    for h in range(DH):
                        last = nc.tensor.matmul(k.ps[:, bank(b, "delta"), h * DV:(h + 1) * DV], head(w1t[b], h),
                                                state[b][:, h], start=True, stop=True)
                    is_full(last, b, "delta")

                def out(c, b):
                    wait_used(pe, c, b, "delta")
                    wait_free(pe, c, b, "out")
                    for h in range(DH):
                        o = k.ps[:, bank(b, "out"), h * DV:(h + 1) * DV]
                        nc.tensor.matmul(o, rows_of(qsT[b], 0, h), state[b][:, h], start=True, stop=False)
                        last = nc.tensor.matmul(o, head(mt[b], h), de[b][:, h], start=False, stop=True)
                    is_full(last, b, "out")
                    for h in range(DH):
                        last = nc.tensor.matmul(k.ps[0:DK, bank(b, "state"), h * DV:(h + 1) * DV], ke[b][:, h],
                                                de[b][:, h], start=True, stop=True)
                    is_full(last, b, "state")

                for b in range(B):
                    pe.wait_ge(s_zero[b], 1)
                turns(pe, {"transposes": transposes, "decay": decay, "kk": kk, "kq": kq, "x0": x0,
                           "level_p": level_p, "level_xy": level_xy, "w1": w1_, "delta": delta, "out": out})

            @block.scalar
            def _(act):
                def evacuate(c, b, name, out, src, func=ACT.Copy):
                    wait_full(act, c, b, name)
                    is_used(nc.scalar.activation(out, src, func), b, name)

                def transposes(c, b):
                    evacuate(c, b, "ksT", ksT[b][:], pair(b, "ksT", 3 * DK))
                    evacuate(c, b, "qsT", qsT[b][:], pair(b, "qsT", 3 * DK))

                def w1_(c, b):
                    evacuate(c, b, "w1T", w1t[b][:], pair(b, "w1T", DK))
                    evacuate(c, b, "w1", w1[b][:].rearrange("p a h d -> p a (h d)"),
                             pair(b, "w1", P, 3 * (DV + DK)))

                def out(c, b):
                    evacuate(c, b, "out", o_all[:, bass.ds(c + b * TB, 1)].rearrange("p o n -> p (o n)"),
                             k.ps[:, bank(b, "out"), 0:DH * DV])

                for b in range(B):
                    for side in used:
                        act.sem_inc(side[b], 1)
                turns(act, {"transposes": transposes, "w1": w1_, "out": out,
                            "decay": lambda c, b: evacuate(c, b, "decay", ex[b][:], pair(b, "decay"), ACT.Exp),
                            "x0": lambda c, b: evacuate(c, b, "X", xx[b][:], pair(b, "X")),
                            "level_p": lambda c, b, i: evacuate(c, b, ("P", i), pp[b][:], pair(b, ("P", i)))})

            @block.vector
            def _(dve):
                v = nc.vector

                def masked_g(c, b):
                    wait_free(dve, c, b, fills[0][0])
                    gt = g[:, bass.ds(c + b * TB, 1)].rearrange("p o h -> p (o h)").unsqueeze(2)
                    v.tensor_tensor(gs[b], k.cf[:, slice(*CF["after"])].unsqueeze(1).broadcast_to([P, DH, P]),
                                    gt.broadcast_to([P, DH, P]), ALU.mult).then_inc(decay_done[b], 1)

                def kk(c, b):
                    wait_full(dve, c, b, "kk")
                    wait_used(dve, c, b, "decay")
                    is_used(v.tensor_tensor(at[b], pair(b, "kk"), ex[b][:], ALU.mult), b, "kk")

                def kq(c, b):
                    wait_full(dve, c, b, "kq")
                    is_used(v.tensor_tensor(mt[b], pair(b, "kq"), ex[b][:], ALU.mult), b, "kq")

                def level_xy(c, b, i):
                    if i < NL - 1:
                        wait_full(dve, c, b, ("X", i))
                        is_used(v.tensor_tensor(xx[b][:], xx[b][:], pair(b, ("X", i)), ALU.subtract), b, ("X", i))
                    wait_full(dve, c, b, ("Y", i))
                    is_used(v.tensor_tensor(yy[b][:], yy[b][:], pair(b, ("Y", i)), ALU.subtract), b, ("Y", i))

                def delta(c, b):
                    wait_full(dve, c, b, "delta")
                    rows = k.ps[:, bank(b, "delta"), 0:DH * DV].rearrange("p (a h d) -> p a h d", a=2, d=DV)
                    is_used(v.tensor_tensor(de[b][:].rearrange("p (a h) d -> p a h d", a=2), w1[b][:, :, :, 0:DV],
                                            rows, ALU.subtract), b, "delta")

                def out(c, b):
                    wait_full(dve, c, b, "state")
                    tt = tot[:, bass.ds(c + b * TB, 1)].rearrange("p o h -> p (o h)").unsqueeze(2)
                    v.tensor_tensor(state[b][:], state[b][:], tt.broadcast_to([DK, DH, DV]),
                                    ALU.mult).then_inc(s_step[b], 1)
                    dve.wait_ge(s_step[b], c + 1)
                    added = k.ps[0:DK, bank(b, "state"), 0:DH * DV].rearrange("p (h d) -> p h d", d=DV)
                    is_used(v.tensor_tensor(state[b][:], state[b][:], added, ALU.add), b, "state")

                turns(dve, {"prepare": masked_g, "kk": kk, "kq": kq, "level_xy": level_xy, "delta": delta, "out": out})


class Kernel:
    pass


def build(nc, ins, out):
    NAMES.clear()
    SEMS.clear()
    k = Kernel()
    k.ins = ins
    ctx = ExitStack()
    with ctx:
        def sb(name, shape, dt=F32):
            return ctx.enter_context(sbuf(nc, name, shape, dt))

        k.ps = ctx.enter_context(nc.psum_tensor("ps", [P, 8, 512], F32))
        k.x = sb("x", [P, NT, D])
        k.h = sb("h", [P, NT, D])
        k.hT = sb("hT", [P, KT, TOK])
        k.mod = sb("mod", [P, 2, B, NMOD])
        k.cf = sb("cf", [P, CF_W])
        k.cb = sb("cb", [P, CB_W], BF16)
        k.identf = k.cf[:, slice(*CF["ident"])]
        k.identb = k.cb[:, slice(*CB["ident"])]
        k.future = k.cb[:, slice(*CB["future"])]
        k.sh = sb("sh", [P, NT, D])
        k.slot = sb("slot", [P, NT, TOPK], I32)
        k.wk = sb("wk", [P, NT, TOPK])
        k.probs = sb("probs", [P, NT, E])
        k.sv = sb("sv", [P, NT, E])
        k.s8 = sb("s8", [P, NT, 8])
        k.table = sb("table", [P, E * CAP[0] // P], I32)
        h_dram = nc.dram_tensor("h_rows", [TOK, D], F32).ap()
        y_dram = [nc.dram_tensor(f"y_rows{n}", [E * CAP[n] + 1, D], F32).ap() for n in (0, 1)]
        k.wo_in = ctx.enter_context(nc.semaphore("wo_in"))

        k.bias_in = ctx.enter_context(nc.semaphore("bias_in"))
        k.w_in = [ctx.enter_context(nc.semaphore(f"w{h}_in")) for h in range(2)]
        with ExitStack() as scope:
            w = scope.enter_context(sbuf(nc, "w", [P, 2, 3, KT, HD]))
            bias = scope.enter_context(sbuf(nc, "bias", [P, 3, HEADS]))
            first_stage(nc, k, w, bias)
            attn = scope.enter_context(sbuf(nc, "attn", [P, HEADS * B, T], F32))
            wo = scope.enter_context(sbuf(nc, "wo", [P, HEADS // 2, D], F32))
            with nc.Block() as block:
                @block.sync
                def _(sp):
                    sp.dma_start(wo[:], ins["w_o"][:, 0:HEADS // 2]).then_inc(k.wo_in, 16)
                    sp.dma_start(k.sh[:], ins["w_o"][:, HEADS // 2:]).then_inc(k.wo_in, 16)
            attention_stage(nc, k, attn, w, bias)
            route_stage(nc, k, 0, h_dram, AttentionOut, attn, wo)
        wide_expert_stage(nc, k, h_dram, y_dram[0])
        renew(nc)
        with ExitStack() as scope:
            def buf(name, shape):
                return scope.enter_context(sbuf(nc, name, shape))

            gate = buf("gate_act", [P, NT, DH * DV])
            g = buf("g", [P, NT, DH])
            tot = buf("tot", [DK, NT, DH])
            o_all = buf("o_all", [P, NT, DH * DV])
            sq = buf("osq", [P, NT, DH * DV])
            scl = buf("scl", [P, NT, 7, DH])
            with sbuf(nc, "qkv", [P, NT, QKV]) as qkv:
                delta_project_stage(nc, k, y_dram[0], qkv, gate, g, scl, tot)
                delta_stage(nc, k, qkv, g, scl, tot, gate, o_all, sq)
            route_stage(nc, k, 1, h_dram, DeltaOut, o_all, sq)
        narrow_expert_stage(nc, k, h_dram, y_dram[1])
        last_stage(nc, k, y_dram[1], out)
        return k


def layouts(a):
    g = {name: np.asarray(v) for name, v in a.items()}

    def rows(m, p=P):
        return np.ascontiguousarray(m.reshape(m.shape[0] // p, p, *m.shape[1:]).swapaxes(0, 1))

    o = {}
    o["cf"], o["cb"] = constants()
    o["x"] = rows(g["L0_attn_query"].reshape(TOK, D))
    for n in (0, 1):
        o[f"c{n}"] = rows(g[f"L{n}_c"].T)
        o[f"wmod{n}"] = rows(g[f"L{n}_wmod"])
    qkv = np.stack([g[f"L0_attn_w_{c}"].reshape(KT, P, HEADS, HD) for c in "qkv"])
    o["w_qkv"] = np.ascontiguousarray(qkv.transpose(3, 2, 0, 1, 4))
    o["b_qkv"] = np.ascontiguousarray(np.stack([g[f"L0_attn_b_{c}"].reshape(HEADS, HD) for c in "qkv"]).transpose(2, 0, 1))
    o["w_o"] = rows(g["L0_attn_w_o"])
    o["b_o"] = g["L0_attn_b_o"]
    o["router0"] = rows(g["L0_ffn_wg_router"].T)
    o["router1"] = rows(g["L1_ffn_gate_w"].T)
    gu0 = np.stack([g["L0_ffn_w_gate"], g["L0_ffn_w_up"]], 2)
    gu1 = g["L1_ffn_w_gate_up"].reshape(E, D, 2, F)
    for n, gu in ((0, gu0), (1, gu1)):
        o[f"w_gu{n}"] = np.ascontiguousarray(gu.reshape(E, KT, P, 2, F).transpose(0, 2, 1, 3, 4))
        wd = g[f"L{n}_ffn_w_down"]
        o[f"w_down{n}"] = np.ascontiguousarray(wd.reshape(E, 2, FH, D).transpose(0, 2, 1, 3))
        o[f"ws_down{n}"] = g[f"L{n}_ffn_ws_down"]
    o["ws_gu0"] = rows(np.stack([g["L0_ffn_ws_gate"], g["L0_ffn_ws_up"]], 1))
    o["ws_gu1"] = rows(g["L1_ffn_ws_gate_up"].reshape(D, 2, FS))
    o["w_qkv1"] = rows(np.concatenate([g["L1_attn_Wq"], g["L1_attn_Wk"], g["L1_attn_Wv"]]).T)
    o["w_gab"] = rows(np.concatenate([g["L1_attn_Wg"], g["L1_attn_Wa"], g["L1_attn_Wb"]]).T)
    conv = np.concatenate([g["L1_attn_conv_q_w"], g["L1_attn_conv_k_w"], g["L1_attn_conv_v_w"]])[:, 0]
    o["conv"] = rows(conv, CH)
    o["A_log"], o["dt_bias"], o["norm_w"] = g["L1_attn_A_log"], g["L1_attn_dt_bias"], g["L1_attn_norm_w"]
    o["w_o1"] = rows(g["L1_attn_Wo"].T)
    return {n: np.ascontiguousarray(v) for n, v in o.items()}


def kernel(**inputs):
    import concourse.bacc as bacc
    from concourse.bass_utils import run_bass_kernel_spmd

    nc = bacc.Bacc("TRN2", target_bir_lowering=False, num_devices=1)
    arrays = {f"in_{n}": v for n, v in layouts(inputs).items()}
    ins = {n[3:]: nc.dram_tensor(n, v.shape, mybir.dt.from_np(v.dtype), kind="ExternalInput").ap()
           for n, v in arrays.items()}
    out = nc.dram_tensor("out", [P, NT, D], F32, kind="ExternalOutput").ap()
    build(nc, ins, out)
    r = run_bass_kernel_spmd(nc, [arrays], core_ids=[0])
    y = r.results[0]["out"]
    return np.ascontiguousarray(y.swapaxes(0, 1)).reshape(B, T, D)
```
